# Optimizing a Trainium2 kernel written in Bass

```python
import numpy as np
import jax
import jax.numpy as jnp

def _softmax(x, axis=-1):
    return jax.nn.softmax(x, axis=axis)

def _gelu(x):
    return jax.nn.gelu(x, approximate=True)

def _silu(x):
    return jax.nn.silu(x)

def _sigmoid(x):
    return jax.nn.sigmoid(x)

def _layernorm(x, axis=-1, eps=1e-05):
    m = jnp.mean(x, axis=axis, keepdims=True)
    v = jnp.var(x, axis=axis, keepdims=True)
    return (x - m) / jnp.sqrt(v + eps)

def _scatter_add(tgt, idx, src, axis=0):
    return tgt.at[idx].add(src)

def _segment_sum(src, seg, n):
    return jax.ops.segment_sum(src, seg, n)
kernel_name = 'mk_perceiver_d1_seqx_r8_aac05e'

def setup_inputs(seed: int=0):
    np.random.seed(seed)
    _w = jnp.asarray

    def _rec_inputs():
        import jax
        import jax.numpy as jnp
        _rk = jax.random.key(seed)
        x = -0.0003929 + 0.9999 * jax.random.normal(jax.random.fold_in(_rk, 1), (64, 64, 512), jnp.float32)
        _lenS = 64 - jax.random.randint(jax.random.fold_in(_rk, 7), (64,), 0, max(1, 64 // 4) + 1, jnp.int32)
        _lenS2 = 128 - jax.random.randint(jax.random.fold_in(_rk, 8), (64,), 0, max(1, 128 // 4) + 1, jnp.int32)
        _ctx_1024P = jax.random.normal(jax.random.fold_in(_rk, 11), (64, 16, 128), jnp.float32)
        _ctx_1024c = jax.random.dirichlet(jax.random.fold_in(_rk, 511), 0.3 * jnp.ones((16,), jnp.float32), (64, 128))
        _ctx_1024t = jnp.einsum('bsk,bkd->bsd', _ctx_1024c, _ctx_1024P)
        _ctx_1024t = _ctx_1024t * jax.lax.rsqrt(jnp.mean(jnp.square(_ctx_1024t)) + 1e-12) * 0.953939
        ctx_1024 = -1.39393e-06 + 0.999914 * (_ctx_1024t + 0.3 * jax.random.normal(jax.random.fold_in(_rk, 611), (64, 128, 128), jnp.float32))
        _validS = jnp.arange(64)[None, :] < _lenS[:, None]
        _validS2 = jnp.arange(128)[None, :] < _lenS2[:, None]
        _causal = jnp.tril(jnp.ones((64, 64), dtype=bool))
        mask_SxS2_ff0 = jnp.where(jnp.ones((64, 128), dtype=bool), 0.0, -1000000000.0).astype(jnp.float32)
        return (x, ctx_1024, mask_SxS2_ff0)
    x, ctx_1024, mask_SxS2_ff0 = _rec_inputs()

    def _L0_xattn_setup():
        import math
        import jax, jax.numpy as jnp
        import numpy as np
        N_HEADS = 32
        N_KV_HEADS = 8
        N_REP = N_HEADS // N_KV_HEADS
        HEAD_DIM = 512 // N_HEADS
        key = jax.random.key(seed)
        kq, kk, kv = jax.random.split(key, 3)
        B, S, T = (2, 256, 256)
        q = jax.random.normal(kq, (B, S, N_HEADS * HEAD_DIM), dtype=jnp.float32)
        k = jax.random.normal(kk, (B, T, N_KV_HEADS * HEAD_DIM), dtype=jnp.float32)
        v = jax.random.normal(kv, (B, T, N_KV_HEADS * HEAD_DIM), dtype=jnp.float32)
        mask = jnp.zeros((S, T), dtype=jnp.float32)
        return {'q': q, 'k': k, 'v': v, 'start_pos': 0, 'mask': mask}
    _L0_xattn_all = _L0_xattn_setup()
    _L0_xattn_in = {k: v for k, v in _L0_xattn_all.items() if k in ()}
    del _L0_xattn_all

    def _L0_attn_setup():
        import jax, jax.numpy as jnp
        import numpy as np
        from jax import lax
        H = 64
        P = 64
        N = 128
        G = 8
        K = 4
        D_MODEL = 512
        I = H * P
        GN = G * N
        CONV_DIM = I + 2 * GN
        PROJ = I + CONV_DIM + H
        EPS = 1e-05
        GROUP_SIZE = I // G

        def _reference_tuple_inner(hidden_states, in_proj_w, conv_weight, conv_bias, dt_bias, A_log, D, norm_weight, out_proj_w):
            B, L, _ = hidden_states.shape
            proj = jnp.einsum('bld,pd->blp', hidden_states, in_proj_w)
            gate = proj[..., :I]
            hbc = proj[..., I:I + CONV_DIM]
            dt = proj[..., -H:]
            pad = jnp.pad(hbc, ((0, 0), (K - 1, 0), (0, 0)))
            conv = conv_bias
            for k in range(K):
                conv = conv + pad[:, k:k + L, :] * conv_weight[:, k]
            xBC = jax.nn.silu(conv)
            x = xBC[..., :I].reshape(B, L, H, P)
            Bm = xBC[..., I:I + GN].reshape(B, L, G, N)
            Cm = xBC[..., I + GN:].reshape(B, L, G, N)
            hpg = H // G
            B_h = jnp.repeat(Bm, hpg, axis=2)
            C_h = jnp.repeat(Cm, hpg, axis=2)
            dt_p = jax.nn.softplus(dt + dt_bias)
            A = -jnp.exp(A_log)
            dA = jnp.exp(dt_p * A)
            dtx = dt_p[..., None] * x

            def step(state, inp):
                dA_t, dtx_t, B_t, C_t = inp
                state = state * dA_t[..., None, None] + dtx_t[..., None] * B_t[:, :, None, :]
                y_t = jnp.einsum('bhpn,bhn->bhp', state, C_t)
                return (state, y_t)
            xs = (jnp.moveaxis(dA, 1, 0), jnp.moveaxis(dtx, 1, 0), jnp.moveaxis(B_h, 1, 0), jnp.moveaxis(C_h, 1, 0))
            state0 = jnp.zeros((B, H, P, N), jnp.float32)
            final_state, ys = lax.scan(step, state0, xs)
            y = jnp.moveaxis(ys, 0, 1) + x * D[None, None, :, None]
            y = y.reshape(B, L, I)
            yg = y.reshape(B, L, G, GROUP_SIZE)
            var = jnp.mean(yg * yg, axis=-1, keepdims=True)
            yn = (yg * lax.rsqrt(var + EPS)).reshape(B, L, I) * norm_weight
            yn = yn * jax.nn.silu(gate)
            out = jnp.einsum('bli,di->bld', yn, out_proj_w)
            conv_state_new = jnp.moveaxis(hbc[:, L - (K - 1):, :], 1, 2)
            return (out, conv_state_new, final_state)
        key = jax.random.key(seed)
        ks = jax.random.split(key, 6)
        B, L = (2, 256)
        s = 0.02
        return {'hidden_states': jax.random.normal(ks[0], (B, L, D_MODEL), jnp.float32), 'in_proj_w': jax.random.normal(ks[1], (PROJ, D_MODEL), jnp.float32) * s, 'conv_weight': jax.random.normal(ks[2], (CONV_DIM, K), jnp.float32) * s, 'conv_bias': jnp.zeros((CONV_DIM,), jnp.float32), 'dt_bias': jnp.ones((H,), jnp.float32), 'A_log': jnp.log(jnp.arange(1, H + 1, dtype=jnp.float32)), 'D': jnp.ones((H,), jnp.float32), 'norm_weight': jnp.ones((I,), jnp.float32), 'out_proj_w': jax.random.normal(ks[3], (D_MODEL, I), jnp.float32) * s}
    _L0_attn_all = _L0_attn_setup()
    _L0_attn_in = {k: v for k, v in _L0_attn_all.items() if k in ('in_proj_w', 'conv_weight', 'conv_bias', 'dt_bias', 'A_log', 'D', 'norm_weight', 'out_proj_w')}
    del _L0_attn_all

    def _L0_ffn_setup():
        import jax, jax.numpy as jnp
        import numpy as np
        K_TOP = 8
        key = jax.random.key(seed)
        k1, k2, k3 = jax.random.split(key, 3)
        B, S, H, E = (4, 512, 512, 64)
        hidden_states = jax.random.normal(k1, (B, S, H), dtype=jnp.float32)
        router_weight = jax.random.normal(k2, (E, H), dtype=jnp.float32)
        router_bias = jnp.zeros((E,), dtype=jnp.float32)
        expert_bias = jax.random.normal(k3, (E, H), dtype=jnp.float32) * 0.1
        return {'hidden_states': hidden_states, 'router_weight': router_weight, 'router_bias': router_bias, 'expert_bias': expert_bias}
    _L0_ffn_all = _L0_ffn_setup()
    _L0_ffn_in = {k: v for k, v in _L0_ffn_all.items() if k in ('router_weight', 'router_bias', 'expert_bias')}
    del _L0_ffn_all
    return {'x': x, 'ctx_1024': ctx_1024, 'mask_SxS2_ff0': mask_SxS2_ff0, 'L0_attn_in_proj_w': _L0_attn_in['in_proj_w'], 'L0_attn_conv_weight': _L0_attn_in['conv_weight'], 'L0_attn_conv_bias': _L0_attn_in['conv_bias'], 'L0_attn_dt_bias': _L0_attn_in['dt_bias'], 'L0_attn_A_log': _L0_attn_in['A_log'], 'L0_attn_D': _L0_attn_in['D'], 'L0_attn_norm_weight': _L0_attn_in['norm_weight'], 'L0_attn_out_proj_w': _L0_attn_in['out_proj_w'], 'L0_ffn_router_weight': _L0_ffn_in['router_weight'], 'L0_ffn_router_bias': _L0_ffn_in['router_bias'], 'L0_ffn_expert_bias': _L0_ffn_in['expert_bias']}

def reference(x, ctx_1024, mask_SxS2_ff0, L0_attn_in_proj_w, L0_attn_conv_weight, L0_attn_conv_bias, L0_attn_dt_bias, L0_attn_A_log, L0_attn_D, L0_attn_norm_weight, L0_attn_out_proj_w, L0_ffn_router_weight, L0_ffn_router_bias, L0_ffn_expert_bias):
    import jax
    import jax.numpy as jnp

    def _L0_xattn_ref(q, k, v, start_pos, mask):
        import math
        import jax, jax.numpy as jnp
        import numpy as np
        N_HEADS = 32
        N_KV_HEADS = 8
        N_REP = N_HEADS // N_KV_HEADS
        HEAD_DIM = 512 // N_HEADS
        b, s, _ = q.shape
        t = k.shape[1]
        xq = q.reshape(b, s, N_KV_HEADS, N_REP, HEAD_DIM)
        xk = k.reshape(b, t, N_KV_HEADS, HEAD_DIM)
        xv = v.reshape(b, t, N_KV_HEADS, HEAD_DIM)
        scores = jnp.einsum('bsgrd,btgd->bgrst', xq, xk) / math.sqrt(HEAD_DIM)
        scores = scores + mask
        probs = jax.nn.softmax(scores.astype(jnp.float32), axis=-1).astype(q.dtype)
        out = jnp.einsum('bgrst,btgd->bsgrd', probs, xv)
        return out.reshape(b, s, N_HEADS * HEAD_DIM)

    def _L0_attn_ref(hidden_states, in_proj_w, conv_weight, conv_bias, dt_bias, A_log, D, norm_weight, out_proj_w):
        import jax, jax.numpy as jnp
        import numpy as np
        from jax import lax
        H = 64
        P = 64
        N = 128
        G = 8
        K = 4
        D_MODEL = 512
        I = H * P
        GN = G * N
        CONV_DIM = I + 2 * GN
        PROJ = I + CONV_DIM + H
        EPS = 1e-05
        GROUP_SIZE = I // G

        def _reference_tuple_inner(hidden_states, in_proj_w, conv_weight, conv_bias, dt_bias, A_log, D, norm_weight, out_proj_w):
            B, L, _ = hidden_states.shape
            proj = jnp.einsum('bld,pd->blp', hidden_states, in_proj_w)
            gate = proj[..., :I]
            hbc = proj[..., I:I + CONV_DIM]
            dt = proj[..., -H:]
            pad = jnp.pad(hbc, ((0, 0), (K - 1, 0), (0, 0)))
            conv = conv_bias
            for k in range(K):
                conv = conv + pad[:, k:k + L, :] * conv_weight[:, k]
            xBC = jax.nn.silu(conv)
            x = xBC[..., :I].reshape(B, L, H, P)
            Bm = xBC[..., I:I + GN].reshape(B, L, G, N)
            Cm = xBC[..., I + GN:].reshape(B, L, G, N)
            hpg = H // G
            B_h = jnp.repeat(Bm, hpg, axis=2)
            C_h = jnp.repeat(Cm, hpg, axis=2)
            dt_p = jax.nn.softplus(dt + dt_bias)
            A = -jnp.exp(A_log)
            dA = jnp.exp(dt_p * A)
            dtx = dt_p[..., None] * x

            def step(state, inp):
                dA_t, dtx_t, B_t, C_t = inp
                state = state * dA_t[..., None, None] + dtx_t[..., None] * B_t[:, :, None, :]
                y_t = jnp.einsum('bhpn,bhn->bhp', state, C_t)
                return (state, y_t)
            xs = (jnp.moveaxis(dA, 1, 0), jnp.moveaxis(dtx, 1, 0), jnp.moveaxis(B_h, 1, 0), jnp.moveaxis(C_h, 1, 0))
            state0 = jnp.zeros((B, H, P, N), jnp.float32)
            final_state, ys = lax.scan(step, state0, xs)
            y = jnp.moveaxis(ys, 0, 1) + x * D[None, None, :, None]
            y = y.reshape(B, L, I)
            yg = y.reshape(B, L, G, GROUP_SIZE)
            var = jnp.mean(yg * yg, axis=-1, keepdims=True)
            yn = (yg * lax.rsqrt(var + EPS)).reshape(B, L, I) * norm_weight
            yn = yn * jax.nn.silu(gate)
            out = jnp.einsum('bli,di->bld', yn, out_proj_w)
            conv_state_new = jnp.moveaxis(hbc[:, L - (K - 1):, :], 1, 2)
            return (out, conv_state_new, final_state)
        return _reference_tuple_inner(hidden_states, in_proj_w, conv_weight, conv_bias, dt_bias, A_log, D, norm_weight, out_proj_w)[0]

    def _L0_ffn_ref(hidden_states, router_weight, router_bias, expert_bias):
        import jax, jax.numpy as jnp
        import numpy as np
        K_TOP = 8
        B, S, H = hidden_states.shape
        E = router_weight.shape[0]
        T = B * S
        flat = hidden_states.reshape(T, H)
        logits = jnp.einsum('th,eh->te', flat, router_weight) + router_bias
        scores = jax.nn.softmax(logits, axis=-1)
        topk_w, topk_idx = jax.lax.top_k(scores, K_TOP)
        w_sum = topk_w.sum(axis=-1, keepdims=True)
        w_dense = jnp.zeros((T, E), dtype=scores.dtype).at[jnp.arange(T)[:, None], topk_idx].add(topk_w)
        bias_mix = jnp.einsum('te,eh->th', w_dense, expert_bias)
        out = flat * w_sum + bias_mix
        return out.reshape(B, S, H)
    x = x + _L0_xattn_ref(_layernorm(x, axis=-1), ctx_1024, ctx_1024, 0, mask_SxS2_ff0)
    x = x + _L0_attn_ref(_layernorm(x, axis=-1), L0_attn_in_proj_w, L0_attn_conv_weight, L0_attn_conv_bias, L0_attn_dt_bias, L0_attn_A_log, L0_attn_D, L0_attn_norm_weight, L0_attn_out_proj_w)
    x = x + _L0_ffn_ref(_layernorm(x, axis=-1), L0_ffn_router_weight, L0_ffn_router_bias, L0_ffn_expert_bias)
    return x

_drawn_inputs = setup_inputs


def setup_inputs(seed=0):
    import zlib

    import numpy as np

    out = dict(_drawn_inputs(seed))
    spreads = {'mask_SxS2_ff0': (0.0, 0.8),
     'L0_attn_conv_bias': (0.0, 0.1),
     'L0_attn_dt_bias': (1.0, 0.6),
     'L0_attn_D': (1.0, 0.2),
     'L0_attn_norm_weight': (1.0, 0.2),
     'L0_ffn_router_bias': (0.0, 0.8)}
    factors = {'L0_attn_A_log': 8.0}
    for name, (base, spread) in spreads.items():
        noise = np.random.default_rng([zlib.crc32(name.encode()), seed]).standard_normal(out[name].shape)
        drawn = base * np.exp(spread * noise) if base else spread * noise
        out[name] = jnp.asarray(drawn.astype(out[name].dtype))
    for name, factor in factors.items():
        out[name] = (out[name] * factor).astype(out[name].dtype)
    return out
```

```python
import concourse.bass as bass
from concourse import mybir
from contextlib import ExitStack

F32 = mybir.dt.float32
ALU = mybir.AluOpType
ACT = mybir.ActivationFunctionType
AX_X = mybir.AxisListType.X

P = 128
BATCH, SEQ, DM = 64, 64, 512
KT = DM // P
PAIRS = BATCH * SEQ // P
TILES = 8
TOK = 512
T_CTX, C_CTX = 128, 128
HD = 16
H, HP, N_ST, G = 64, 64, 128, 8
HG = H // G
CT = 6
GATES = 4
E = 64
EPS = 1e-5
WORK = 30600




class Signal:

    def __init__(self, sem, per, credit=0):
        self.sem, self.per, self.credit = sem, per, credit

    def at(self, turn, n):
        return turn * self.per + (n + self.credit)


def build(nc, x, ctx_in, mask, w_groups, w_dt, w_out, conv_w, conv_b, dt_bias, a_log, d_skip, norm_w,
          w_router, b_router, e_bias, ident_in, parity_in, eye_in, out, xt_d, da_d):
    x_v = x.rearrange("(n b) s d -> n (b s) d", b=2)
    out_v = out.rearrange("(n b) s d -> (b s) n d", b=2)
    ctx_v = ctx_in.rearrange("(n b) t c -> n t b c", b=2)

    with ExitStack() as ctx:
        def sb(name, shape):
            return ctx.enter_context(nc.sbuf_tensor(name, shape, F32))

        def sem(name):
            return ctx.enter_context(nc.semaphore(name))

        def signal(name, per, credit=0):
            return Signal(sem(name), per, credit)

        bank = [ctx.enter_context(nc.psum_tensor(f"bank{i}", [P, 512], F32)) for i in range(8)]

        acc = sb("acc", [P, PAIRS, DM])
        ident = sb("ident", [P, P])
        parity = sb("parity", [P, 2])
        eye = sb("eye", [P, TOK])
        half_neg = sb("half_neg", [P, 4])
        dt_tok = sb("dt_tok", [P, PAIRS, H])
        cw = sb("cw", [P, G * CT, 4])
        cb = sb("cb", [P, G * CT])
        dsk = sb("dsk", [P, G * 4])
        nw = sb("nw", [P, G * 4])
        small = sb("small", [P, 64])
        work = sb("work", [P, WORK])
        used = [0]

        def view(*shape, parts=P):
            n = 1
            for s in shape:
                n *= s
            v = work[0:parts, used[0]:used[0] + n]
            used[0] += n
            assert used[0] <= WORK
            if len(shape) == 1:
                return v
            names = "abcd"[:len(shape)]
            return v.rearrange(f"p ({' '.join(names)}) -> p {' '.join(names)}",
                               **{k: s for k, s in zip(names, shape)})

        def acc_pair(i):
            return acc[:, (i + 4) % PAIRS, :]

        consts_in = sem("consts_in")
        N_CONSTS = 16 * 9
        half_set = sem("half_set")
        b_go = sem("b_go")
        c_go = sem("c_go")
        stand = sem("stand")

        used[0] = 0
        maskb = view(T_CTX)
        ctx_sb = view(2, C_CTX)
        k_rep = view(2, 8 * 4 * HD)
        v17 = view(2, 8, HD + 1)
        k_eo = view(2, 2, KT * T_CTX)
        xh = view(DM)
        xhT = view(KT, P)
        prob = view(2, 4, 4 * T_CTX)
        pt = view(2, 4 * P)
        att = view(256)
        stats = small[:, 0:6]
        mv = small[:, 8:10]
        rstd = small[:, 12:13]
        mx = small[:, 16:32]
        rden = small[:, 32:48]
        vpe = small[:, 11:12]

        a_x = signal("a_x", 16)
        a_ctx = signal("a_ctx", 16)
        a_ln = signal("a_ln", 3)
        a_rstd = signal("a_rstd", 1)
        a_xh = signal("a_xh", 1)
        a_rep = signal("a_rep", 2)
        a_front = signal("a_front", 3)
        a_kT = signal("a_kT", 5)
        a_v17 = signal("a_v17", 1, 1)
        a_score = signal("a_score", 2)
        a_masked = signal("a_masked", 8)
        a_max = signal("a_max", 2)
        a_sub = signal("a_sub", 2)
        a_exp = signal("a_exp", 2)
        a_pt = signal("a_pt", 8)
        a_pt_sb = signal("a_pt_sb", 8)
        a_pv = signal("a_pv", 8)
        a_out = signal("a_out", 6)

        def load_pair(sp, i, first=False):
            if not first:
                sp.wait_ge(a_x.sem, a_x.at(i - 1, 16))
            sp.dma_start(acc_pair(i), x_v[i]).then_inc(a_x.sem, 16)
            if not first:
                sp.wait_ge(a_rep.sem, a_rep.at(i - 1, 2))
                sp.sem_inc(stand, 1)
                sp.wait_ge(a_v17.sem, a_v17.at(i - 1, 1))
                sp.sem_inc(stand, 1)
            sp.dma_start(ctx_sb, ctx_v[i]).then_inc(a_ctx.sem, 16)

        def norm_pair(dve, i, first=False):
            dve.wait_ge(a_x.sem, a_x.at(i, 16))
            if not first:
                dve.wait_ge(a_xh.sem, a_xh.at(i - 1, 1))
            dve.bn_stats(stats, acc_pair(i)).then_inc(a_ln.sem, 1)
            dve.wait_ge(a_ln.sem, a_ln.at(i, 1))
            dve.sem_inc(stand, 1)
            dve.bn_aggr(mv, stats).then_inc(a_ln.sem, 1)
            dve.wait_ge(a_ln.sem, a_ln.at(i, 2))
            dve.tensor_scalar(vpe, mv[:, 1:2], EPS, None, ALU.add).then_inc(a_ln.sem, 1)

        def apply_norm(dve, i, first=False):
            dve.wait_ge(a_rstd.sem, a_rstd.at(i, 1))
            if not first:
                dve.wait_ge(a_front.sem, a_front.at(i - 1, 1))
            dve.tensor_scalar(xh, acc_pair(i), mv[:, 0:1], rstd, ALU.subtract, ALU.mult).then_inc(a_xh.sem, 1)

        def pool_front(pool, i, first=False):
            pool.wait_ge(a_ln.sem, a_ln.at(i, 3))
            pool.tensor_tensor(rstd, vpe, half_neg[:, 0:1], ALU.pow).then_inc(a_rstd.sem, 1)
            pool.wait_ge(a_ctx.sem, a_ctx.at(i, 16))
            if not first:
                pool.wait_ge(a_front.sem, a_front.at(i - 1, 3))
            pool.sem_inc(stand, 1)
            for b in range(2):
                kv = ctx_sb[:, b, :].rearrange("p (g o d) -> p g o d", o=1, d=HD).broadcast_to([P, 8, 4, HD])
                pool.tensor_copy(k_rep[:, b, :].rearrange("p (g o d) -> p g o d", o=4, d=HD), kv) \
                    .then_inc(a_rep.sem, 1)
            if not first:
                pool.wait_ge(a_pv.sem, a_pv.at(i - 1, 8))
            pool.sem_inc(stand, 1)
            pool.tensor_copy(v17[:, :, :, 0:HD], ctx_sb.rearrange("p b (g d) -> p b g d", d=HD)) \
                .then_inc(a_v17.sem, 1)

        def pe_front(pe, i, first=False, second=False):
            pe.wait_ge(a_xh.sem, a_xh.at(i, 1))
            if not first:
                pe.wait_ge(a_kT.sem, a_kT.at(i - 1, 1))
            for j in range(KT):
                mm = pe.transpose(bank[6][:, j * P:(j + 1) * P], xh[:, j * P:(j + 1) * P], ident[:, :])
            mm.then_inc(a_front.sem, 1)
            pe.wait_ge(a_rep.sem, a_rep.at(i, 2))
            if not (first or second):
                pe.wait_ge(a_pt_sb.sem, a_pt_sb.at(i - 1, 0))
            for b in range(2):
                for j in range(KT):
                    mm = pe.transpose(bank[4 + b][:, j * T_CTX:(j + 1) * T_CTX],
                                      k_rep[:, b, j * P:(j + 1) * P], ident[:, :])
                mm.then_inc(a_front.sem, 1)

        def act_front(act, i, first=False):
            act.wait_ge(a_front.sem, a_front.at(i, 1))
            if not first:
                act.wait_ge(a_score.sem, a_score.at(i - 1, 2))
            act.activation(xhT, bank[6][:, :], ACT.Copy).then_inc(a_kT.sem, 1)
            for b in range(2):
                act.wait_ge(a_front.sem, a_front.at(i, 2 + b))
                for e in range(2):
                    act.activation(k_eo[:, b, e, :], bank[4 + b][:, :], ACT.Copy, scale=parity[:, e:e + 1]) \
                        .then_inc(a_kT.sem, 1)

        def pe_scores(pe, i, half, first=False):
            if half == 0:
                pe.wait_ge(a_kT.sem, a_kT.at(i, 5))
                if not first:
                    pe.wait_ge(a_masked.sem, a_masked.at(i, 0))
            else:
                pe.wait_ge(a_masked.sem, a_masked.at(i, 4))
            for jj in range(2):
                j = 2 * half + jj
                for e in range(2):
                    col = (2 * jj + e) * T_CTX
                    for r in range(4):
                        for b in range(2):
                            mm = pe.matmul(bank[r][64 * b:64 * b + 64, col:col + T_CTX],
                                           xhT[32 * r:32 * r + 32, j, 64 * b:64 * b + 64],
                                           k_eo[32 * r:32 * r + 32, b, e, j * T_CTX:(j + 1) * T_CTX],
                                           start=True, stop=True)
            mm.then_inc(a_score.sem, 1)

        def dve_mask(dve, i, half, first=False):
            dve.wait_ge(a_score.sem, a_score.at(i, half + 1))
            if not first:
                dve.wait_ge(a_pt.sem, a_pt.at(i - 1, 4 * half + 4))
            for r in range(4):
                dve.scalar_tensor_tensor(
                    out=prob[:, half, r, :].rearrange("p (h t) -> p h t", t=T_CTX),
                    in0=bank[r][:, :].rearrange("p (h t) -> p h t", t=T_CTX), scalar=HD ** -0.5,
                    in1=maskb.unsqueeze(1).broadcast_to([P, 4, T_CTX]),
                    op0=ALU.mult, op1=ALU.add).then_inc(a_masked.sem, 1)

        def dve_softmax(dve, i, half, first=False):
            heads = prob[:, half, :, :].rearrange("p r (h t) -> p (r h) t", t=T_CTX)
            dve.wait_ge(a_masked.sem, a_masked.at(i, 4 * half + 4))
            if not (first and half == 0):
                dve.wait_ge(a_sub.sem, a_sub.at(i, half))
            dve.tensor_reduce(mx, heads, AX_X, ALU.max).then_inc(a_max.sem, 1)
            dve.wait_ge(a_max.sem, a_max.at(i, half + 1))
            dve.tensor_tensor(heads, heads, mx.unsqueeze(2).broadcast_to([P, 16, T_CTX]), ALU.subtract) \
                .then_inc(a_sub.sem, 1)

        def act_exp(act, i, half):
            act.wait_ge(a_sub.sem, a_sub.at(i, half + 1))
            act.activation(prob[:, half, :, :], prob[:, half, :, :], ACT.Exp).then_inc(a_exp.sem, 1)

        def pe_values(pe, i, half, first=False, last=False):
            def turn_probs(r):
                if r == 0:
                    pe.wait_ge(a_exp.sem, a_exp.at(i, half + 1))
                if 4 * half + r < 2 and not last:
                    pe.wait_ge(a_kT.sem, a_kT.at(i + 1, 3 + 2 * r))
                else:
                    pe.wait_ge(a_pt_sb.sem, a_pt_sb.at(i, 4 * half + r - 1))
                for q in range(4):
                    mm = pe.transpose(bank[4 + r % 2][:, q * P:(q + 1) * P], prob[:, half, r, q * P:(q + 1) * P],
                                      ident[:, :])
                mm.then_inc(a_pt.sem, 1)

            def weigh(r):
                pe.wait_ge(a_pt_sb.sem, a_pt_sb.at(i, 4 * half + r + 1))
                if r == 0:
                    pe.wait_ge(a_v17.sem, a_v17.at(i, 1))
                    if half == 1:
                        pe.wait_ge(a_out.sem, a_out.at(i, 2))
                    elif not first:
                        pe.wait_ge(a_out.sem, a_out.at(i - 1, 5))
                for q in range(4):
                    jj, e = q // 2, q % 2
                    kv = 4 * half + 2 * jj + r // 2
                    col = (8 * jj + 2 * r + e) * (HD + 1)
                    for b in range(2):
                        mm = pe.matmul(bank[7][64 * b:64 * b + 64, col:col + HD + 1],
                                       pt[:, r % 2, q * P + 64 * b:q * P + 64 * b + 64], v17[:, b, kv, :],
                                       start=True, stop=True)
                mm.then_inc(a_pv.sem, 1)

            turn_probs(0)
            for r in range(1, 4):
                turn_probs(r)
                weigh(r - 1)
            weigh(3)

        def act_copy_probs(act, i, half, first=False):
            for r in range(4):
                act.wait_ge(a_pt.sem, a_pt.at(i, 4 * half + r + 1))
                n = 4 * half + r - 1
                if n >= 1:
                    act.wait_ge(a_pv.sem, a_pv.at(i, n))
                elif not first:
                    act.wait_ge(a_pv.sem, a_pv.at(i - 1, n + 8))
                act.activation(pt[:, r % 2, :], bank[4 + r % 2][:, :], ACT.Copy).then_inc(a_pt_sb.sem, 1)

        def dve_out(dve, i, half, first=False):
            o = bank[7][:, 0:16 * (HD + 1)].rearrange("p (h d) -> p h d", d=HD + 1)
            dve.wait_ge(a_pv.sem, a_pv.at(i, 4 * half + 4))
            if not (first and half == 0):
                dve.wait_ge(a_out.sem, a_out.at(i, 3 * half))
            dve.reciprocal(rden, o[:, :, HD]).then_inc(a_out.sem, 1)
            dve.wait_ge(a_out.sem, a_out.at(i, 3 * half + 1))
            dve.tensor_tensor(att.rearrange("p (h d) -> p h d", d=HD), o[:, :, 0:HD],
                              rden.unsqueeze(2).broadcast_to([P, 16, HD]), ALU.mult).then_inc(a_out.sem, 1)
            dve.wait_ge(a_out.sem, a_out.at(i, 3 * half + 2))
            x_half = acc_pair(i)[:, 256 * half:256 * half + 256]
            if half == 0:
                dve.wait_ge(a_xh.sem, a_xh.at(i, 1))
            dve.tensor_tensor(x_half, x_half, att, ALU.add).then_inc(a_out.sem, 1)

        used[0] = 0
        b_xh = view(4, DM)
        b_xT = view(KT, TOK)
        w_dt_sb = view(KT, H)
        dtb = view(1, parts=H)
        alog = view(1, parts=H)
        a_neg = view(2, parts=H)
        absv = view(TOK, parts=H)
        expv = view(TOK, parts=H)
        lnv = view(TOK, parts=H)
        dtv = view(TOK, parts=H)
        dav = view(8, SEQ, parts=H)
        b_stats = view(4, 6)
        b_mv = view(4, 2)
        b_vpe = view(4)
        b_rstd = view(4)

        b_w = signal("b_w", 48)
        b_a = signal("b_a", 2)
        b_stat = signal("b_stat", 9)
        b_rs = signal("b_rs", 1)
        b_xn = signal("b_xn", 4)
        b_t = signal("b_t", 4)
        b_tc = signal("b_tc", 4)
        b_st = signal("b_st", 16)
        b_dt = signal("b_dt", 1)
        b_sp = signal("b_sp", 4)
        b_sm = signal("b_sm", 2)
        b_z = signal("b_z", 1)
        b_da = signal("b_da", 16)
        b_tt = signal("b_tt", 1)
        b_tk = signal("b_tk", 1)

        def acc_slot(tile):
            return (tile + 1) % TILES

        def b_dve(dve, u, first=False):
            slot = acc_slot(u)
            for q in range(4):
                dve.bn_stats(b_stats[:, q, :], acc[:, slot * 4 + q, :]).then_inc(b_stat.sem, 1)
            if not first:
                dve.wait_ge(b_xn.sem, b_xn.at(u - 1, 4))
            for q in range(4):
                dve.wait_ge(b_stat.sem, b_stat.at(u, q + 1))
                dve.sem_inc(stand, 1)
                dve.bn_aggr(b_mv[:, q, :], b_stats[:, q, :]).then_inc(b_stat.sem, 1)
            dve.wait_ge(b_stat.sem, b_stat.at(u, 8))
            dve.tensor_scalar(b_vpe, b_mv[:, :, 1], EPS, None, ALU.add).then_inc(b_stat.sem, 1)
            dve.wait_ge(b_rs.sem, b_rs.at(u, 1))
            if not first:
                dve.wait_ge(b_t.sem, b_t.at(u - 1, 4))
            for q in range(4):
                dve.tensor_scalar(b_xh[:, q, :], acc[:, slot * 4 + q, :], b_mv[:, q, 0:1], b_rstd[:, q:q + 1],
                                  ALU.subtract, ALU.mult).then_inc(b_xn.sem, 1)
            dve.wait_ge(b_sp.sem, b_sp.at(u, 1))
            if not first:
                dve.wait_ge(b_tt.sem, b_tt.at(u - 1, 1))
                dve.wait_ge(b_sp.sem, b_sp.at(u - 1, 4))
            dve.tensor_scalar(dtv, bank[4][0:H, :], dtb, 0.0, ALU.add, ALU.max).then_inc(b_sm.sem, 1)
            dve.wait_ge(b_sm.sem, b_sm.at(u, 1))
            dve.wait_ge(b_sp.sem, b_sp.at(u, 3))
            dve.tensor_tensor(dtv, dtv, lnv, ALU.add).then_inc(b_sm.sem, 1)
            dve.wait_ge(b_tt.sem, b_tt.at(u, 1))
            dve.tensor_copy(dt_tok[:, bass.ds(u * 4, 4), :], bank[5][:, 0:4 * H].rearrange("p (q h) -> p q h", h=H)) \
                .then_inc(b_tk.sem, 1)

        def b_pool(pool, u, first=False):
            pool.wait_ge(b_stat.sem, b_stat.at(u, 9))
            pool.tensor_tensor(b_rstd, b_vpe, half_neg[:, :], ALU.pow).then_inc(b_rs.sem, 1)
            pool.wait_ge(b_sp.sem, b_sp.at(u, 4))
            pool.sem_inc(stand, 1)
            pool.memset(dav[:, :, 0:1], 0.0).then_inc(b_z.sem, 1)

        def b_pe(pe, u, first=False):
            pe.wait_ge(b_xn.sem, b_xn.at(u, 4))
            for k in range(KT):
                if not first:
                    pe.wait_ge(b_tc.sem, b_tc.at(u - 1, k + 1))
                for q in range(4):
                    mm = pe.transpose(bank[k][:, q * P:(q + 1) * P], b_xh[:, q, k * P:(k + 1) * P], ident[:, :])
                mm.then_inc(b_t.sem, 1)
            if first:
                pe.wait_ge(b_w.sem, 48)
            else:
                pe.wait_ge(b_sm.sem, b_sm.at(u - 1, 1))
            for k in range(KT):
                pe.wait_ge(b_tc.sem, b_tc.at(u, k + 1))
                mm = pe.matmul(bank[4][0:H, :], w_dt_sb[:, k, :], b_xT[:, k, :], start=k == 0, stop=k == KT - 1)
            mm.then_inc(b_dt.sem, 1)
            pe.wait_ge(b_sm.sem, b_sm.at(u, 2))
            if not first:
                pe.wait_ge(b_tk.sem, b_tk.at(u - 1, 1))
            pe.sem_inc(stand, 1)
            for q in range(4):
                mm = pe.transpose(bank[5][:, q * H:(q + 1) * H], dtv[:, q * P:(q + 1) * P], ident[0:H, 0:H])
            mm.then_inc(b_tt.sem, 1)

        def b_act(act, u, first=False):
            for k in range(KT):
                act.wait_ge(b_t.sem, b_t.at(u, k + 1))
                if k == 0 and not first:
                    act.wait_ge(b_st.sem, b_st.at(u - 1, 16))
                    act.wait_ge(b_dt.sem, b_dt.at(u - 1, 1))
                act.activation(b_xT[:, k, :], bank[k][:, :], ACT.Copy).then_inc(b_tc.sem, 1)
            act.wait_ge(b_dt.sem, b_dt.at(u, 1))
            act.activation(absv, bank[4][0:H, :], ACT.Abs, bias=dtb).then_inc(b_sp.sem, 1)
            act.wait_ge(b_sp.sem, b_sp.at(u, 1))
            act.activation(expv, absv, ACT.Exp, scale=-1.0).then_inc(b_sp.sem, 1)
            act.wait_ge(b_sp.sem, b_sp.at(u, 2))
            if not first:
                act.wait_ge(b_sm.sem, b_sm.at(u - 1, 2))
            act.activation(lnv, expv, ACT.Ln, bias=1.0).then_inc(b_sp.sem, 1)
            act.wait_ge(b_sm.sem, b_sm.at(u, 2))
            if not first:
                act.wait_ge(b_da.sem, b_da.at(u - 1, 16))
            act.activation(dav, dtv.rearrange("p (b t) -> p b t", t=SEQ), ACT.Exp, scale=a_neg[:, 1:2]).then_inc(b_sp.sem, 1)

        def b_sp_store(sp, u):
            sp.wait_ge(b_tc.sem, b_tc.at(u, 4))
            sp.sem_inc(stand, 1)
            sp.dma_start(xt_d[u], b_xT).then_inc(b_st.sem, 16)
            sp.wait_ge(b_z.sem, b_z.at(u, 1))
            sp.sem_inc(stand, 1)
            sp.dma_start(da_d[bass.ds(u * 8, 8)].rearrange("b h t -> h b t"), dav).then_inc(b_da.sem, 16)
            sp.wait_ge(b_st.sem, b_st.at(u, 16))
            sp.wait_ge(b_da.sem, b_da.at(u, 16))
            sp.sem_inc(stand, 1)

        used[0] = 0
        w_bcx = view(KT, CT * P)
        w_gate = view(KT, GATES * P)
        w_o = view(4, DM)
        xT = view(2, KT, TOK)
        cv = view(3, TOK)
        bc = view(2, TOK)
        xs = view(4, TOK)
        gs = view(4, TOK)
        y = view(4, TOK)
        yn = view(4, TOK)
        sq = view(4, TOK)
        mm_sb = view(4, HG * SEQ)
        da = view(4, HG * SEQ)
        dtx = view(4, 4 * P)
        ms = view(4)
        rr = view(4)
        ones = view(1)

        c_xt = [signal(f"c_xt{n}", 16) for n in range(2)]
        c_da = signal("c_da", 32)
        c_wbcx = signal("c_wbcx", 16)
        c_wgate = signal("c_wgate", 16)
        c_wo = signal("c_wo", 16)
        c_wn = signal("c_wn", 1)
        c_init = signal("c_init", 2)
        c_proj = signal("c_proj", CT + GATES)
        c_cb = signal("c_cb", 1)
        c_t = signal("c_t", 4)
        c_y = signal("c_y", 2)
        c_norm = signal("c_norm", 1)
        c_o = signal("c_o", 4)
        c_tap = signal("c_tap", CT)
        c_silu = signal("c_silu", CT)
        c_gate = signal("c_gate", GATES, GATES)
        c_sq = signal("c_sq", 1)
        c_xd = signal("c_xd", 4, 4)
        c_conv = signal("c_conv", 3 * CT)
        c_yadd = signal("c_yadd", 4)
        c_yn = signal("c_yn", 1)
        c_rms = signal("c_rms", 1)
        c_r = signal("c_r", 1)
        c_acc = signal("c_acc", 4)
        c_scan = signal("c_scan", 4)
        c_m = signal("c_m", 4, 4)
        c_dtx = signal("c_dtx", 4, 4)

        def project(pe, it, n, first_wait=None):
            b = bank[n % 3]
            if n >= 3:
                m, turn = n - 3, it
            else:
                m, turn = (9, 7, 8)[n], it - 1
            if m < CT:
                pe.wait_ge(c_conv.sem, c_conv.at(turn, 3 * m + 3))
            else:
                pe.wait_ge(c_gate.sem, c_gate.at(turn, m - CT + 1))
            w = w_bcx[:, :, n * P:(n + 1) * P] if n < CT else w_gate[:, :, (n - CT) * P:(n - CT + 1) * P]
            for k in range(KT):
                mm = pe.matmul(b[:, :], w[:, k, :], xT[:, par_of[0], k, :], start=k == 0, stop=k == KT - 1)
            mm.then_inc(c_proj.sem, 1)

        par_of = [0]

        def heads_out(pe, it, half):
            pe.wait_ge(c_m.sem, c_m.at(it - 1, 2 * half + 2))
            pe.wait_ge(c_dtx.sem, c_dtx.at(it - 1, 2 * half + 2))
            if half == 1:
                pe.wait_ge(c_yadd.sem, c_yadd.at(it, 2))
            pe.sem_inc(stand, 1)
            for q2 in range(2):
                q = 2 * half + q2
                for h in range(HG):
                    for b in range(2):
                        mm = pe.matmul(bank[4 + b][64 * (h % 2):64 * (h % 2) + 64,
                                                   (h // 2) * P + q2 * SEQ:(h // 2) * P + (q2 + 1) * SEQ],
                                       dtx[64 * b:64 * b + 64, q, h * HP:(h + 1) * HP],
                                       mm_sb[64 * b:64 * b + 64, q, h * SEQ:(h + 1) * SEQ], start=True, stop=True)
            mm.then_inc(c_y.sem, 1)

        def out_product(pe, it):
            pe.wait_ge(c_sq.sem, c_sq.at(it, 1))
            for q in range(4):
                for t in range(4):
                    mm = pe.matmul(bank[3][:, q:q + 1], sq[:, t, q * P:(q + 1) * P], ones, start=t == 0, stop=t == 3)
            mm.then_inc(c_norm.sem, 1)
            pe.wait_ge(c_yn.sem, c_yn.at(it, 1))
            for q in range(4):
                if q >= 2:
                    pe.wait_ge(c_acc.sem, c_acc.at(it, q - 1))
                for t in range(4):
                    mm = pe.matmul(bank[6 + q % 2][:, :], yn[:, t, q * P:(q + 1) * P], w_o[:, t, :],
                                   start=t == 0, stop=t == 3)
                mm.then_inc(c_o.sem, 1)

        def c_pe_turn(pe, g, j, par):
            it = g * TILES + j * 2 + par
            par_of[0] = par
            pe.wait_ge(c_xt[par].sem, c_xt[par].at(g * 4 + j, 16))
            pe.wait_ge(c_wbcx.sem, c_wbcx.at(g, 16))
            project(pe, it, 0)
            project(pe, it, 1)
            heads_out(pe, it, 0)
            project(pe, it, 2)
            heads_out(pe, it, 1)
            for n in range(3, CT):
                project(pe, it, n)
            if par == 1:
                pe.wait_ge(c_wn.sem, c_wn.at(g, 1))
            out_product(pe, it)
            pe.wait_ge(c_wgate.sem, c_wgate.at(g, 16))
            for n in range(CT, CT + GATES):
                project(pe, it, n)
            pe.wait_ge(c_silu.sem, c_silu.at(it, 2))
            pe.wait_ge(c_rms.sem, c_rms.at(it, 1))
            for q in range(4):
                for b in range(2):
                    at = q * P + b * SEQ
                    mm = pe.matmul(bank[3][64 * b:64 * b + 64, q * SEQ:(q + 1) * SEQ], bc[:, 0, at:at + SEQ],
                                   bc[:, 1, at:at + SEQ], start=True, stop=True)
            mm.then_inc(c_cb.sem, 1)
            pe.wait_ge(c_silu.sem, c_silu.at(it, CT))
            for q in range(4):
                if q < 2:
                    pe.wait_ge(c_acc.sem, c_acc.at(it, 3 + q))
                else:
                    pe.wait_ge(c_dtx.sem, c_dtx.at(it, q - 1))
                for t in range(4):
                    mm = pe.transpose(bank[6 + q % 2][:, t * P:(t + 1) * P], xs[:, t, q * P:(q + 1) * P], ident[:, :])
                mm.then_inc(c_t.sem, 1)

        def c_act_turn(act, g, j, par):
            it = g * TILES + j * 2 + par

            def tap(n):
                i = g * CT + n
                act.wait_ge(c_proj.sem, c_proj.at(it, n + 1))
                if n >= 3:
                    act.wait_ge(c_silu.sem, c_silu.at(it, n - 2))
                act.sem_inc(stand, 1)
                act.activation(cv[:, n % 3, :], bank[n % 3][:, :], ACT.Identity, bias=cb[:, bass.ds(i, 1)],
                               scale=cw[:, bass.ds(i, 1), 3]).then_inc(c_tap.sem, 1)

            def silu(n):
                act.wait_ge(c_conv.sem, c_conv.at(it, 3 * n + 3))
                act.activation(bc[:, n, :] if n < 2 else xs[:, n - 2, :], cv[:, n % 3, :], ACT.Silu) \
                    .then_inc(c_silu.sem, 1)

            tap(0)
            tap(1)
            for n in range(CT - 2):
                silu(n)
                tap(n + 2)
                if n == 2:
                    act.wait_ge(c_yadd.sem, c_yadd.at(it, 4))
                    act.activation(sq, y, ACT.Square).then_inc(c_sq.sem, 1)
            silu(CT - 2)
            silu(CT - 1)
            act.wait_ge(c_yn.sem, c_yn.at(it, 1))
            for t in range(4):
                act.wait_ge(c_silu.sem, c_silu.at(it, 3 + t))
                act.sem_inc(stand, 1)
                act.activation(y[:, t, :], xs[:, t, :], ACT.Copy, scale=dsk[:, bass.ds(g * 4 + t, 1)]).then_inc(c_xd.sem, 1)
            for n in range(GATES):
                act.wait_ge(c_proj.sem, c_proj.at(it, CT + n + 1))
                act.activation(gs[:, n, :], bank[(CT + n) % 3][:, :], ACT.Silu).then_inc(c_gate.sem, 1)

        def y_add(dve, it, half):
            dve.wait_ge(c_y.sem, c_y.at(it, half + 1))
            if half == 0:
                dve.wait_ge(c_xd.sem, c_xd.at(it - 1, 4))
            for b in range(2):
                part = y.rearrange("p c (q b t) -> p c q b t", b=2, t=SEQ)[:, :, 2 * half:2 * half + 2, b, :]
                dve.tensor_tensor(part, part, bank[4 + b][:, :].rearrange("p (c q t) -> p c q t", q=2, t=SEQ), ALU.add) \
                    .then_inc(c_yadd.sem, 1)

        def y_gate(dve, it):
            dve.wait_ge(c_yadd.sem, c_yadd.at(it, 4))
            dve.wait_ge(c_gate.sem, c_gate.at(it - 1, GATES))
            dve.tensor_tensor(yn, y, gs, ALU.mult).then_inc(c_yn.sem, 1)

        def add_out(dve, it, slot):
            dve.wait_ge(c_norm.sem, c_norm.at(it, 1))
            dve.tensor_scalar(ms, bank[3][:, 0:4], 1.0 / 512, EPS, ALU.mult, ALU.add).then_inc(c_rms.sem, 1)
            dve.wait_ge(c_r.sem, c_r.at(it, 1))
            for q in range(4):
                dve.wait_ge(c_o.sem, c_o.at(it, q + 1))
                a = acc[:, slot * 4 + q, :]
                dve.scalar_tensor_tensor(out=a, in0=bank[6 + q % 2][:, :], scalar=rr[:, q:q + 1], in1=a,
                                         op0=ALU.mult, op1=ALU.add).then_inc(c_acc.sem, 1)

        def c_dve_turn(dve, g, j, par):
            it = g * TILES + j * 2 + par
            u = j * 2 + par

            def conv(n):
                i = g * CT + n
                h = bank[n % 3][:, :].rearrange("p (b t) -> p b t", t=SEQ)
                o = cv[:, n % 3, :].rearrange("p (b t) -> p b t", t=SEQ)
                for tap in range(3):
                    s = 3 - tap
                    if tap == 0:
                        dve.wait_ge(c_tap.sem, c_tap.at(it, n + 1))
                    else:
                        dve.wait_ge(c_conv.sem, c_conv.at(it, 3 * n + tap))
                    dve.scalar_tensor_tensor(out=o[:, :, s:], in0=h[:, :, 0:SEQ - s], scalar=cw[:, bass.ds(i, 1), tap],
                                             in1=o[:, :, s:], op0=ALU.mult, op1=ALU.add).then_inc(c_conv.sem, 1)

            conv(0)
            conv(1)
            y_add(dve, it, 0)
            conv(2)
            y_add(dve, it, 1)
            conv(3)
            y_gate(dve, it)
            conv(4)
            conv(5)
            add_out(dve, it, u)
            dve.wait_ge(c_da.sem, c_da.at(it, 32))
            for q in range(4):
                dve.tensor_tensor_scan(mm_sb[:, q, :], da[:, q, :], eye[:, :], 0.0, ALU.mult, ALU.add) \
                    .then_inc(c_scan.sem, 1)
            dve.wait_ge(c_cb.sem, c_cb.at(it, 1))
            for q in range(4):
                dve.wait_ge(c_scan.sem, c_scan.at(it, q + 1))
                m = mm_sb[:, q, :].rearrange("p (h t) -> p h t", t=SEQ)
                dve.tensor_tensor(m, m, bank[3][:, q * SEQ:(q + 1) * SEQ].unsqueeze(1).broadcast_to([P, HG, SEQ]),
                                  ALU.mult).then_inc(c_m.sem, 1)
            for q in range(4):
                dve.wait_ge(c_t.sem, c_t.at(it, q + 1))
                dt = dt_tok[:, u * 4 + q, bass.ds(g * HG, HG)].unsqueeze(2).broadcast_to([P, HG, HP])
                dve.tensor_tensor(dtx[:, q, :].rearrange("p (h c) -> p h c", c=HP),
                                  bank[6 + q % 2][:, :].rearrange("p (h c) -> p h c", c=HP), dt, ALU.mult) \
                    .then_inc(c_dtx.sem, 1)

        def c_pool_turn(pool, it):
            pool.wait_ge(c_rms.sem, c_rms.at(it, 1))
            pool.tensor_tensor(rr, ms, half_neg[:, :], ALU.pow).then_inc(c_r.sem, 1)

        def c_pool_group(pool, g):
            c_pool_turn(pool, g * TILES)
            pool.wait_ge(c_o.sem, c_o.at(g * TILES, 4))
            pool.sem_inc(stand, 1)
            pool.dma_start(w_o, w_out[g]).then_inc(c_wo.sem, 16)
            pool.wait_ge(c_wo.sem, c_wo.at(g, 16))
            pool.sem_inc(stand, 1)
            pool.tensor_tensor(w_o, w_o, nw[:, bass.ds(g * 4, 4)].unsqueeze(2).broadcast_to([P, 4, DM]), ALU.mult) \
                .then_inc(c_wn.sem, 1)
            with pool.Fori(1, TILES) as u:
                c_pool_turn(pool, g * TILES + u)

        def load_da(sp, tile, g):
            for b in range(2):
                src = da_d[bass.ds(tile * 8, 8)].rearrange("(q b) h t -> b q (h t)", b=2)[b][
                    :, bass.ds(g * (HG * SEQ), HG * SEQ)]
                sp.dma_start(da[64 * b:64 * b + 64], src.unsqueeze(0).broadcast_to([64, 4, HG * SEQ])) \
                    .then_inc(c_da.sem, 16)

        def c_sp_turn(sp, g, j, par, last=False):
            it = g * TILES + j * 2 + par
            u = j * 2 + par
            final = isinstance(j, int) and u == TILES - 1
            if not (final and last):
                sp.wait_ge(c_scan.sem, c_scan.at(it, 4))
                sp.sem_inc(stand, 1)
                sp.wait_ge(c_da.sem, c_da.at(it, 32))
                sp.sem_inc(stand, 1)
                load_da(sp, 0 if final else u + 1, g + 1 if final else g)
            if not (isinstance(j, int) and j == 3 and last):
                sp.wait_ge(c_proj.sem, c_proj.at(it, CT + GATES))
                sp.sem_inc(stand, 1)
                sp.dma_start(xT[:, par], xt_d[par] if isinstance(j, int) and j == 3 else xt_d[u + 2]) \
                    .then_inc(c_xt[par].sem, 16)
            if final and not last:
                sp.dma_start(w_bcx, w_groups[g + 1][:, :, 0:CT * P]).then_inc(c_wbcx.sem, 16)
                sp.dma_start(w_gate, w_groups[g + 1][:, :, CT * P:]).then_inc(c_wgate.sem, 16)

        def c_sp(sp):
            sp.dma_start(w_bcx, w_groups[0][:, :, 0:CT * P]).then_inc(c_wbcx.sem, 16)
            sp.dma_start(w_gate, w_groups[0][:, :, CT * P:]).then_inc(c_wgate.sem, 16)
            for par in range(2):
                sp.dma_start(xT[:, par], xt_d[par]).then_inc(c_xt[par].sem, 16)
            load_da(sp, 0, 0)

            def group(g, last=False):
                with sp.Fori(0, 3) as j:
                    c_sp_turn(sp, g, j, 0)
                    c_sp_turn(sp, g, j, 1)
                c_sp_turn(sp, g, 3, 0, last)
                c_sp_turn(sp, g, 3, 1, last)

            with sp.Fori(0, G - 1) as g:
                group(g)
            group(G - 1, last=True)

        used[0] = 0
        wr = view(KT, E)
        br = view(E)
        eb = view(DM, parts=E)
        d_xh = view(4, DM)
        d_xT = view(KT, TOK)
        lg = view(4, E)
        d_mx = view(4)
        top = view(4, 8)
        rest = view(4, E)
        wd = view(4, E)
        d_sum = view(4)
        d_rs = view(4)
        d_ts = view(4)
        ws = view(4)
        wT = view(TOK, parts=E)
        d_stats = view(4, 6)
        d_mv = view(4, 2)
        d_vpe = view(4)
        d_rstd = view(4)

        d_w = signal("d_w", 48)
        d_stat = signal("d_stat", 9)
        d_rp = signal("d_rp", 1)
        d_xn = signal("d_xn", 4)
        d_t = signal("d_t", 4)
        d_tc = signal("d_tc", 4)
        d_lg = signal("d_lg", 1)
        d_l = signal("d_l", 3)
        d_e = signal("d_e", 1)
        d_k = signal("d_k", 14)
        d_wt = signal("d_wt", 1)
        d_wc = signal("d_wc", 1)
        d_mix = signal("d_mix", 4)
        d_o = signal("d_o", 8)
        d_st = signal("d_st", 16)

        def d_dve(dve, n, first=False):
            for q in range(4):
                dve.bn_stats(d_stats[:, q, :], acc[:, n * 4 + q, :]).then_inc(d_stat.sem, 1)
            for q in range(4):
                dve.wait_ge(d_stat.sem, d_stat.at(n, q + 1))
                dve.sem_inc(stand, 1)
                dve.bn_aggr(d_mv[:, q, :], d_stats[:, q, :]).then_inc(d_stat.sem, 1)
            dve.wait_ge(d_stat.sem, d_stat.at(n, 8))
            dve.tensor_scalar(d_vpe, d_mv[:, :, 1], EPS, None, ALU.add).then_inc(d_stat.sem, 1)
            dve.wait_ge(d_rp.sem, d_rp.at(n, 1))
            for q in range(4):
                dve.tensor_scalar(d_xh[:, q, :], acc[:, n * 4 + q, :], d_mv[:, q, 0:1], d_rstd[:, q:q + 1],
                                  ALU.subtract, ALU.mult).then_inc(d_xn.sem, 1)
            dve.wait_ge(d_lg.sem, d_lg.at(n, 1))
            dve.tensor_tensor(lg, bank[4][:, 0:4 * E].rearrange("p (q e) -> p q e", e=E),
                              br.unsqueeze(1).broadcast_to([P, 4, E]), ALU.add).then_inc(d_l.sem, 1)
            dve.wait_ge(d_l.sem, d_l.at(n, 1))
            dve.tensor_reduce(d_mx, lg, AX_X, ALU.max).then_inc(d_l.sem, 1)
            dve.wait_ge(d_l.sem, d_l.at(n, 2))
            dve.tensor_tensor(lg, lg, d_mx.unsqueeze(2).broadcast_to([P, 4, E]), ALU.subtract).then_inc(d_l.sem, 1)
            dve.wait_ge(d_e.sem, d_e.at(n, 1))
            dve.tensor_reduce(d_sum, lg, AX_X, ALU.add).then_inc(d_k.sem, 1)
            for q in range(4):
                dve.max(top[:, q, :], lg[:, q, :]).then_inc(d_k.sem, 1)
            dve.wait_ge(d_k.sem, d_k.at(n, 1))
            dve.reciprocal(d_rs, d_sum).then_inc(d_k.sem, 1)
            dve.wait_ge(d_k.sem, d_k.at(n, 5))
            dve.tensor_reduce(d_ts, top, AX_X, ALU.add).then_inc(d_k.sem, 1)
            for q in range(4):
                dve.sem_inc(stand, 1)
                dve.match_replace(rest[:, q, :], top[:, q, :], lg[:, q, :], 0.0).then_inc(d_k.sem, 1)
            dve.wait_ge(d_k.sem, d_k.at(n, 11))
            dve.tensor_tensor(wd, lg, rest, ALU.subtract).then_inc(d_k.sem, 1)
            dve.wait_ge(d_k.sem, d_k.at(n, 12))
            dve.tensor_tensor(wd, wd, d_rs.unsqueeze(2).broadcast_to([P, 4, E]), ALU.mult).then_inc(d_k.sem, 1)
            dve.tensor_tensor(ws, d_ts, d_rs, ALU.mult).then_inc(d_k.sem, 1)
            dve.wait_ge(d_k.sem, d_k.at(n, 14))
            for q in range(4):
                a = acc[:, n * 4 + q, :]
                dve.scalar_tensor_tensor(out=a, in0=d_xh[:, q, :], scalar=ws[:, q:q + 1], in1=a,
                                         op0=ALU.mult, op1=ALU.add).then_inc(d_o.sem, 1)
            for q in range(4):
                a = acc[:, n * 4 + q, :]
                dve.wait_ge(d_o.sem, d_o.at(n, q + 1))
                dve.wait_ge(d_mix.sem, d_mix.at(n, q + 1))
                dve.tensor_tensor(a, a, bank[6 + q % 2][:, :], ALU.add).then_inc(d_o.sem, 1)

        def d_pe(pe, n, first=False):
            pe.wait_ge(d_xn.sem, d_xn.at(n, 4))
            for k in range(KT):
                if not first:
                    pe.wait_ge(d_tc.sem, d_tc.at(n - 1, k + 1))
                for q in range(4):
                    mm = pe.transpose(bank[k][:, q * P:(q + 1) * P], d_xh[:, q, k * P:(k + 1) * P], ident[:, :])
                mm.then_inc(d_t.sem, 1)
            pe.wait_ge(d_tc.sem, d_tc.at(n, 4))
            for q in range(4):
                for k in range(KT):
                    mm = pe.matmul(bank[4][:, q * E:(q + 1) * E], d_xT[:, k, q * P:(q + 1) * P], wr[:, k, :],
                                   start=k == 0, stop=k == KT - 1)
            mm.then_inc(d_lg.sem, 1)
            pe.wait_ge(d_k.sem, d_k.at(n, 13))
            pe.sem_inc(stand, 1)
            for q in range(4):
                mm = pe.transpose(bank[5][0:E, q * P:(q + 1) * P], wd[:, q, :], ident[:, :])
            mm.then_inc(d_wt.sem, 1)
            pe.wait_ge(d_wc.sem, d_wc.at(n, 1))
            for q in range(4):
                if q >= 2:
                    pe.wait_ge(d_o.sem, d_o.at(n, q + 3))
                elif not first:
                    pe.wait_ge(d_o.sem, d_o.at(n - 1, q + 7))
                pe.sem_inc(stand, 1)
                pe.matmul(bank[6 + q % 2][:, :], wT[:, q * P:(q + 1) * P], eb, start=True, stop=True) \
                    .then_inc(d_mix.sem, 1)

        def d_act(act, n, first=False):
            for k in range(KT):
                act.wait_ge(d_t.sem, d_t.at(n, k + 1))
                act.activation(d_xT[:, k, :], bank[k][:, :], ACT.Copy).then_inc(d_tc.sem, 1)
            act.wait_ge(d_l.sem, d_l.at(n, 3))
            act.activation(lg, lg, ACT.Exp).then_inc(d_e.sem, 1)
            act.wait_ge(d_wt.sem, d_wt.at(n, 1))
            act.activation(wT, bank[5][0:E, :], ACT.Copy).then_inc(d_wc.sem, 1)

        def d_pool(pool, n):
            pool.wait_ge(d_stat.sem, d_stat.at(n, 9))
            pool.tensor_tensor(d_rstd, d_vpe, half_neg[:, :], ALU.pow).then_inc(d_rp.sem, 1)

        def d_sp(sp):
            sp.wait_ge(c_acc.sem, c_acc.at(G * TILES, 4))
            for dst, src in ((wr, w_router), (br, b_router.broadcast_to([P, E])), (eb, e_bias)):
                sp.dma_start(dst, src).then_inc(d_w.sem, 16)
            for n in range(TILES):
                t = (n + 7) % TILES
                sp.wait_ge(d_o.sem, d_o.at(n, 8))
                sp.dma_start(out_v[:, 4 * t:4 * t + 4, :], acc[:, 4 * n:4 * n + 4, :]).then_inc(d_st.sem, 16)
            sp.wait_ge(d_st.sem, d_st.at(TILES - 1, 16))

        block = ctx.enter_context(nc.Block())

        @block.sync
        def _(sp):
            for dst, src in ((ident[:, :], ident_in), (parity[:, :], parity_in), (eye[:, :], eye_in),
                             (cw[:, :, :], conv_w), (cb[:, :], conv_b), (dsk[:, :], d_skip), (nw[:, :], norm_w),
                             (maskb[0:SEQ, :], mask), (maskb[SEQ:P, :], mask)):
                sp.dma_start(dst, src).then_inc(consts_in, 16)
            load_pair(sp, 0, first=True)
            with sp.Fori(1, PAIRS) as i:
                load_pair(sp, i)
            sp.wait_ge(a_out.sem, a_out.at(PAIRS - 1, 6))
            sp.wait_ge(b_go, 1)
            for dst, src in ((w_dt_sb, w_dt), (dtb, dt_bias), (alog, a_log)):
                sp.dma_start(dst, src).then_inc(b_w.sem, 16)
            with sp.Fori(0, TILES) as u:
                b_sp_store(sp, u)
            sp.wait_ge(c_go, 5)
            c_sp(sp)
            d_sp(sp)

        @block.gpsimd
        def _(pool):
            pool.memset(half_neg[:, :], -0.5).then_inc(half_set, 1)
            pool.memset(v17[:, :, :, HD:HD + 1], 1.0).then_inc(a_v17.sem, 1)
            pool.wait_ge(half_set, 1)
            pool_front(pool, 0, first=True)
            with pool.Fori(1, PAIRS) as i:
                pool_front(pool, i)
            def b_turns():
                b_pool(pool, 0, first=True)
                with pool.Fori(1, TILES) as u:
                    b_pool(pool, u)
            pool.wait_ge(b_go, 1)
            b_turns()
            pool.wait_ge(b_tk.sem, b_tk.at(TILES - 1, 1))
            pool.wait_ge(b_sp.sem, b_sp.at(TILES - 1, 4))
            pool.wait_ge(b_da.sem, b_da.at(TILES - 1, 16))
            pool.wait_ge(b_st.sem, b_st.at(TILES - 1, 16))
            pool.memset(mm_sb, 0.0).then_inc(c_m.sem, 4)
            pool.memset(dtx, 0.0).then_inc(c_dtx.sem, 4)
            pool.memset(y, 0.0).then_inc(c_xd.sem, 4)
            pool.memset(gs, 0.0).then_inc(c_gate.sem, 4)
            pool.memset(w_o, 0.0).then_inc(c_init.sem, 1)
            pool.memset(ones, 1.0).then_inc(c_init.sem, 1)
            pool.wait_ge(c_init.sem, 2)
            pool.sem_inc(c_go, 5)
            with pool.Fori(0, G) as g:
                c_pool_group(pool, g)
            c_pool_turn(pool, G * TILES)
            pool.wait_ge(d_w.sem, 48)
            d_pool(pool, 0)
            with pool.Fori(1, TILES) as n:
                d_pool(pool, n)

        @block.scalar
        def _(act):
            act.wait_ge(consts_in, N_CONSTS)
            act_front(act, 0, first=True)

            def turn(i, first=False, last=False):
                act_exp(act, i, 0)
                if not last:
                    act_front(act, i + 1)
                act_copy_probs(act, i, 0, first)
                act_exp(act, i, 1)
                act_copy_probs(act, i, 1)

            turn(0, first=True)
            with act.Fori(1, PAIRS - 1) as i:
                turn(i)
            turn(PAIRS - 1, last=True)
            act.wait_ge(b_w.sem, 48)
            act.activation(a_neg[:, 0:1], alog, ACT.Exp).then_inc(b_a.sem, 1)
            act.wait_ge(b_a.sem, 1)
            act.activation(a_neg[:, 1:2], a_neg[:, 0:1], ACT.Copy, scale=-1.0).then_inc(b_a.sem, 1)
            act.wait_ge(b_a.sem, 2)
            b_act(act, 0, first=True)
            with act.Fori(1, TILES) as u:
                b_act(act, u)
            act.wait_ge(c_go, 5)
            with act.Fori(0, G) as g:
                with act.Fori(0, 4) as j:
                    c_act_turn(act, g, j, 0)
                    c_act_turn(act, g, j, 1)
            act.wait_ge(c_yadd.sem, c_yadd.at(G * TILES, 4))
            act.activation(sq, y, ACT.Square).then_inc(c_sq.sem, 1)
            act.wait_ge(d_w.sem, 48)
            d_act(act, 0, first=True)
            with act.Fori(1, TILES) as n:
                d_act(act, n)

        @block.vector
        def _(dve):
            norm_pair(dve, 0, first=True)
            apply_norm(dve, 0, first=True)
            dve.wait_ge(consts_in, N_CONSTS)

            def turn(i, first=False, last=False):
                dve_mask(dve, i, 0, first)
                if not last:
                    norm_pair(dve, i + 1)
                dve_softmax(dve, i, 0, first)
                if not last:
                    apply_norm(dve, i + 1)
                dve_mask(dve, i, 1, first)
                dve_softmax(dve, i, 1)
                dve_out(dve, i, 0, first)
                dve_out(dve, i, 1)

            turn(0, first=True)
            with dve.Fori(1, PAIRS - 1) as i:
                turn(i)
            turn(PAIRS - 1, last=True)
            dve.wait_ge(a_out.sem, a_out.at(PAIRS - 1, 6))
            dve.wait_ge(a_pv.sem, a_pv.at(PAIRS - 1, 8))
            dve.sem_inc(b_go, 1)
            dve.wait_ge(b_w.sem, 48)
            b_dve(dve, 0, first=True)
            with dve.Fori(1, TILES) as u:
                b_dve(dve, u)
            dve.wait_ge(c_go, 5)
            with dve.Fori(0, G) as g:
                with dve.Fori(0, 4) as j:
                    c_dve_turn(dve, g, j, 0)
                    c_dve_turn(dve, g, j, 1)
            y_add(dve, G * TILES, 0)
            y_add(dve, G * TILES, 1)
            y_gate(dve, G * TILES)
            add_out(dve, G * TILES, 0)
            dve.wait_ge(d_w.sem, 48)
            d_dve(dve, 0, first=True)
            with dve.Fori(1, TILES) as n:
                d_dve(dve, n)

        @block.tensor
        def _(pe):
            pe.wait_ge(consts_in, N_CONSTS)
            pe_front(pe, 0, first=True)

            def turn(i, first=False, last=False):
                pe_scores(pe, i, 0, first)
                pe_scores(pe, i, 1)
                if not last:
                    pe_front(pe, i + 1, second=first)
                pe_values(pe, i, 0, first, last)
                pe_values(pe, i, 1)

            turn(0, first=True)
            with pe.Fori(1, PAIRS - 1) as i:
                turn(i)
            turn(PAIRS - 1, last=True)
            b_pe(pe, 0, first=True)
            with pe.Fori(1, TILES) as u:
                b_pe(pe, u)
            pe.wait_ge(c_go, 5)
            with pe.Fori(0, G) as g:
                with pe.Fori(0, 4) as j:
                    c_pe_turn(pe, g, j, 0)
                    c_pe_turn(pe, g, j, 1)
            heads_out(pe, G * TILES, 0)
            heads_out(pe, G * TILES, 1)
            out_product(pe, G * TILES)
            pe.wait_ge(d_w.sem, 48)
            d_pe(pe, 0, first=True)
            with pe.Fori(1, TILES) as n:
                d_pe(pe, n)


def kernel(**inputs):
    import numpy as np
    import concourse.bacc as bacc
    from concourse.bass_utils import run_bass_kernel_spmd

    a = {k: np.asarray(v) for k, v in inputs.items()}
    w = a["L0_attn_in_proj_w"]
    inner, gn = H * HP, G * N_ST
    gate_r = w[:inner].reshape(G, 512, DM)
    x_r = w[inner:2 * inner].reshape(G, 512, DM)
    b_r = w[2 * inner:2 * inner + gn].reshape(G, P, DM)
    c_r = w[2 * inner + gn:2 * inner + 2 * gn].reshape(G, P, DM)

    def k_major(rows):
        g, n, _ = rows.shape
        return rows.transpose(0, 2, 1).reshape(g, KT, P, n).transpose(0, 2, 1, 3)

    def channel_tiles(rows):
        xs = rows[:inner].reshape(G, 4, P, -1)
        bs = rows[inner:inner + gn].reshape(G, 1, P, -1)
        cs = rows[inner + gn:].reshape(G, 1, P, -1)
        return np.concatenate([bs, cs, xs], 1).transpose(2, 0, 1, 3).reshape(P, G * CT, -1)

    arrays = {
        "x": a["x"], "ctx": a["ctx_1024"], "mask": a["mask_SxS2_ff0"],
        "w_groups": k_major(np.concatenate([b_r, c_r, x_r, gate_r], 1)),
        "w_dt": k_major(w[-H:][None])[0],
        "w_out": a["L0_attn_out_proj_w"].T.reshape(G, 4, P, DM).transpose(0, 2, 1, 3),
        "conv_w": channel_tiles(a["L0_attn_conv_weight"]),
        "conv_b": channel_tiles(a["L0_attn_conv_bias"][:, None])[:, :, 0],
        "dt_bias": a["L0_attn_dt_bias"][:, None], "a_log": a["L0_attn_A_log"][:, None],
        "d_skip": np.repeat(a["L0_attn_D"], HP).reshape(G * 4, P).T,
        "norm_w": a["L0_attn_norm_weight"].reshape(G * 4, P).T,
        "w_router": a["L0_ffn_router_weight"].T.reshape(KT, P, E).transpose(1, 0, 2),
        "b_router": a["L0_ffn_router_bias"][None],
        "e_bias": a["L0_ffn_expert_bias"],
        "ident": np.eye(P, dtype=np.float32),
        "parity": np.stack([1 - np.arange(P) // HD % 2, np.arange(P) // HD % 2], 1).astype(np.float32),
        "eye": np.tile(np.eye(SEQ, dtype=np.float32), (2, HG)),
    }
    arrays = {f"in_{k}": np.ascontiguousarray(v) for k, v in arrays.items()}
    nc = bacc.Bacc("TRN2", target_bir_lowering=False, num_devices=1)
    args = [nc.dram_tensor(k, v.shape, F32, kind="ExternalInput").ap() for k, v in arrays.items()]
    out = nc.dram_tensor("out", [BATCH, SEQ, DM], F32, kind="ExternalOutput").ap()
    xt_d = nc.dram_tensor("xt", [TILES, P, KT, TOK], F32).ap()
    da_d = nc.dram_tensor("da", [BATCH, H, SEQ], F32).ap()
    build(nc, *args, out, xt_d, da_d)
    r = run_bass_kernel_spmd(nc, [arrays], core_ids=[0])
    return r.results[0]["out"]
```

```python
import concourse.bass as bass
from concourse import mybir
from contextlib import ExitStack

F32 = mybir.dt.float32
F16 = mybir.dt.float16
U32 = mybir.dt.uint32
ALU = mybir.AluOpType
ACT = mybir.ActivationFunctionType
AX_X = mybir.AxisListType.X

P = 128
BATCH, SEQ, DM = 64, 64, 512
KT = DM // P
PAIRS = BATCH * SEQ // P
TILES = 8
TOK = 512
T_CTX, C_CTX = 128, 128
HD = 16
H, HP, N_ST, G = 64, 64, 128, 8
HG = H // G
CT = 6
GATES = 4
E = 64
W_TILES = G * (CT + GATES)
W_TURN = (3, 2)
X_SCALE = 1024.0
W_TOP = 2.0 ** 14
EXPONENT = 0x7F800000
EPS = 1e-5
WORK = 30600




class Signal:

    def __init__(self, sem, per, credit=0):
        self.sem, self.per, self.credit = sem, per, credit

    def at(self, turn, n):
        return turn * self.per + (n + self.credit)


def build(nc, x, ctx_in, mask, w_in, w_dt, w_out, conv_w, conv_b, dt_bias, a_log, d_skip, norm_w,
          w_router, b_router, e_bias, ident_in, parity_in, eye_in, out, xt_d, da_d, w_d):
    x_v = x.rearrange("(n b) s d -> n (b s) d", b=2)
    out_v = out.rearrange("(n b) s d -> (b s) n d", b=2)
    ctx_v = ctx_in.rearrange("(n b) t c -> n t b c", b=2)

    with ExitStack() as ctx:
        def sb(name, shape):
            return ctx.enter_context(nc.sbuf_tensor(name, shape, F32))

        def sem(name):
            return ctx.enter_context(nc.semaphore(name))

        def signal(name, per, credit=0):
            return Signal(sem(name), per, credit)

        bank = [ctx.enter_context(nc.psum_tensor(f"bank{i}", [P, 512], F32)) for i in range(8)]

        acc = sb("acc", [P, PAIRS, DM])
        ident = sb("ident", [P, P])
        parity = sb("parity", [P, 2])
        eye = sb("eye", [P, TOK])
        half_neg = sb("half_neg", [P, 4])
        dt_tok = sb("dt_tok", [P, PAIRS, H])
        cw = sb("cw", [P, G * CT, 4])
        cb = sb("cb", [P, G * CT])
        dsk = sb("dsk", [P, G * 4])
        nw = sb("nw", [P, G * 4])
        small = sb("small", [P, 64])
        w_unscale = sb("w_unscale", [P, W_TILES])
        work = sb("work", [P, WORK])
        used = [0]

        def view(*shape, parts=P):
            n = 1
            for s in shape:
                n *= s
            v = work[0:parts, used[0]:used[0] + n]
            used[0] += n
            assert used[0] <= WORK
            if len(shape) == 1:
                return v
            names = "abcd"[:len(shape)]
            return v.rearrange(f"p ({' '.join(names)}) -> p {' '.join(names)}",
                               **{k: s for k, s in zip(names, shape)})

        def halves(v):
            return v.bitcast(F16)

        def acc_pair(i):
            return acc[:, (i + 4) % PAIRS, :]

        consts_in = sem("consts_in")
        N_CONSTS = 16 * 9
        half_set = sem("half_set")
        v_zero = sem("v_zero")
        b_go = sem("b_go")
        c_go = sem("c_go")
        stand = sem("stand")

        used[0] = 0
        maskb = view(T_CTX)
        ctx_sb = view(2, 2, C_CTX)
        k_rep = view(2, 8 * 4 * HD)
        v32 = view(2, 2, 8, 32)
        k_eo = view(2, 2, KT * T_CTX)
        xh = view(DM)
        xhT = view(KT, P)
        prob = view(2, 4, 4 * T_CTX)
        pt = view(2, 4 * P)
        att = view(256)
        outT = view(512)
        w_f = view(sum(W_TURN), KT * P)
        w_s = halves(view(sum(W_TURN), KT * P)).rearrange("p t (s c) -> p t s c", s=2)
        w_max = view(8)
        stats = small[:, 0:6]
        mv = small[:, 8:10]
        rstd = small[:, 12:13]
        low = small[:, 16:48].rearrange("p (f h) -> p f h", f=2)
        rden = small[:, 48:64]
        vpe = small[:, 11:12]

        a_x = signal("a_x", 16)
        a_ctx = [signal(f"a_ctx{n}", 16) for n in range(2)]
        a_ln = signal("a_ln", 3)
        a_rstd = signal("a_rstd", 1)
        a_xh = signal("a_xh", 1)
        a_rep = signal("a_rep", 2)
        a_front = signal("a_front", 3)
        a_kT = signal("a_kT", 5)
        a_v = signal("a_v", 1, 1)
        a_score = signal("a_score", 2)
        a_masked = signal("a_masked", 8)
        a_max = signal("a_max", 2)
        a_sub = signal("a_sub", 2)
        a_exp = signal("a_exp", 10)
        a_pt = signal("a_pt", 8)
        a_pt_sb = signal("a_pt_sb", 8)
        a_pv = signal("a_pv", 8)
        a_outT = signal("a_outT", 2)
        a_back = signal("a_back", 2)
        a_out = signal("a_out", 6)

        a_win = [signal(f"a_win{n}", 16) for n in range(2)]
        a_wmax = signal("a_wmax", 1)
        a_wall = signal("a_wall", 1)
        a_wsc = signal("a_wsc", 4)
        a_whi = signal("a_whi", 1)
        a_wlo = signal("a_wlo", 1)
        a_wst = [signal(f"a_wst{n}", 16) for n in range(2)]

        def w_cut(par):
            return slice(0, W_TURN[0]) if par == 0 else slice(W_TURN[0], sum(W_TURN))

        def w_tiles(r, par):
            return bass.ds(r * sum(W_TURN) + par * W_TURN[0], W_TURN[par])

        def load_w(sp, r, par, first=False):
            if not first:
                sp.wait_ge(a_whi.sem, a_whi.at(2 * r + par - 2, 1))
                sp.wait_ge(a_wlo.sem, a_wlo.at(2 * r + par - 2, 1))
            sp.sem_inc(stand, 1)
            sp.dma_start(w_f[:, w_cut(par)], w_in[:, w_tiles(r, par)]).then_inc(a_win[par].sem, 16)

        def store_w(sp, r, par):
            sp.wait_ge(a_wlo.sem, a_wlo.at(2 * r + par, 1))
            sp.sem_inc(stand, 1)
            sp.dma_start(w_d[:, w_tiles(r, par)], w_s[:, w_cut(par)]).then_inc(a_wst[par].sem, 16)

        def dve_w_max(dve, i, r, par, first=False):
            dve.wait_ge(a_win[par].sem, a_win[par].at(r, 16))
            if not first:
                dve.wait_ge(a_wall.sem, a_wall.at(i - 1, 1))
            dve.sem_inc(stand, 1)
            dve.tensor_reduce(w_max[:, 0:1], w_f[:, w_cut(par)].rearrange("p t c -> p (t c)"), AX_X, ALU.max,
                              apply_absolute_value=True).then_inc(a_wmax.sem, 1)

        def pool_w_max(pool, i, first=False):
            pool.wait_ge(a_wmax.sem, a_wmax.at(i, 1))
            if not first:
                pool.wait_ge(a_wsc.sem, a_wsc.at(i - 1, 1))
            pool.sem_inc(stand, 1)
            pool.partition_all_reduce(w_max[:, 1:2], w_max[:, 0:1], P, bass.bass_isa.ReduceOp.max) \
                .then_inc(a_wall.sem, 1)

        def dve_w_scale(dve, i, r, par, first=False):
            dve.wait_ge(a_wall.sem, a_wall.at(i, 1))
            if not first:
                dve.wait_ge(a_wlo.sem, a_wlo.at(i - 1, 1))
                dve.wait_ge(a_wsc.sem, a_wsc.at(i - 1, 4))
            dve.sem_inc(stand, 1)
            dve.tensor_scalar(w_max[:, 2:3].bitcast(U32), w_max[:, 1:2].bitcast(U32), EXPONENT, None,
                              ALU.bitwise_and).then_inc(a_wsc.sem, 1)
            dve.wait_ge(a_wsc.sem, a_wsc.at(i, 1))
            dve.sem_inc(stand, 1)
            dve.tensor_scalar(w_max[:, 3:4], w_max[:, 2:3], 1 / W_TOP, 2.0 ** -100, ALU.mult, ALU.max) \
                .then_inc(a_wsc.sem, 1)
            dve.wait_ge(a_wsc.sem, a_wsc.at(i, 2))
            dve.sem_inc(stand, 1)
            dve.tensor_scalar(w_unscale[:, w_tiles(r, par)], w_max[:, 3:4].broadcast_to([P, W_TURN[par]]),
                              1 / X_SCALE, None, ALU.mult).then_inc(a_wsc.sem, 1)
            dve.reciprocal(w_max[:, 4:5], w_max[:, 3:4]).then_inc(a_wsc.sem, 1)

        def act_w_high(act, i, r, par, first=False):
            act.wait_ge(a_wsc.sem, a_wsc.at(i, 4))
            if not first:
                act.wait_ge(a_wst[par].sem, a_wst[par].at(r - 1, 16))
            act.sem_inc(stand, 1)
            act.activation(w_s[:, w_cut(par), 0], w_f[:, w_cut(par)], ACT.Copy, scale=w_max[:, 4:5]) \
                .then_inc(a_whi.sem, 1)

        def dve_w_low(dve, i, par):
            dve.wait_ge(a_whi.sem, a_whi.at(i, 1))
            dve.sem_inc(stand, 1)
            dve.scalar_tensor_tensor(out=w_s[:, w_cut(par), 1], in0=w_f[:, w_cut(par)], scalar=w_max[:, 4:5],
                                     in1=w_s[:, w_cut(par), 0], op0=ALU.mult, op1=ALU.subtract) \
                .then_inc(a_wlo.sem, 1)

        def load_pair(sp, i, par, first=False, second=False):
            if not first:
                sp.wait_ge(a_x.sem, a_x.at(i - 1, 16))
            sp.dma_start(acc_pair(i), x_v[i]).then_inc(a_x.sem, 16)
            if not (first or second):
                sp.wait_ge(a_rep.sem, a_rep.at(i - 2, 2))
                sp.sem_inc(stand, 1)
                sp.wait_ge(a_v.sem, a_v.at(i - 2, 1))
                sp.sem_inc(stand, 1)
            sp.dma_start(ctx_sb[:, par], ctx_v[i]).then_inc(a_ctx[par].sem, 16)

        def norm_pair(dve, i, first=False):
            dve.wait_ge(a_x.sem, a_x.at(i, 16))
            if not first:
                dve.wait_ge(a_xh.sem, a_xh.at(i - 1, 1))
            dve.bn_stats(stats, acc_pair(i)).then_inc(a_ln.sem, 1)
            dve.wait_ge(a_ln.sem, a_ln.at(i, 1))
            dve.sem_inc(stand, 1)
            dve.bn_aggr(mv, stats).then_inc(a_ln.sem, 1)
            dve.wait_ge(a_ln.sem, a_ln.at(i, 2))
            dve.tensor_scalar(vpe, mv[:, 1:2], EPS, None, ALU.add).then_inc(a_ln.sem, 1)

        def apply_norm(dve, i, first=False):
            dve.wait_ge(a_rstd.sem, a_rstd.at(i, 1))
            if not first:
                dve.wait_ge(a_front.sem, a_front.at(i - 1, 1))
            dve.tensor_scalar(xh, acc_pair(i), mv[:, 0:1], rstd, ALU.subtract, ALU.mult).then_inc(a_xh.sem, 1)

        def pool_front(pool, i, par, turns, first=False):
            pool.wait_ge(a_ln.sem, a_ln.at(i, 3))
            pool.tensor_tensor(rstd, vpe, half_neg[:, 0:1], ALU.pow).then_inc(a_rstd.sem, 1)
            pool.wait_ge(a_ctx[par].sem, a_ctx[par].at(turns, 16))
            if not first:
                pool.wait_ge(a_front.sem, a_front.at(i - 1, 3))
            pool.sem_inc(stand, 1)
            for b in range(2):
                kv = ctx_sb[:, par, b, :].rearrange("p (g o d) -> p g o d", o=1, d=HD).broadcast_to([P, 8, 4, HD])
                pool.tensor_copy(k_rep[:, b, :].rearrange("p (g o d) -> p g o d", o=4, d=HD), kv) \
                    .then_inc(a_rep.sem, 1)

        def pool_values(pool, i, par, first=False):
            if not first:
                pool.wait_ge(a_pv.sem, a_pv.at(i - 2, 8))
            pool.sem_inc(stand, 1)
            pool.tensor_copy(v32[:, par, :, :, 0:HD], ctx_sb[:, par].rearrange("p b (g d) -> p b g d", d=HD)) \
                .then_inc(a_v.sem, 1)

        def pe_front_x(pe, i, first=False):
            pe.wait_ge(a_xh.sem, a_xh.at(i, 1))
            if not first:
                pe.wait_ge(a_kT.sem, a_kT.at(i - 1, 1))
            for j in range(KT):
                mm = pe.transpose(bank[6][:, j * P:(j + 1) * P], xh[:, j * P:(j + 1) * P], ident[:, :])
            mm.then_inc(a_front.sem, 1)

        def pe_front_k(pe, i, first=False):
            pe.wait_ge(a_rep.sem, a_rep.at(i, 2))
            for b in range(2):
                if not first:
                    pe.wait_ge(a_pt_sb.sem, a_pt_sb.at(i - 1, 3 + b))
                for j in range(KT):
                    mm = pe.transpose(bank[4 + b][:, j * T_CTX:(j + 1) * T_CTX],
                                      k_rep[:, b, j * P:(j + 1) * P], ident[:, :])
                mm.then_inc(a_front.sem, 1)

        def act_front_x(act, i, first=False):
            act.wait_ge(a_front.sem, a_front.at(i, 1))
            if not first:
                act.wait_ge(a_score.sem, a_score.at(i - 1, 2))
            act.activation(xhT, bank[6][:, :], ACT.Copy).then_inc(a_kT.sem, 1)

        def act_front_k(act, i):
            for b in range(2):
                act.wait_ge(a_front.sem, a_front.at(i, 2 + b))
                for e in range(2):
                    act.activation(k_eo[:, b, e, :], bank[4 + b][:, :], ACT.Copy, scale=parity[:, e:e + 1]) \
                        .then_inc(a_kT.sem, 1)

        def pe_scores(pe, i, half, first=False):
            if half == 0:
                pe.wait_ge(a_kT.sem, a_kT.at(i, 5))
                if not first:
                    pe.wait_ge(a_masked.sem, a_masked.at(i, 0))
            else:
                pe.wait_ge(a_masked.sem, a_masked.at(i, 4))
            for jj in range(2):
                j = 2 * half + jj
                for r in range(4):
                    for b in range(2):
                        mm = pe.matmul(bank[r][64 * b:64 * b + 64, 256 * jj:256 * jj + 256],
                                       xhT[32 * r:32 * r + 32, j, 64 * b:64 * b + 64],
                                       k_eo[32 * r:32 * r + 32, b, :, j * T_CTX:(j + 1) * T_CTX],
                                       start=True, stop=True)
            mm.then_inc(a_score.sem, 1)

        def dve_mask(dve, i, half, first=False):
            dve.wait_ge(a_score.sem, a_score.at(i, half + 1))
            if not first:
                dve.wait_ge(a_pt.sem, a_pt.at(i - 1, 4 * half + 4))
            for r in range(4):
                dve.scalar_tensor_tensor(
                    out=prob[:, half, r, :].rearrange("p (h t) -> p h t", t=T_CTX),
                    in0=bank[r][:, :].rearrange("p (h t) -> p h t", t=T_CTX), scalar=-HD ** -0.5,
                    in1=maskb.unsqueeze(1).broadcast_to([P, 4, T_CTX]),
                    op0=ALU.mult, op1=ALU.subtract).then_inc(a_masked.sem, 1)

        def dve_softmax(dve, i, half):
            heads = prob[:, half, :, :].rearrange("p r (h t) -> p (r h) t", t=T_CTX)
            dve.wait_ge(a_masked.sem, a_masked.at(i, 4 * half + 4))
            dve.tensor_reduce(low[:, half, :], heads, AX_X, ALU.min).then_inc(a_max.sem, 1)
            dve.wait_ge(a_max.sem, a_max.at(i, half + 1))
            dve.tensor_tensor(heads[:, 0:12, :], heads[:, 0:12, :],
                              low[:, half, 0:12].unsqueeze(2).broadcast_to([P, 12, T_CTX]), ALU.subtract) \
                .then_inc(a_sub.sem, 1)

        def act_exp(act, i, half):
            act.wait_ge(a_sub.sem, a_sub.at(i, half + 1))
            act.activation(prob[:, half, 0:3, :], prob[:, half, 0:3, :], ACT.Exp, scale=-1.0).then_inc(a_exp.sem, 1)
            for h in range(4):
                p = prob[:, half, 3, h * T_CTX:(h + 1) * T_CTX]
                act.activation(p, p, ACT.Exp, scale=-1.0, bias=low[:, half, 12 + h:13 + h]).then_inc(a_exp.sem, 1)

        def pe_values(pe, i, half, par, first=False, last=False):
            def turn_probs(c):
                if c == 0:
                    pe.wait_ge(a_exp.sem, a_exp.at(i, 5 * half + 1))
                elif c == 1:
                    pe.wait_ge(a_exp.sem, a_exp.at(i, 5 * half + 5))
                if c >= 2 or (half == 1 and last):
                    pe.wait_ge(a_pt_sb.sem, a_pt_sb.at(i, 4 * half + c - 1))
                elif half == 1:
                    pe.wait_ge(a_kT.sem, a_kT.at(i + 1, 3 + 2 * c))
                elif not first:
                    pe.wait_ge(a_pt_sb.sem, a_pt_sb.at(i - 1, 7 + c))
                for r in range(4):
                    at = (2 * (c // 2) + r % 2) * T_CTX
                    mm = pe.transpose(bank[4 + c % 2][:, r * P:(r + 1) * P],
                                      prob[:, half, 2 * (c % 2) + r // 2, at:at + T_CTX], ident[:, :])
                mm.then_inc(a_pt.sem, 1)

            def weigh(c):
                pe.wait_ge(a_pt_sb.sem, a_pt_sb.at(i, 4 * half + c + 1))
                if c == 0:
                    pe.wait_ge(a_v.sem, a_v.at(i, 1))
                    if half == 1:
                        pe.wait_ge(a_out.sem, a_out.at(i, 2))
                    elif not first:
                        pe.wait_ge(a_out.sem, a_out.at(i - 1, 5))
                    pe.sem_inc(stand, 1)
                for b in range(2):
                    mm = pe.matmul(bank[7][32 * c:32 * c + 32, :].rearrange("p (r b s) -> p r b s", r=4, b=2)[:, :, b, :],
                                   v32[:, par, b, 4 * half + c, :],
                                   pt[:, c % 2, :].rearrange("p (r b s) -> p r b s", r=4, b=2)[:, :, b, :],
                                   start=True, stop=True)
                mm.then_inc(a_pv.sem, 1)

            turn_probs(0)
            for c in range(1, 4):
                turn_probs(c)
                weigh(c - 1)
            weigh(3)

        def act_outT(act, i, half):
            act.wait_ge(a_pv.sem, a_pv.at(i, 4 * half + 4))
            act.activation(outT, bank[7][:, :], ACT.Copy).then_inc(a_outT.sem, 1)

        def pe_back(pe, i, half):
            pe.wait_ge(a_outT.sem, a_outT.at(i, half + 1))
            for r in range(4):
                mm = pe.transpose(bank[7][:, r * P:(r + 1) * P], outT[:, r * P:(r + 1) * P], ident[:, :])
            mm.then_inc(a_back.sem, 1)

        def act_copy_probs(act, i, half, first=False):
            for r in range(4):
                act.wait_ge(a_pt.sem, a_pt.at(i, 4 * half + r + 1))
                n = 4 * half + r - 1
                if n >= 1:
                    act.wait_ge(a_pv.sem, a_pv.at(i, n))
                elif not first:
                    act.wait_ge(a_pv.sem, a_pv.at(i - 1, n + 8))
                act.activation(pt[:, r % 2, :], bank[4 + r % 2][:, :], ACT.Copy).then_inc(a_pt_sb.sem, 1)

        def dve_out(dve, i, half, first=False):
            o = bank[7][:, :].rearrange("p (r c d) -> p r c d", r=4, d=32)
            rd = rden.rearrange("p (r c) -> p r c", r=4)
            dve.wait_ge(a_back.sem, a_back.at(i, half + 1))
            if not (first and half == 0):
                dve.wait_ge(a_out.sem, a_out.at(i, 3 * half))
            dve.reciprocal(rd, o[:, :, :, HD]).then_inc(a_out.sem, 1)
            dve.wait_ge(a_out.sem, a_out.at(i, 3 * half + 1))
            dve.tensor_tensor(att.rearrange("p (c r d) -> p r c d", r=4, d=HD), o[:, :, :, 0:HD],
                              rd.unsqueeze(3).broadcast_to([P, 4, 4, HD]), ALU.mult).then_inc(a_out.sem, 1)
            dve.wait_ge(a_out.sem, a_out.at(i, 3 * half + 2))
            x_half = acc_pair(i)[:, 256 * half:256 * half + 256]
            if half == 0:
                dve.wait_ge(a_xh.sem, a_xh.at(i, 1))
            dve.tensor_tensor(x_half, x_half, att, ALU.add).then_inc(a_out.sem, 1)

        def a_turns(engine, turn):
            turn(0, 0, 0, first=True)
            turn(1, 0, 1)
            with engine.Fori(1, PAIRS // 2 - 1) as r:
                turn(2 * r, r, 0)
                turn(2 * r + 1, r, 1)
            turn(PAIRS - 2, PAIRS // 2 - 1, 0, late=True)
            turn(PAIRS - 1, PAIRS // 2 - 1, 1, late=True, last=True)

        used[0] = 0
        b_xh = view(4, DM)
        b_xT = view(KT, TOK)
        b_split = halves(view(2, KT, TOK // 2))
        w_dt_sb = view(KT, H)
        dtb = view(1, parts=H)
        alog = view(1, parts=H)
        a_neg = view(2, parts=H)
        absv = view(TOK, parts=H)
        expv = view(TOK, parts=H)
        lnv = view(TOK, parts=H)
        dtv = view(TOK, parts=H)
        dav = view(8, SEQ, parts=H)
        b_stats = view(4, 6)
        b_mv = view(4, 2)
        b_vpe = view(4)
        b_rstd = view(4)

        b_w = signal("b_w", 48)
        b_a = signal("b_a", 2)
        b_stat = signal("b_stat", 9)
        b_rs = signal("b_rs", 1)
        b_xn = signal("b_xn", 4)
        b_t = signal("b_t", 4)
        b_tc = signal("b_tc", 4)
        b_hi = signal("b_hi", 4)
        b_lo = signal("b_lo", 4)
        b_st = signal("b_st", 16)
        b_dt = signal("b_dt", 1)
        b_sp = signal("b_sp", 4)
        b_sm = signal("b_sm", 2)
        b_z = signal("b_z", 1)
        b_da = signal("b_da", 16)
        b_tt = signal("b_tt", 1)
        b_tk = signal("b_tk", 1)

        def acc_slot(tile):
            return (tile + 1) % TILES

        def b_dve(dve, u, first=False):
            slot = acc_slot(u)
            for q in range(4):
                dve.bn_stats(b_stats[:, q, :], acc[:, slot * 4 + q, :]).then_inc(b_stat.sem, 1)
            if not first:
                dve.wait_ge(b_xn.sem, b_xn.at(u - 1, 4))
            for q in range(4):
                dve.wait_ge(b_stat.sem, b_stat.at(u, q + 1))
                dve.sem_inc(stand, 1)
                dve.bn_aggr(b_mv[:, q, :], b_stats[:, q, :]).then_inc(b_stat.sem, 1)
            dve.wait_ge(b_stat.sem, b_stat.at(u, 8))
            dve.tensor_scalar(b_vpe, b_mv[:, :, 1], EPS, None, ALU.add).then_inc(b_stat.sem, 1)
            dve.wait_ge(b_rs.sem, b_rs.at(u, 1))
            if not first:
                dve.wait_ge(b_t.sem, b_t.at(u - 1, 4))
            for q in range(4):
                dve.tensor_scalar(b_xh[:, q, :], acc[:, slot * 4 + q, :], b_mv[:, q, 0:1], b_rstd[:, q:q + 1],
                                  ALU.subtract, ALU.mult).then_inc(b_xn.sem, 1)
            for k in range(KT):
                dve.wait_ge(b_hi.sem, b_hi.at(u, k + 1))
                dve.scalar_tensor_tensor(out=b_split[:, 1, k, :], in0=bank[k][:, :], scalar=X_SCALE,
                                         in1=b_split[:, 0, k, :], op0=ALU.mult, op1=ALU.subtract) \
                    .then_inc(b_lo.sem, 1)
            dve.wait_ge(b_sp.sem, b_sp.at(u, 1))
            if not first:
                dve.wait_ge(b_tt.sem, b_tt.at(u - 1, 1))
                dve.wait_ge(b_sp.sem, b_sp.at(u - 1, 4))
            dve.tensor_scalar(dtv, bank[4][0:H, :], dtb, 0.0, ALU.add, ALU.max).then_inc(b_sm.sem, 1)
            dve.wait_ge(b_sm.sem, b_sm.at(u, 1))
            dve.wait_ge(b_sp.sem, b_sp.at(u, 3))
            dve.tensor_tensor(dtv, dtv, lnv, ALU.add).then_inc(b_sm.sem, 1)
            dve.wait_ge(b_tt.sem, b_tt.at(u, 1))
            dve.tensor_copy(dt_tok[:, bass.ds(u * 4, 4), :], bank[5][:, 0:4 * H].rearrange("p (q h) -> p q h", h=H)) \
                .then_inc(b_tk.sem, 1)

        def b_pool(pool, u, first=False):
            pool.wait_ge(b_stat.sem, b_stat.at(u, 9))
            pool.tensor_tensor(b_rstd, b_vpe, half_neg[:, :], ALU.pow).then_inc(b_rs.sem, 1)
            pool.wait_ge(b_sp.sem, b_sp.at(u, 4))
            pool.sem_inc(stand, 1)
            pool.memset(dav[:, :, 0:1], 0.0).then_inc(b_z.sem, 1)

        def b_pe(pe, u, first=False):
            pe.wait_ge(b_xn.sem, b_xn.at(u, 4))
            for k in range(KT):
                if not first:
                    pe.wait_ge(b_lo.sem, b_lo.at(u - 1, k + 1))
                for q in range(4):
                    mm = pe.transpose(bank[k][:, q * P:(q + 1) * P], b_xh[:, q, k * P:(k + 1) * P], ident[:, :])
                mm.then_inc(b_t.sem, 1)
            if first:
                pe.wait_ge(b_w.sem, 48)
            else:
                pe.wait_ge(b_sm.sem, b_sm.at(u - 1, 1))
            for k in range(KT):
                pe.wait_ge(b_tc.sem, b_tc.at(u, k + 1))
                mm = pe.matmul(bank[4][0:H, :], w_dt_sb[:, k, :], b_xT[:, k, :], start=k == 0, stop=k == KT - 1)
            mm.then_inc(b_dt.sem, 1)
            pe.wait_ge(b_sm.sem, b_sm.at(u, 2))
            if not first:
                pe.wait_ge(b_tk.sem, b_tk.at(u - 1, 1))
            pe.sem_inc(stand, 1)
            for q in range(4):
                mm = pe.transpose(bank[5][:, q * H:(q + 1) * H], dtv[:, q * P:(q + 1) * P], ident[0:H, 0:H])
            mm.then_inc(b_tt.sem, 1)

        def b_act(act, u, first=False):
            for k in range(KT):
                act.wait_ge(b_t.sem, b_t.at(u, k + 1))
                if k == 0 and not first:
                    act.wait_ge(b_st.sem, b_st.at(u - 1, 16))
                    act.wait_ge(b_dt.sem, b_dt.at(u - 1, 1))
                act.activation(b_xT[:, k, :], bank[k][:, :], ACT.Copy).then_inc(b_tc.sem, 1)
                act.activation(b_split[:, 0, k, :], bank[k][:, :], ACT.Copy, scale=X_SCALE).then_inc(b_hi.sem, 1)
            act.wait_ge(b_dt.sem, b_dt.at(u, 1))
            act.activation(absv, bank[4][0:H, :], ACT.Abs, bias=dtb).then_inc(b_sp.sem, 1)
            act.wait_ge(b_sp.sem, b_sp.at(u, 1))
            act.activation(expv, absv, ACT.Exp, scale=-1.0).then_inc(b_sp.sem, 1)
            act.wait_ge(b_sp.sem, b_sp.at(u, 2))
            if not first:
                act.wait_ge(b_sm.sem, b_sm.at(u - 1, 2))
            act.activation(lnv, expv, ACT.Ln, bias=1.0).then_inc(b_sp.sem, 1)
            act.wait_ge(b_sm.sem, b_sm.at(u, 2))
            if not first:
                act.wait_ge(b_da.sem, b_da.at(u - 1, 16))
            act.activation(dav, dtv.rearrange("p (b t) -> p b t", t=SEQ), ACT.Exp, scale=a_neg[:, 1:2]).then_inc(b_sp.sem, 1)

        def b_sp_store(sp, u):
            sp.wait_ge(b_lo.sem, b_lo.at(u, 4))
            sp.sem_inc(stand, 1)
            sp.dma_start(xt_d[u], b_split).then_inc(b_st.sem, 16)
            sp.wait_ge(b_z.sem, b_z.at(u, 1))
            sp.sem_inc(stand, 1)
            sp.dma_start(da_d[bass.ds(u * 8, 8)].rearrange("b h t -> h b t"), dav).then_inc(b_da.sem, 16)
            sp.wait_ge(b_st.sem, b_st.at(u, 16))
            sp.wait_ge(b_da.sem, b_da.at(u, 16))
            sp.sem_inc(stand, 1)

        used[0] = 0
        w_g = halves(view(CT + GATES, KT * P)).rearrange("p n (s k c) -> p n s k c", s=2, k=KT)
        w_o = view(4, DM)
        xT = halves(view(2, 2, KT, TOK // 2))
        cv = view(3, TOK)
        bc = view(2, TOK)
        xs = view(4, TOK)
        gs = view(4, TOK)
        y = view(4, TOK)
        yn = view(4, TOK)
        sq = view(4, TOK)
        mm_sb = view(4, HG * SEQ)
        da = view(4, HG * SEQ)
        dtx = view(4, 4 * P)
        ms = view(4)
        rr = view(4)
        ones = view(1)

        c_xt = [signal(f"c_xt{n}", 16) for n in range(2)]
        c_da = signal("c_da", 32)
        c_wbcx = signal("c_wbcx", 16)
        c_wgate = signal("c_wgate", 16)
        c_wo = signal("c_wo", 16)
        c_wn = signal("c_wn", 1)
        c_init = signal("c_init", 3)
        c_proj = signal("c_proj", CT + GATES)
        c_cb = signal("c_cb", 1)
        c_t = signal("c_t", 4)
        c_y = signal("c_y", 2)
        c_norm = signal("c_norm", 1)
        c_o = signal("c_o", 4)
        c_tap = signal("c_tap", CT)
        c_silu = signal("c_silu", CT)
        c_gate = signal("c_gate", GATES, GATES)
        c_sq = signal("c_sq", 1)
        c_ssum = signal("c_ssum", 2)
        c_xd = signal("c_xd", 4, 4)
        c_conv = signal("c_conv", 3 * CT)
        c_yadd = signal("c_yadd", 4)
        c_yn = signal("c_yn", 1)
        c_rms = signal("c_rms", 1)
        c_r = signal("c_r", 1)
        c_acc = signal("c_acc", 4)
        c_scan = signal("c_scan", 4)
        c_m = signal("c_m", 4, 4)
        c_dtx = signal("c_dtx", 4, 4)

        def project(pe, it, par, n):
            b = bank[n % 3]
            if n >= 3:
                m, turn = n - 3, it
            else:
                m, turn = (9, 7, 8)[n], it - 1
            if m < CT:
                pe.wait_ge(c_conv.sem, c_conv.at(turn, 3 * m + 3))
            else:
                pe.wait_ge(c_gate.sem, c_gate.at(turn, m - CT + 1))
            steps = [(w_part, x_part, k) for w_part, x_part in ((0, 0), (0, 1), (1, 0)) for k in range(KT)]
            for s, (w_part, x_part, k) in enumerate(steps):
                mm = pe.matmul(b[:, :], w_g[:, n, w_part, k, :], xT[:, par, x_part, k, :],
                               start=s == 0, stop=s == len(steps) - 1)
            mm.then_inc(c_proj.sem, 1)

        def heads_out(pe, it, half):
            pe.wait_ge(c_m.sem, c_m.at(it - 1, 2 * half + 2))
            pe.wait_ge(c_dtx.sem, c_dtx.at(it - 1, 2 * half + 2))
            pe.sem_inc(stand, 1)
            for q2 in range(2):
                q = 2 * half + q2
                for h in range(HG):
                    for b in range(2):
                        mm = pe.matmul(bank[4 + 2 * half + b][64 * (h % 2):64 * (h % 2) + 64,
                                                   (h // 2) * P + q2 * SEQ:(h // 2) * P + (q2 + 1) * SEQ],
                                       dtx[64 * b:64 * b + 64, q, h * HP:(h + 1) * HP],
                                       mm_sb[64 * b:64 * b + 64, q, h * SEQ:(h + 1) * SEQ], start=True, stop=True)
            mm.then_inc(c_y.sem, 1)

        def norm_sums(pe, it):
            pe.wait_ge(c_ssum.sem, c_ssum.at(it, 2))
            for q in range(4):
                mm = pe.matmul(bank[3][:, q:q + 1], sq[:, 0, q * P:(q + 1) * P], ones, start=True, stop=True)
            mm.then_inc(c_norm.sem, 1)

        def out_product(pe, it, q):
            if q == 0:
                pe.wait_ge(c_yn.sem, c_yn.at(it, 1))
            if q >= 2:
                pe.wait_ge(c_acc.sem, c_acc.at(it, q - 1))
            for t in range(4):
                mm = pe.matmul(bank[6 + q % 2][:, :], yn[:, t, q * P:(q + 1) * P], w_o[:, t, :],
                               start=t == 0, stop=t == 3)
            mm.then_inc(c_o.sem, 1)

        def cb_product(pe, it):
            pe.wait_ge(c_silu.sem, c_silu.at(it, 2))
            pe.wait_ge(c_rms.sem, c_rms.at(it, 1))
            for q in range(4):
                for b in range(2):
                    at = q * P + b * SEQ
                    mm = pe.matmul(bank[3][64 * b:64 * b + 64, q * SEQ:(q + 1) * SEQ], bc[:, 0, at:at + SEQ],
                                   bc[:, 1, at:at + SEQ], start=True, stop=True)
            mm.then_inc(c_cb.sem, 1)

        def turn_x(pe, it, q):
            if q == 0:
                pe.wait_ge(c_silu.sem, c_silu.at(it, CT))
                pe.wait_ge(c_yadd.sem, c_yadd.at(it, 4))
            if q >= 2:
                pe.wait_ge(c_acc.sem, c_acc.at(it, q + 1))
            for t in range(4):
                mm = pe.transpose(bank[4 + q][:, t * P:(t + 1) * P], xs[:, t, q * P:(q + 1) * P], ident[:, :])
            mm.then_inc(c_t.sem, 1)

        def c_pe_turn(pe, g, j, par):
            it = g * TILES + j * 2 + par
            heads_out(pe, it, 0)
            pe.wait_ge(c_xt[par].sem, c_xt[par].at(g * 4 + j, 16))
            pe.wait_ge(c_wbcx.sem, c_wbcx.at(g, 16))
            project(pe, it, par, 0)
            project(pe, it, par, 1)
            heads_out(pe, it, 1)
            for n in range(2, CT):
                project(pe, it, par, n)
            if par == 1:
                pe.wait_ge(c_wn.sem, c_wn.at(g, 1))
            out_product(pe, it, 0)
            out_product(pe, it, 1)
            norm_sums(pe, it)
            pe.wait_ge(c_wgate.sem, c_wgate.at(g, 16))
            project(pe, it, par, CT)
            out_product(pe, it, 2)
            cb_product(pe, it)
            project(pe, it, par, CT + 1)
            out_product(pe, it, 3)
            turn_x(pe, it, 0)
            turn_x(pe, it, 1)
            project(pe, it, par, CT + 2)
            project(pe, it, par, CT + 3)
            turn_x(pe, it, 2)
            turn_x(pe, it, 3)

        def c_act_turn(act, g, j, par):
            it = g * TILES + j * 2 + par

            def tap(n):
                i = g * CT + n
                act.wait_ge(c_proj.sem, c_proj.at(it, n + 1))
                if n >= 3:
                    act.wait_ge(c_silu.sem, c_silu.at(it, n - 2))
                act.sem_inc(stand, 1)
                act.activation(cv[:, n % 3, :], bank[n % 3][:, :], ACT.Identity, bias=cb[:, bass.ds(i, 1)],
                               scale=cw[:, bass.ds(i, 1), 3]).then_inc(c_tap.sem, 1)

            def silu(n):
                act.wait_ge(c_conv.sem, c_conv.at(it, 3 * n + 3))
                act.activation(bc[:, n, :] if n < 2 else xs[:, n - 2, :], cv[:, n % 3, :], ACT.Silu) \
                    .then_inc(c_silu.sem, 1)

            tap(0)
            tap(1)
            for n in range(CT - 2):
                silu(n)
                tap(n + 2)
                if n == 2:
                    act.wait_ge(c_yadd.sem, c_yadd.at(it, 4))
                    act.activation(sq, y, ACT.Square).then_inc(c_sq.sem, 1)
            silu(CT - 2)
            silu(CT - 1)
            act.wait_ge(c_yn.sem, c_yn.at(it, 1))
            for t in range(4):
                act.wait_ge(c_silu.sem, c_silu.at(it, 3 + t))
                act.sem_inc(stand, 1)
                act.activation(y[:, t, :], xs[:, t, :], ACT.Copy, scale=dsk[:, bass.ds(g * 4 + t, 1)]).then_inc(c_xd.sem, 1)
            for n in range(GATES):
                act.wait_ge(c_proj.sem, c_proj.at(it, CT + n + 1))
                act.sem_inc(stand, 1)
                act.activation(gs[:, n, :], bank[(CT + n) % 3][:, :], ACT.Silu,
                               scale=w_unscale[:, bass.ds(g * (CT + GATES) + CT + n, 1)]).then_inc(c_gate.sem, 1)

        def y_add(dve, it, half):
            dve.wait_ge(c_y.sem, c_y.at(it, half + 1))
            if half == 0:
                dve.wait_ge(c_xd.sem, c_xd.at(it - 1, 4))
            for b in range(2):
                part = y.rearrange("p c (q b t) -> p c q b t", b=2, t=SEQ)[:, :, 2 * half:2 * half + 2, b, :]
                dve.tensor_tensor(part, part, bank[4 + 2 * half + b][:, :].rearrange("p (c q t) -> p c q t", q=2, t=SEQ), ALU.add) \
                    .then_inc(c_yadd.sem, 1)

        def y_gate(dve, it):
            dve.wait_ge(c_yadd.sem, c_yadd.at(it, 4))
            dve.wait_ge(c_gate.sem, c_gate.at(it - 1, GATES))
            dve.tensor_tensor(yn, y, gs, ALU.mult).then_inc(c_yn.sem, 1)

        def mean_square(dve, it):
            dve.wait_ge(c_norm.sem, c_norm.at(it, 1))
            dve.tensor_scalar(ms, bank[3][:, 0:4], 1.0 / 512, EPS, ALU.mult, ALU.add).then_inc(c_rms.sem, 1)
            dve.wait_ge(c_r.sem, c_r.at(it, 1))

        def add_out(dve, it, slot, q):
            dve.wait_ge(c_o.sem, c_o.at(it, q + 1))
            a = acc[:, slot * 4 + q, :]
            dve.scalar_tensor_tensor(out=a, in0=bank[6 + q % 2][:, :], scalar=rr[:, q:q + 1], in1=a,
                                     op0=ALU.mult, op1=ALU.add).then_inc(c_acc.sem, 1)

        def c_dve_turn(dve, g, j, par):
            it = g * TILES + j * 2 + par
            u = j * 2 + par

            def conv(n):
                i = g * CT + n
                h = bank[n % 3][:, :].rearrange("p (b t) -> p b t", t=SEQ)
                o = cv[:, n % 3, :].rearrange("p (b t) -> p b t", t=SEQ)
                for tap in range(3):
                    s = 3 - tap
                    if tap == 0:
                        dve.wait_ge(c_tap.sem, c_tap.at(it, n + 1))
                    else:
                        dve.wait_ge(c_conv.sem, c_conv.at(it, 3 * n + tap))
                    dve.scalar_tensor_tensor(out=o[:, :, s:], in0=h[:, :, 0:SEQ - s], scalar=cw[:, bass.ds(i, 1), tap],
                                             in1=o[:, :, s:], op0=ALU.mult, op1=ALU.add).then_inc(c_conv.sem, 1)

            conv(0)
            conv(1)
            y_add(dve, it, 0)
            y_add(dve, it, 1)
            conv(2)
            y_gate(dve, it)
            conv(3)
            conv(4)
            conv(5)
            mean_square(dve, it)
            add_out(dve, it, u, 0)
            add_out(dve, it, u, 1)
            dve.wait_ge(c_da.sem, c_da.at(it, 32))
            for q in range(4):
                dve.tensor_tensor_scan(mm_sb[:, q, :], da[:, q, :], eye[:, :], 0.0, ALU.mult, ALU.add) \
                    .then_inc(c_scan.sem, 1)
            add_out(dve, it, u, 2)
            dve.wait_ge(c_cb.sem, c_cb.at(it, 1))
            for q in range(4):
                dve.wait_ge(c_scan.sem, c_scan.at(it, q + 1))
                m = mm_sb[:, q, :].rearrange("p (h t) -> p h t", t=SEQ)
                dve.tensor_tensor(m, m, bank[3][:, q * SEQ:(q + 1) * SEQ].unsqueeze(1).broadcast_to([P, HG, SEQ]),
                                  ALU.mult).then_inc(c_m.sem, 1)
            add_out(dve, it, u, 3)
            for q in range(4):
                dve.wait_ge(c_t.sem, c_t.at(it, q + 1))
                dt = dt_tok[:, u * 4 + q, bass.ds(g * HG, HG)].unsqueeze(2).broadcast_to([P, HG, HP])
                dve.tensor_tensor(dtx[:, q, :].rearrange("p (h c) -> p h c", c=HP),
                                  bank[4 + q][:, :].rearrange("p (h c) -> p h c", c=HP), dt, ALU.mult) \
                    .then_inc(c_dtx.sem, 1)

        def c_pool_turn(pool, it):
            pool.wait_ge(c_sq.sem, c_sq.at(it, 1))
            pool.tensor_tensor(sq[:, 0:2, :], sq[:, 0:2, :], sq[:, 2:4, :], ALU.add).then_inc(c_ssum.sem, 1)
            pool.wait_ge(c_ssum.sem, c_ssum.at(it, 1))
            pool.tensor_tensor(sq[:, 0, :], sq[:, 0, :], sq[:, 1, :], ALU.add).then_inc(c_ssum.sem, 1)
            pool.wait_ge(c_rms.sem, c_rms.at(it, 1))
            pool.tensor_tensor(rr, ms, half_neg[:, :], ALU.pow).then_inc(c_r.sem, 1)

        def c_pool_group(pool, g):
            c_pool_turn(pool, g * TILES)
            pool.wait_ge(c_o.sem, c_o.at(g * TILES, 4))
            pool.sem_inc(stand, 1)
            pool.dma_start(w_o, w_out[g]).then_inc(c_wo.sem, 16)
            pool.wait_ge(c_wo.sem, c_wo.at(g, 16))
            pool.sem_inc(stand, 1)
            pool.tensor_tensor(w_o, w_o, nw[:, bass.ds(g * 4, 4)].unsqueeze(2).broadcast_to([P, 4, DM]), ALU.mult) \
                .then_inc(c_wn.sem, 1)
            with pool.Fori(1, TILES) as u:
                c_pool_turn(pool, g * TILES + u)

        def load_da(sp, tile, g):
            for b in range(2):
                src = da_d[bass.ds(tile * 8, 8)].rearrange("(q b) h t -> b q (h t)", b=2)[b][
                    :, bass.ds(g * (HG * SEQ), HG * SEQ)]
                sp.dma_start(da[64 * b:64 * b + 64], src.unsqueeze(0).broadcast_to([64, 4, HG * SEQ])) \
                    .then_inc(c_da.sem, 16)

        def load_weights(sp, g, a, b, arrived):
            sp.dma_start(w_g[:, a:b].rearrange("p n s k c -> p n (s k c)"),
                         w_d[:, bass.ds(g * (CT + GATES) + a, b - a)].rearrange("p n s c -> p n (s c)")) \
                .then_inc(arrived.sem, 16)

        def c_sp_turn(sp, g, j, par, last=False):
            it = g * TILES + j * 2 + par
            u = j * 2 + par
            final = isinstance(j, int) and u == TILES - 1
            if final and not last:
                sp.wait_ge(c_proj.sem, c_proj.at(it, CT))
                sp.sem_inc(stand, 1)
                load_weights(sp, g + 1, 0, CT, c_wbcx)
            if not (final and last):
                sp.wait_ge(c_scan.sem, c_scan.at(it, 4))
                sp.sem_inc(stand, 1)
                sp.wait_ge(c_da.sem, c_da.at(it, 32))
                sp.sem_inc(stand, 1)
                load_da(sp, 0 if final else u + 1, g + 1 if final else g)
            if not (isinstance(j, int) and j == 3 and last):
                sp.wait_ge(c_proj.sem, c_proj.at(it, CT + GATES))
                sp.sem_inc(stand, 1)
                sp.dma_start(xT[:, par], xt_d[par] if isinstance(j, int) and j == 3 else xt_d[u + 2]) \
                    .then_inc(c_xt[par].sem, 16)
            if final and not last:
                load_weights(sp, g + 1, CT, CT + GATES, c_wgate)

        def c_sp(sp):
            load_weights(sp, 0, 0, CT, c_wbcx)
            load_weights(sp, 0, CT, CT + GATES, c_wgate)
            for par in range(2):
                sp.dma_start(xT[:, par], xt_d[par]).then_inc(c_xt[par].sem, 16)
            load_da(sp, 0, 0)

            def group(g, last=False):
                with sp.Fori(0, 3) as j:
                    c_sp_turn(sp, g, j, 0)
                    c_sp_turn(sp, g, j, 1)
                c_sp_turn(sp, g, 3, 0, last)
                c_sp_turn(sp, g, 3, 1, last)

            with sp.Fori(0, G - 1) as g:
                group(g)
            group(G - 1, last=True)

        used[0] = 0
        wr = view(KT, E)
        br = view(E)
        eb = view(DM, parts=E)
        d_xh = view(4, DM)
        d_xT = view(KT, TOK)
        lg = view(4, E)
        d_mx = view(4)
        top = view(4, 8)
        rest = view(4, E)
        wd = view(4, E)
        d_sum = view(4)
        d_rs = view(4)
        d_ts = view(4)
        ws = view(4)
        wT = view(TOK, parts=E)
        d_stats = view(4, 6)
        d_mv = view(4, 2)
        d_vpe = view(4)
        d_rstd = view(4)

        d_w = signal("d_w", 48)
        d_stat = signal("d_stat", 9)
        d_rp = signal("d_rp", 1)
        d_xn = signal("d_xn", 4)
        d_t = signal("d_t", 4)
        d_tc = signal("d_tc", 4)
        d_lg = signal("d_lg", 1)
        d_l = signal("d_l", 3)
        d_e = signal("d_e", 1)
        d_k = signal("d_k", 14)
        d_wt = signal("d_wt", 1)
        d_wc = signal("d_wc", 1)
        d_mix = signal("d_mix", 4)
        d_o = signal("d_o", 8)
        d_st = signal("d_st", 16)

        def d_dve(dve, n, first=False):
            for q in range(4):
                dve.bn_stats(d_stats[:, q, :], acc[:, n * 4 + q, :]).then_inc(d_stat.sem, 1)
            for q in range(4):
                dve.wait_ge(d_stat.sem, d_stat.at(n, q + 1))
                dve.sem_inc(stand, 1)
                dve.bn_aggr(d_mv[:, q, :], d_stats[:, q, :]).then_inc(d_stat.sem, 1)
            dve.wait_ge(d_stat.sem, d_stat.at(n, 8))
            dve.tensor_scalar(d_vpe, d_mv[:, :, 1], EPS, None, ALU.add).then_inc(d_stat.sem, 1)
            dve.wait_ge(d_rp.sem, d_rp.at(n, 1))
            for q in range(4):
                dve.tensor_scalar(d_xh[:, q, :], acc[:, n * 4 + q, :], d_mv[:, q, 0:1], d_rstd[:, q:q + 1],
                                  ALU.subtract, ALU.mult).then_inc(d_xn.sem, 1)
            dve.wait_ge(d_lg.sem, d_lg.at(n, 1))
            dve.tensor_tensor(lg, bank[4][:, 0:4 * E].rearrange("p (q e) -> p q e", e=E),
                              br.unsqueeze(1).broadcast_to([P, 4, E]), ALU.add).then_inc(d_l.sem, 1)
            dve.wait_ge(d_l.sem, d_l.at(n, 1))
            dve.tensor_reduce(d_mx, lg, AX_X, ALU.max).then_inc(d_l.sem, 1)
            dve.wait_ge(d_l.sem, d_l.at(n, 2))
            dve.tensor_tensor(lg, lg, d_mx.unsqueeze(2).broadcast_to([P, 4, E]), ALU.subtract).then_inc(d_l.sem, 1)
            dve.wait_ge(d_e.sem, d_e.at(n, 1))
            dve.tensor_reduce(d_sum, lg, AX_X, ALU.add).then_inc(d_k.sem, 1)
            for q in range(4):
                dve.max(top[:, q, :], lg[:, q, :]).then_inc(d_k.sem, 1)
            dve.wait_ge(d_k.sem, d_k.at(n, 1))
            dve.reciprocal(d_rs, d_sum).then_inc(d_k.sem, 1)
            dve.wait_ge(d_k.sem, d_k.at(n, 5))
            dve.tensor_reduce(d_ts, top, AX_X, ALU.add).then_inc(d_k.sem, 1)
            for q in range(4):
                dve.sem_inc(stand, 1)
                dve.match_replace(rest[:, q, :], top[:, q, :], lg[:, q, :], 0.0).then_inc(d_k.sem, 1)
            dve.wait_ge(d_k.sem, d_k.at(n, 11))
            dve.tensor_tensor(wd, lg, rest, ALU.subtract).then_inc(d_k.sem, 1)
            dve.wait_ge(d_k.sem, d_k.at(n, 12))
            dve.tensor_tensor(wd, wd, d_rs.unsqueeze(2).broadcast_to([P, 4, E]), ALU.mult).then_inc(d_k.sem, 1)
            dve.tensor_tensor(ws, d_ts, d_rs, ALU.mult).then_inc(d_k.sem, 1)
            dve.wait_ge(d_k.sem, d_k.at(n, 14))
            for q in range(4):
                a = acc[:, n * 4 + q, :]
                dve.scalar_tensor_tensor(out=a, in0=d_xh[:, q, :], scalar=ws[:, q:q + 1], in1=a,
                                         op0=ALU.mult, op1=ALU.add).then_inc(d_o.sem, 1)
            for q in range(4):
                a = acc[:, n * 4 + q, :]
                dve.wait_ge(d_o.sem, d_o.at(n, q + 1))
                dve.wait_ge(d_mix.sem, d_mix.at(n, q + 1))
                dve.tensor_tensor(a, a, bank[6 + q % 2][:, :], ALU.add).then_inc(d_o.sem, 1)

        def d_pe(pe, n, first=False):
            pe.wait_ge(d_xn.sem, d_xn.at(n, 4))
            for k in range(KT):
                if not first:
                    pe.wait_ge(d_tc.sem, d_tc.at(n - 1, k + 1))
                for q in range(4):
                    mm = pe.transpose(bank[k][:, q * P:(q + 1) * P], d_xh[:, q, k * P:(k + 1) * P], ident[:, :])
                mm.then_inc(d_t.sem, 1)
            pe.wait_ge(d_tc.sem, d_tc.at(n, 4))
            for q in range(4):
                for k in range(KT):
                    mm = pe.matmul(bank[4][:, q * E:(q + 1) * E], d_xT[:, k, q * P:(q + 1) * P], wr[:, k, :],
                                   start=k == 0, stop=k == KT - 1)
            mm.then_inc(d_lg.sem, 1)
            pe.wait_ge(d_k.sem, d_k.at(n, 13))
            pe.sem_inc(stand, 1)
            for q in range(4):
                mm = pe.transpose(bank[5][0:E, q * P:(q + 1) * P], wd[:, q, :], ident[:, :])
            mm.then_inc(d_wt.sem, 1)
            pe.wait_ge(d_wc.sem, d_wc.at(n, 1))
            for q in range(4):
                if q >= 2:
                    pe.wait_ge(d_o.sem, d_o.at(n, q + 3))
                elif not first:
                    pe.wait_ge(d_o.sem, d_o.at(n - 1, q + 7))
                pe.sem_inc(stand, 1)
                pe.matmul(bank[6 + q % 2][:, :], wT[:, q * P:(q + 1) * P], eb, start=True, stop=True) \
                    .then_inc(d_mix.sem, 1)

        def d_act(act, n, first=False):
            for k in range(KT):
                act.wait_ge(d_t.sem, d_t.at(n, k + 1))
                act.activation(d_xT[:, k, :], bank[k][:, :], ACT.Copy).then_inc(d_tc.sem, 1)
            act.wait_ge(d_l.sem, d_l.at(n, 3))
            act.activation(lg, lg, ACT.Exp).then_inc(d_e.sem, 1)
            act.wait_ge(d_wt.sem, d_wt.at(n, 1))
            act.activation(wT, bank[5][0:E, :], ACT.Copy).then_inc(d_wc.sem, 1)

        def d_pool(pool, n):
            pool.wait_ge(d_stat.sem, d_stat.at(n, 9))
            pool.tensor_tensor(d_rstd, d_vpe, half_neg[:, :], ALU.pow).then_inc(d_rp.sem, 1)

        def d_sp(sp):
            sp.wait_ge(c_acc.sem, c_acc.at(G * TILES, 4))
            for dst, src in ((wr, w_router), (br, b_router.broadcast_to([P, E])), (eb, e_bias)):
                sp.dma_start(dst, src).then_inc(d_w.sem, 16)
            for n in range(TILES):
                t = (n + 7) % TILES
                sp.wait_ge(d_o.sem, d_o.at(n, 8))
                sp.dma_start(out_v[:, 4 * t:4 * t + 4, :], acc[:, 4 * n:4 * n + 4, :]).then_inc(d_st.sem, 16)
            sp.wait_ge(d_st.sem, d_st.at(TILES - 1, 16))

        block = ctx.enter_context(nc.Block())

        @block.sync
        def _(sp):
            for dst, src in ((ident[:, :], ident_in), (parity[:, :], parity_in), (eye[:, :], eye_in),
                             (cw[:, :, :], conv_w), (cb[:, :], conv_b), (dsk[:, :], d_skip), (nw[:, :], norm_w),
                             (maskb[0:SEQ, :], mask), (maskb[SEQ:P, :], mask)):
                sp.dma_start(dst, src).then_inc(consts_in, 16)
            load_pair(sp, 0, 0, first=True)
            load_pair(sp, 1, 1, second=True)
            load_w(sp, 0, 0, first=True)
            load_w(sp, 0, 1, first=True)
            load_pair(sp, 2, 0)
            load_pair(sp, 3, 1)
            with sp.Fori(2, PAIRS // 2) as r:
                for par in range(2):
                    load_pair(sp, 2 * r + par, par)
                    store_w(sp, r - 2, par)
                    load_w(sp, r - 1, par)
            for par in range(2):
                store_w(sp, PAIRS // 2 - 2, par)
                load_w(sp, PAIRS // 2 - 1, par)
            for par in range(2):
                store_w(sp, PAIRS // 2 - 1, par)
            for par in range(2):
                sp.wait_ge(a_wst[par].sem, a_wst[par].at(PAIRS // 2 - 1, 16))
            sp.wait_ge(a_out.sem, a_out.at(PAIRS - 1, 6))
            sp.wait_ge(b_go, 1)
            for dst, src in ((w_dt_sb, w_dt), (dtb, dt_bias), (alog, a_log)):
                sp.dma_start(dst, src).then_inc(b_w.sem, 16)
            with sp.Fori(0, TILES) as u:
                b_sp_store(sp, u)
            sp.wait_ge(c_go, 5)
            c_sp(sp)
            d_sp(sp)

        @block.gpsimd
        def _(pool):
            pool.memset(half_neg[:, :], -0.5).then_inc(half_set, 1)
            pool.memset(v32, 0.0).then_inc(v_zero, 1)
            pool.wait_ge(v_zero, 1)
            pool.memset(v32[:, :, :, :, HD:HD + 1].rearrange("p a b g o -> p (a b g) o"), 1.0).then_inc(a_v.sem, 1)
            pool.wait_ge(half_set, 1)
            pool_front(pool, 0, 0, 0, first=True)
            pool_values(pool, 0, 0, first=True)
            pool_front(pool, 1, 1, 0)
            pool_values(pool, 1, 1, first=True)
            for par in range(2):
                pool_front(pool, 2 + par, par, 1)
                pool_w_max(pool, par, first=par == 0)
                pool_values(pool, 2 + par, par)
            with pool.Fori(1, PAIRS // 2 - 1) as r:
                for par in range(2):
                    pool_front(pool, 2 * r + 2 + par, par, r + 1)
                    pool_w_max(pool, 2 * r + par)
                    pool_values(pool, 2 * r + 2 + par, par)
            pool_w_max(pool, PAIRS - 2)
            pool_w_max(pool, PAIRS - 1)
            def b_turns():
                b_pool(pool, 0, first=True)
                with pool.Fori(1, TILES) as u:
                    b_pool(pool, u)
            pool.wait_ge(b_go, 1)
            b_turns()
            pool.wait_ge(b_tk.sem, b_tk.at(TILES - 1, 1))
            pool.wait_ge(b_sp.sem, b_sp.at(TILES - 1, 4))
            pool.wait_ge(b_da.sem, b_da.at(TILES - 1, 16))
            pool.wait_ge(b_st.sem, b_st.at(TILES - 1, 16))
            pool.memset(mm_sb, 0.0).then_inc(c_m.sem, 4)
            pool.memset(dtx, 0.0).then_inc(c_dtx.sem, 4)
            pool.memset(y, 0.0).then_inc(c_xd.sem, 4)
            pool.memset(gs, 0.0).then_inc(c_gate.sem, 4)
            pool.memset(w_o, 0.0).then_inc(c_init.sem, 1)
            pool.memset(ones, 1.0).then_inc(c_init.sem, 1)
            pool.wait_ge(a_wsc.sem, a_wsc.at(PAIRS - 1, 4))
            taps = cw[:, :, :].rearrange("p (g n) t -> p g n t", n=CT)
            pool.tensor_tensor(taps, taps, w_unscale[:, :].rearrange("p (g n) -> p g n", n=CT + GATES)
                               [:, :, 0:CT].unsqueeze(3).broadcast_to([P, G, CT, 4]), ALU.mult).then_inc(c_init.sem, 1)
            pool.wait_ge(c_init.sem, 3)
            pool.sem_inc(c_go, 5)
            with pool.Fori(0, G) as g:
                c_pool_group(pool, g)
            c_pool_turn(pool, G * TILES)
            pool.wait_ge(d_w.sem, 48)
            d_pool(pool, 0)
            with pool.Fori(1, TILES) as n:
                d_pool(pool, n)

        @block.scalar
        def _(act):
            act.wait_ge(consts_in, N_CONSTS)
            act_front_x(act, 0, first=True)
            act_front_k(act, 0)
            act_exp(act, 0, 0)

            def turn(i, r, par, first=False, late=False, last=False):
                if not last:
                    act_front_x(act, i + 1)
                act_copy_probs(act, i, 0, first)
                act_outT(act, i, 0)
                if not last:
                    act_front_k(act, i + 1)
                act_exp(act, i, 1)
                act_copy_probs(act, i, 1)
                act_outT(act, i, 1)
                act_w_high(act, i, r, par, first=isinstance(r, int) and r == 0)
                if not last:
                    act_exp(act, i + 1, 0)

            a_turns(act, turn)
            act.wait_ge(b_w.sem, 48)
            act.activation(a_neg[:, 0:1], alog, ACT.Exp).then_inc(b_a.sem, 1)
            act.wait_ge(b_a.sem, 1)
            act.activation(a_neg[:, 1:2], a_neg[:, 0:1], ACT.Copy, scale=-1.0).then_inc(b_a.sem, 1)
            act.wait_ge(b_a.sem, 2)
            b_act(act, 0, first=True)
            with act.Fori(1, TILES) as u:
                b_act(act, u)
            act.wait_ge(c_go, 5)
            with act.Fori(0, G) as g:
                with act.Fori(0, 4) as j:
                    c_act_turn(act, g, j, 0)
                    c_act_turn(act, g, j, 1)
            act.wait_ge(c_yadd.sem, c_yadd.at(G * TILES, 4))
            act.activation(sq, y, ACT.Square).then_inc(c_sq.sem, 1)
            act.wait_ge(d_w.sem, 48)
            d_act(act, 0, first=True)
            with act.Fori(1, TILES) as n:
                d_act(act, n)

        @block.vector
        def _(dve):
            norm_pair(dve, 0, first=True)
            apply_norm(dve, 0, first=True)
            dve.wait_ge(consts_in, N_CONSTS)
            norm_pair(dve, 1)
            dve_mask(dve, 0, 0, first=True)
            dve_softmax(dve, 0, 0)
            apply_norm(dve, 1)

            def turn(i, r, par, first=False, late=False, last=False):
                dve_mask(dve, i, 1, first)
                if not first:
                    dve_out(dve, i - 1, 1)
                if not late:
                    norm_pair(dve, i + 2)
                dve_softmax(dve, i, 1)
                if not late:
                    apply_norm(dve, i + 2)
                dve_w_max(dve, i, r, par, first)
                dve_w_scale(dve, i, r, par, first)
                if not last:
                    dve_mask(dve, i + 1, 0)
                dve_out(dve, i, 0, first)
                if not last:
                    dve_softmax(dve, i + 1, 0)
                dve_w_low(dve, i, par)

            a_turns(dve, turn)
            dve_out(dve, PAIRS - 1, 1)
            dve.wait_ge(a_out.sem, a_out.at(PAIRS - 1, 6))
            dve.sem_inc(b_go, 1)
            dve.wait_ge(b_w.sem, 48)
            b_dve(dve, 0, first=True)
            with dve.Fori(1, TILES) as u:
                b_dve(dve, u)
            dve.wait_ge(c_go, 5)
            with dve.Fori(0, G) as g:
                with dve.Fori(0, 4) as j:
                    c_dve_turn(dve, g, j, 0)
                    c_dve_turn(dve, g, j, 1)
            y_add(dve, G * TILES, 0)
            y_add(dve, G * TILES, 1)
            y_gate(dve, G * TILES)
            mean_square(dve, G * TILES)
            for q in range(4):
                add_out(dve, G * TILES, 0, q)
            dve.wait_ge(d_w.sem, 48)
            d_dve(dve, 0, first=True)
            with dve.Fori(1, TILES) as n:
                d_dve(dve, n)

        @block.tensor
        def _(pe):
            pe.wait_ge(consts_in, N_CONSTS)
            pe_front_x(pe, 0, first=True)
            pe_front_k(pe, 0, first=True)
            pe_scores(pe, 0, 0, first=True)

            def turn(i, r, par, first=False, late=False, last=False):
                pe_scores(pe, i, 1)
                if not first:
                    pe_back(pe, i - 1, 1)
                if not last:
                    pe_front_x(pe, i + 1)
                pe_values(pe, i, 0, par, first)
                if not last:
                    pe_front_k(pe, i + 1)
                    pe_scores(pe, i + 1, 0)
                pe_back(pe, i, 0)
                pe_values(pe, i, 1, par, last=last)

            a_turns(pe, turn)
            pe_back(pe, PAIRS - 1, 1)
            b_pe(pe, 0, first=True)
            with pe.Fori(1, TILES) as u:
                b_pe(pe, u)
            pe.wait_ge(c_go, 5)
            with pe.Fori(0, G) as g:
                with pe.Fori(0, 4) as j:
                    c_pe_turn(pe, g, j, 0)
                    c_pe_turn(pe, g, j, 1)
            heads_out(pe, G * TILES, 0)
            heads_out(pe, G * TILES, 1)
            out_product(pe, G * TILES, 0)
            out_product(pe, G * TILES, 1)
            norm_sums(pe, G * TILES)
            out_product(pe, G * TILES, 2)
            out_product(pe, G * TILES, 3)
            pe.wait_ge(d_w.sem, 48)
            d_pe(pe, 0, first=True)
            with pe.Fori(1, TILES) as n:
                d_pe(pe, n)


def kernel(**inputs):
    import numpy as np
    import concourse.bacc as bacc
    from concourse.bass_utils import run_bass_kernel_spmd

    a = {k: np.asarray(v) for k, v in inputs.items()}
    w = a["L0_attn_in_proj_w"]
    inner, gn = H * HP, G * N_ST
    gate_r = w[:inner].reshape(G, 512, DM)
    x_r = w[inner:2 * inner].reshape(G, 512, DM)
    b_r = w[2 * inner:2 * inner + gn].reshape(G, P, DM)
    c_r = w[2 * inner + gn:2 * inner + 2 * gn].reshape(G, P, DM)

    def k_major(rows):
        g, n, _ = rows.shape
        return rows.transpose(0, 2, 1).reshape(g, KT, P, n).transpose(0, 2, 1, 3)

    def channel_slices(rows):
        return rows.reshape(W_TILES, P, KT, P).transpose(3, 0, 2, 1).reshape(P, W_TILES, KT * P)

    def channel_tiles(rows):
        xs = rows[:inner].reshape(G, 4, P, -1)
        bs = rows[inner:inner + gn].reshape(G, 1, P, -1)
        cs = rows[inner + gn:].reshape(G, 1, P, -1)
        return np.concatenate([bs, cs, xs], 1).transpose(2, 0, 1, 3).reshape(P, G * CT, -1)

    arrays = {
        "x": a["x"], "ctx": a["ctx_1024"], "mask": a["mask_SxS2_ff0"],
        "w_in": channel_slices(np.concatenate([b_r, c_r, x_r, gate_r], 1)),
        "w_dt": k_major(w[-H:][None])[0],
        "w_out": a["L0_attn_out_proj_w"].T.reshape(G, 4, P, DM).transpose(0, 2, 1, 3),
        "conv_w": channel_tiles(a["L0_attn_conv_weight"]),
        "conv_b": channel_tiles(a["L0_attn_conv_bias"][:, None])[:, :, 0],
        "dt_bias": a["L0_attn_dt_bias"][:, None], "a_log": a["L0_attn_A_log"][:, None],
        "d_skip": np.repeat(a["L0_attn_D"], HP).reshape(G * 4, P).T,
        "norm_w": a["L0_attn_norm_weight"].reshape(G * 4, P).T,
        "w_router": a["L0_ffn_router_weight"].T.reshape(KT, P, E).transpose(1, 0, 2),
        "b_router": a["L0_ffn_router_bias"][None],
        "e_bias": a["L0_ffn_expert_bias"],
        "ident": np.eye(P, dtype=np.float32),
        "parity": np.stack([1 - np.arange(P) // HD % 2, np.arange(P) // HD % 2], 1).astype(np.float32),
        "eye": np.tile(np.eye(SEQ, dtype=np.float32), (2, HG)),
    }
    arrays = {f"in_{k}": np.ascontiguousarray(v) for k, v in arrays.items()}
    nc = bacc.Bacc("TRN2", target_bir_lowering=False, num_devices=1)
    args = [nc.dram_tensor(k, v.shape, F32, kind="ExternalInput").ap() for k, v in arrays.items()]
    out = nc.dram_tensor("out", [BATCH, SEQ, DM], F32, kind="ExternalOutput").ap()
    xt_d = nc.dram_tensor("xt", [TILES, P, 2, KT, TOK], F16).ap()
    w_d = nc.dram_tensor("w_split", [P, W_TILES, 2, KT * P], F16).ap()
    da_d = nc.dram_tensor("da", [BATCH, H, SEQ], F32).ap()
    build(nc, *args, out, xt_d, da_d, w_d)
    r = run_bass_kernel_spmd(nc, [arrays], core_ids=[0])
    return r.results[0]["out"]
```

```python
import concourse.bass as bass
from concourse import mybir
from contextlib import ExitStack

F32 = mybir.dt.float32
F16 = mybir.dt.float16
U32 = mybir.dt.uint32
ALU = mybir.AluOpType
ACT = mybir.ActivationFunctionType
AX_X = mybir.AxisListType.X

P = 128
BATCH, SEQ, DM = 64, 64, 512
KT = DM // P
PAIRS = BATCH * SEQ // P
TILES = 8
TOK = 512
T_CTX, C_CTX = 128, 128
HD = 16
H, HP, N_ST, G = 64, 64, 128, 8
HG = H // G
CT = 6
GATES = 4
E = 64
W_TILES = G * (CT + GATES)
X_BANK = (4, 6, 5, 7)
W_TURN = (3, 2)
X_SCALE = 1024.0
W_TOP = 2.0 ** 14
EXPONENT = 0x7F800000
FLOOR = 2.0 ** -60
EPS = 1e-5
WORK = 33500




class Signal:

    def __init__(self, sem, per, credit=0):
        self.sem, self.per, self.credit = sem, per, credit

    def at(self, turn, n):
        return turn * self.per + (n + self.credit)


def build(nc, x, ctx_in, mask, w_in, w_dt, w_out, conv_w, conv_b, dt_bias, a_log, d_skip, norm_w,
          w_router, b_router, e_bias, ident_in, parity_in, eye_in, out, xt_d, da_d, w_d, wo_d):
    x_v = x.rearrange("(n b) s d -> n (b s) d", b=2)
    out_v = out.rearrange("(n b) s d -> (b s) n d", b=2)
    ctx_v = ctx_in.rearrange("(n b) t c -> n t b c", b=2)

    with ExitStack() as ctx:
        def sb(name, shape):
            return ctx.enter_context(nc.sbuf_tensor(name, shape, F32))

        def sem(name):
            return ctx.enter_context(nc.semaphore(name))

        def signal(name, per, credit=0):
            return Signal(sem(name), per, credit)

        bank = [ctx.enter_context(nc.psum_tensor(f"bank{i}", [P, 512], F32)) for i in range(8)]

        acc = sb("acc", [P, PAIRS, DM])
        ident = sb("ident", [P, P])
        parity = sb("parity", [P, 2])
        eye = sb("eye", [P, TOK])
        half_neg = sb("half_neg", [P, 4])
        dt_tok = sb("dt_tok", [P, PAIRS, H])
        cw = sb("cw", [P, G * CT, 4])
        cb = sb("cb", [P, G * CT])
        dsk = sb("dsk", [P, G * 4])
        nw = sb("nw", [P, G * 4])
        small = sb("small", [P, 64])
        wo_unscale = sb("wo_unscale", [P, G])
        w_unscale = sb("w_unscale", [P, W_TILES])
        work = sb("work", [P, WORK])
        used = [0]

        def view(*shape, parts=P):
            n = 1
            for s in shape:
                n *= s
            v = work[0:parts, used[0]:used[0] + n]
            used[0] += n
            assert used[0] <= WORK
            if len(shape) == 1:
                return v
            names = "abcd"[:len(shape)]
            return v.rearrange(f"p ({' '.join(names)}) -> p {' '.join(names)}",
                               **{k: s for k, s in zip(names, shape)})

        def halves(v):
            return v.bitcast(F16)

        def acc_pair(i):
            return acc[:, (i + 4) % PAIRS, :]

        consts_in = sem("consts_in")
        N_CONSTS = 16 * 9
        half_set = sem("half_set")
        v_zero = sem("v_zero")
        b_go = sem("b_go")
        c_go = sem("c_go")
        stand = sem("stand")

        def power_of_two(dve, m, steps, turn, n):
            dve.tensor_scalar(m[:, 2:3].bitcast(U32), m[:, 1:2].bitcast(U32), EXPONENT, None,
                              ALU.bitwise_and).then_inc(steps.sem, 1)
            dve.wait_ge(steps.sem, steps.at(turn, n + 1))
            dve.sem_inc(stand, 1)
            dve.tensor_scalar(m[:, 3:4], m[:, 2:3], 1 / W_TOP, FLOOR, ALU.mult, ALU.max).then_inc(steps.sem, 1)
            dve.wait_ge(steps.sem, steps.at(turn, n + 2))
            dve.sem_inc(stand, 1)
            dve.reciprocal(m[:, 4:5], m[:, 3:4]).then_inc(steps.sem, 1)

        used[0] = 0
        maskb = view(T_CTX)
        ctx_sb = view(2, 2, C_CTX)
        k_rep = view(2, 8 * 4 * HD)
        v32 = view(2, 2, 8, 32)
        k_eo = view(2, 2, KT * T_CTX)
        xh = view(DM)
        xhT = view(KT, P)
        prob = view(2, 4, 4 * T_CTX)
        pt = view(2, 4 * P)
        att = view(256)
        outT = view(512)
        w_f = view(sum(W_TURN), KT * P)
        w_s = halves(view(sum(W_TURN), KT * P)).rearrange("p t (s c) -> p t s c", s=2)
        w_max = view(8)
        stats = small[:, 0:6]
        mv = small[:, 8:10]
        rstd = small[:, 12:13]
        low = small[:, 16:48].rearrange("p (f h) -> p f h", f=2)
        rden = small[:, 48:64]
        vpe = small[:, 11:12]

        a_x = signal("a_x", 16)
        a_ctx = [signal(f"a_ctx{n}", 16) for n in range(2)]
        a_ln = signal("a_ln", 3)
        a_rstd = signal("a_rstd", 1)
        a_xh = signal("a_xh", 1)
        a_rep = signal("a_rep", 2)
        a_front = signal("a_front", 3)
        a_kT = signal("a_kT", 5)
        a_v = signal("a_v", 1, 1)
        a_score = signal("a_score", 2)
        a_masked = signal("a_masked", 8)
        a_max = signal("a_max", 2)
        a_sub = signal("a_sub", 2)
        a_exp = signal("a_exp", 10)
        a_pt = signal("a_pt", 8)
        a_pt_sb = signal("a_pt_sb", 8)
        a_pv = signal("a_pv", 8)
        a_outT = signal("a_outT", 2)
        a_back = signal("a_back", 2)
        a_out = signal("a_out", 6)

        a_win = [signal(f"a_win{n}", 16) for n in range(2)]
        a_wmax = signal("a_wmax", 1)
        a_wall = signal("a_wall", 1)
        a_wsc = signal("a_wsc", 4)
        a_whi = signal("a_whi", 1)
        a_wlo = signal("a_wlo", 1)
        a_wst = [signal(f"a_wst{n}", 16) for n in range(2)]

        def w_cut(par):
            return slice(0, W_TURN[0]) if par == 0 else slice(W_TURN[0], sum(W_TURN))

        def w_tiles(r, par):
            return bass.ds(r * sum(W_TURN) + par * W_TURN[0], W_TURN[par])

        def load_w(sp, r, par, first=False):
            if not first:
                sp.wait_ge(a_whi.sem, a_whi.at(2 * r + par - 2, 1))
                sp.wait_ge(a_wlo.sem, a_wlo.at(2 * r + par - 2, 1))
            sp.sem_inc(stand, 1)
            sp.dma_start(w_f[:, w_cut(par)], w_in[:, w_tiles(r, par)]).then_inc(a_win[par].sem, 16)

        def store_w(sp, r, par):
            sp.wait_ge(a_wlo.sem, a_wlo.at(2 * r + par, 1))
            sp.sem_inc(stand, 1)
            sp.dma_start(w_d[:, w_tiles(r, par)], w_s[:, w_cut(par)]).then_inc(a_wst[par].sem, 16)

        def dve_w_max(dve, i, r, par, first=False):
            dve.wait_ge(a_win[par].sem, a_win[par].at(r, 16))
            if not first:
                dve.wait_ge(a_wall.sem, a_wall.at(i - 1, 1))
            dve.sem_inc(stand, 1)
            dve.tensor_reduce(w_max[:, 0:1], w_f[:, w_cut(par)].rearrange("p t c -> p (t c)"), AX_X, ALU.max,
                              apply_absolute_value=True).then_inc(a_wmax.sem, 1)

        def pool_w_max(pool, i, first=False):
            pool.wait_ge(a_wmax.sem, a_wmax.at(i, 1))
            if not first:
                pool.wait_ge(a_wsc.sem, a_wsc.at(i - 1, 1))
            pool.sem_inc(stand, 1)
            pool.partition_all_reduce(w_max[:, 1:2], w_max[:, 0:1], P, bass.bass_isa.ReduceOp.max) \
                .then_inc(a_wall.sem, 1)

        def dve_w_scale(dve, i, r, par, first=False):
            dve.wait_ge(a_wall.sem, a_wall.at(i, 1))
            if not first:
                dve.wait_ge(a_wlo.sem, a_wlo.at(i - 1, 1))
                dve.wait_ge(a_wsc.sem, a_wsc.at(i - 1, 4))
            dve.sem_inc(stand, 1)
            dve.tensor_scalar(w_max[:, 2:3].bitcast(U32), w_max[:, 1:2].bitcast(U32), EXPONENT, None,
                              ALU.bitwise_and).then_inc(a_wsc.sem, 1)
            dve.wait_ge(a_wsc.sem, a_wsc.at(i, 1))
            dve.sem_inc(stand, 1)
            dve.tensor_scalar(w_max[:, 3:4], w_max[:, 2:3], 1 / W_TOP, FLOOR, ALU.mult, ALU.max) \
                .then_inc(a_wsc.sem, 1)
            dve.wait_ge(a_wsc.sem, a_wsc.at(i, 2))
            dve.sem_inc(stand, 1)
            dve.tensor_scalar(w_unscale[:, w_tiles(r, par)], w_max[:, 3:4].broadcast_to([P, W_TURN[par]]),
                              1 / X_SCALE, None, ALU.mult).then_inc(a_wsc.sem, 1)
            dve.reciprocal(w_max[:, 4:5], w_max[:, 3:4]).then_inc(a_wsc.sem, 1)

        def act_w_high(act, i, r, par, first=False):
            act.wait_ge(a_wsc.sem, a_wsc.at(i, 4))
            if not first:
                act.wait_ge(a_wst[par].sem, a_wst[par].at(r - 1, 16))
            act.sem_inc(stand, 1)
            act.activation(w_s[:, w_cut(par), 0], w_f[:, w_cut(par)], ACT.Copy, scale=w_max[:, 4:5]) \
                .then_inc(a_whi.sem, 1)

        def dve_w_low(dve, i, par):
            dve.wait_ge(a_whi.sem, a_whi.at(i, 1))
            dve.sem_inc(stand, 1)
            dve.scalar_tensor_tensor(out=w_s[:, w_cut(par), 1], in0=w_f[:, w_cut(par)], scalar=w_max[:, 4:5],
                                     in1=w_s[:, w_cut(par), 0], op0=ALU.mult, op1=ALU.subtract) \
                .then_inc(a_wlo.sem, 1)

        def load_pair(sp, i, par, first=False, second=False):
            if not first:
                sp.wait_ge(a_x.sem, a_x.at(i - 1, 16))
            sp.dma_start(acc_pair(i), x_v[i]).then_inc(a_x.sem, 16)
            if not (first or second):
                sp.wait_ge(a_rep.sem, a_rep.at(i - 2, 2))
                sp.sem_inc(stand, 1)
                sp.wait_ge(a_v.sem, a_v.at(i - 2, 1))
                sp.sem_inc(stand, 1)
            sp.dma_start(ctx_sb[:, par], ctx_v[i]).then_inc(a_ctx[par].sem, 16)

        def norm_pair(dve, i, first=False):
            dve.wait_ge(a_x.sem, a_x.at(i, 16))
            if not first:
                dve.wait_ge(a_xh.sem, a_xh.at(i - 1, 1))
            dve.bn_stats(stats, acc_pair(i)).then_inc(a_ln.sem, 1)
            dve.wait_ge(a_ln.sem, a_ln.at(i, 1))
            dve.sem_inc(stand, 1)
            dve.bn_aggr(mv, stats).then_inc(a_ln.sem, 1)
            dve.wait_ge(a_ln.sem, a_ln.at(i, 2))
            dve.tensor_scalar(vpe, mv[:, 1:2], EPS, None, ALU.add).then_inc(a_ln.sem, 1)

        def apply_norm(dve, i, first=False):
            dve.wait_ge(a_rstd.sem, a_rstd.at(i, 1))
            if not first:
                dve.wait_ge(a_front.sem, a_front.at(i - 1, 1))
            dve.tensor_scalar(xh, acc_pair(i), mv[:, 0:1], rstd, ALU.subtract, ALU.mult).then_inc(a_xh.sem, 1)

        def pool_front(pool, i, par, turns, first=False):
            pool.wait_ge(a_ln.sem, a_ln.at(i, 3))
            pool.tensor_tensor(rstd, vpe, half_neg[:, 0:1], ALU.pow).then_inc(a_rstd.sem, 1)
            pool.wait_ge(a_ctx[par].sem, a_ctx[par].at(turns, 16))
            if not first:
                pool.wait_ge(a_front.sem, a_front.at(i - 1, 3))
            pool.sem_inc(stand, 1)
            for b in range(2):
                kv = ctx_sb[:, par, b, :].rearrange("p (g o d) -> p g o d", o=1, d=HD).broadcast_to([P, 8, 4, HD])
                pool.tensor_copy(k_rep[:, b, :].rearrange("p (g o d) -> p g o d", o=4, d=HD), kv) \
                    .then_inc(a_rep.sem, 1)

        def pool_values(pool, i, par, first=False):
            if not first:
                pool.wait_ge(a_pv.sem, a_pv.at(i - 2, 8))
            pool.sem_inc(stand, 1)
            pool.tensor_copy(v32[:, par, :, :, 0:HD], ctx_sb[:, par].rearrange("p b (g d) -> p b g d", d=HD)) \
                .then_inc(a_v.sem, 1)

        def pe_front_x(pe, i, first=False):
            pe.wait_ge(a_xh.sem, a_xh.at(i, 1))
            if not first:
                pe.wait_ge(a_kT.sem, a_kT.at(i - 1, 1))
            for j in range(KT):
                mm = pe.transpose(bank[6][:, j * P:(j + 1) * P], xh[:, j * P:(j + 1) * P], ident[:, :])
            mm.then_inc(a_front.sem, 1)

        def pe_front_k(pe, i, first=False):
            pe.wait_ge(a_rep.sem, a_rep.at(i, 2))
            for b in range(2):
                if not first:
                    pe.wait_ge(a_pt_sb.sem, a_pt_sb.at(i - 1, 3 + b))
                for j in range(KT):
                    mm = pe.transpose(bank[4 + b][:, j * T_CTX:(j + 1) * T_CTX],
                                      k_rep[:, b, j * P:(j + 1) * P], ident[:, :])
                mm.then_inc(a_front.sem, 1)

        def act_front_x(act, i, first=False):
            act.wait_ge(a_front.sem, a_front.at(i, 1))
            if not first:
                act.wait_ge(a_score.sem, a_score.at(i - 1, 2))
            act.activation(xhT, bank[6][:, :], ACT.Copy).then_inc(a_kT.sem, 1)

        def act_front_k(act, i):
            for b in range(2):
                act.wait_ge(a_front.sem, a_front.at(i, 2 + b))
                for e in range(2):
                    act.activation(k_eo[:, b, e, :], bank[4 + b][:, :], ACT.Copy, scale=parity[:, e:e + 1]) \
                        .then_inc(a_kT.sem, 1)

        def pe_scores(pe, i, half, first=False):
            if half == 0:
                pe.wait_ge(a_kT.sem, a_kT.at(i, 5))
                if not first:
                    pe.wait_ge(a_masked.sem, a_masked.at(i, 0))
            else:
                pe.wait_ge(a_masked.sem, a_masked.at(i, 4))
            for jj in range(2):
                j = 2 * half + jj
                for r in range(4):
                    for b in range(2):
                        mm = pe.matmul(bank[r][64 * b:64 * b + 64, 256 * jj:256 * jj + 256],
                                       xhT[32 * r:32 * r + 32, j, 64 * b:64 * b + 64],
                                       k_eo[32 * r:32 * r + 32, b, :, j * T_CTX:(j + 1) * T_CTX],
                                       start=True, stop=True)
            mm.then_inc(a_score.sem, 1)

        def dve_mask(dve, i, half, first=False):
            dve.wait_ge(a_score.sem, a_score.at(i, half + 1))
            if not first:
                dve.wait_ge(a_pt.sem, a_pt.at(i - 1, 4 * half + 4))
            for r in range(4):
                dve.scalar_tensor_tensor(
                    out=prob[:, half, r, :].rearrange("p (h t) -> p h t", t=T_CTX),
                    in0=bank[r][:, :].rearrange("p (h t) -> p h t", t=T_CTX), scalar=-HD ** -0.5,
                    in1=maskb.unsqueeze(1).broadcast_to([P, 4, T_CTX]),
                    op0=ALU.mult, op1=ALU.subtract).then_inc(a_masked.sem, 1)

        def dve_softmax(dve, i, half):
            heads = prob[:, half, :, :].rearrange("p r (h t) -> p (r h) t", t=T_CTX)
            dve.wait_ge(a_masked.sem, a_masked.at(i, 4 * half + 4))
            dve.tensor_reduce(low[:, half, :], heads, AX_X, ALU.min).then_inc(a_max.sem, 1)
            dve.wait_ge(a_max.sem, a_max.at(i, half + 1))
            dve.tensor_tensor(heads[:, 0:12, :], heads[:, 0:12, :],
                              low[:, half, 0:12].unsqueeze(2).broadcast_to([P, 12, T_CTX]), ALU.subtract) \
                .then_inc(a_sub.sem, 1)

        def act_exp(act, i, half):
            act.wait_ge(a_sub.sem, a_sub.at(i, half + 1))
            act.activation(prob[:, half, 0:3, :], prob[:, half, 0:3, :], ACT.Exp, scale=-1.0).then_inc(a_exp.sem, 1)
            for h in range(4):
                p = prob[:, half, 3, h * T_CTX:(h + 1) * T_CTX]
                act.activation(p, p, ACT.Exp, scale=-1.0, bias=low[:, half, 12 + h:13 + h]).then_inc(a_exp.sem, 1)

        def pe_values(pe, i, half, par, first=False, last=False):
            def turn_probs(c):
                if c == 0:
                    pe.wait_ge(a_exp.sem, a_exp.at(i, 5 * half + 1))
                elif c == 1:
                    pe.wait_ge(a_exp.sem, a_exp.at(i, 5 * half + 5))
                if c >= 2 or (half == 1 and last):
                    pe.wait_ge(a_pt_sb.sem, a_pt_sb.at(i, 4 * half + c - 1))
                elif half == 1:
                    pe.wait_ge(a_kT.sem, a_kT.at(i + 1, 3 + 2 * c))
                elif not first:
                    pe.wait_ge(a_pt_sb.sem, a_pt_sb.at(i - 1, 7 + c))
                for r in range(4):
                    at = (2 * (c // 2) + r % 2) * T_CTX
                    mm = pe.transpose(bank[4 + c % 2][:, r * P:(r + 1) * P],
                                      prob[:, half, 2 * (c % 2) + r // 2, at:at + T_CTX], ident[:, :])
                mm.then_inc(a_pt.sem, 1)

            def weigh(c):
                pe.wait_ge(a_pt_sb.sem, a_pt_sb.at(i, 4 * half + c + 1))
                if c == 0:
                    pe.wait_ge(a_v.sem, a_v.at(i, 1))
                    if half == 1:
                        pe.wait_ge(a_out.sem, a_out.at(i, 2))
                    elif not first:
                        pe.wait_ge(a_out.sem, a_out.at(i - 1, 5))
                    pe.sem_inc(stand, 1)
                for b in range(2):
                    mm = pe.matmul(bank[7][32 * c:32 * c + 32, :].rearrange("p (r b s) -> p r b s", r=4, b=2)[:, :, b, :],
                                   v32[:, par, b, 4 * half + c, :],
                                   pt[:, c % 2, :].rearrange("p (r b s) -> p r b s", r=4, b=2)[:, :, b, :],
                                   start=True, stop=True)
                mm.then_inc(a_pv.sem, 1)

            turn_probs(0)
            for c in range(1, 4):
                turn_probs(c)
                weigh(c - 1)
            weigh(3)

        def act_outT(act, i, half):
            act.wait_ge(a_pv.sem, a_pv.at(i, 4 * half + 4))
            act.activation(outT, bank[7][:, :], ACT.Copy).then_inc(a_outT.sem, 1)

        def pe_back(pe, i, half):
            pe.wait_ge(a_outT.sem, a_outT.at(i, half + 1))
            for r in range(4):
                mm = pe.transpose(bank[7][:, r * P:(r + 1) * P], outT[:, r * P:(r + 1) * P], ident[:, :])
            mm.then_inc(a_back.sem, 1)

        def act_copy_probs(act, i, half, first=False):
            for r in range(4):
                act.wait_ge(a_pt.sem, a_pt.at(i, 4 * half + r + 1))
                n = 4 * half + r - 1
                if n >= 1:
                    act.wait_ge(a_pv.sem, a_pv.at(i, n))
                elif not first:
                    act.wait_ge(a_pv.sem, a_pv.at(i - 1, n + 8))
                act.activation(pt[:, r % 2, :], bank[4 + r % 2][:, :], ACT.Copy).then_inc(a_pt_sb.sem, 1)

        def dve_out(dve, i, half, first=False):
            o = bank[7][:, :].rearrange("p (r c d) -> p r c d", r=4, d=32)
            rd = rden.rearrange("p (r c) -> p r c", r=4)
            dve.wait_ge(a_back.sem, a_back.at(i, half + 1))
            if not (first and half == 0):
                dve.wait_ge(a_out.sem, a_out.at(i, 3 * half))
            dve.reciprocal(rd, o[:, :, :, HD]).then_inc(a_out.sem, 1)
            dve.wait_ge(a_out.sem, a_out.at(i, 3 * half + 1))
            dve.tensor_tensor(att.rearrange("p (c r d) -> p r c d", r=4, d=HD), o[:, :, :, 0:HD],
                              rd.unsqueeze(3).broadcast_to([P, 4, 4, HD]), ALU.mult).then_inc(a_out.sem, 1)
            dve.wait_ge(a_out.sem, a_out.at(i, 3 * half + 2))
            x_half = acc_pair(i)[:, 256 * half:256 * half + 256]
            if half == 0:
                dve.wait_ge(a_xh.sem, a_xh.at(i, 1))
            dve.tensor_tensor(x_half, x_half, att, ALU.add).then_inc(a_out.sem, 1)

        def a_turns(engine, turn):
            turn(0, 0, 0, first=True)
            turn(1, 0, 1)
            with engine.Fori(1, PAIRS // 2 - 1) as r:
                turn(2 * r, r, 0)
                turn(2 * r + 1, r, 1)
            turn(PAIRS - 2, PAIRS // 2 - 1, 0, late=True)
            turn(PAIRS - 1, PAIRS // 2 - 1, 1, late=True, last=True)

        used[0] = 0
        b_xh = view(4, DM)
        b_xT = view(KT, TOK)
        b_split = halves(view(2, 2, KT, TOK // 2))
        w_dt_sb = view(KT, H)
        dtb = view(1, parts=H)
        alog = view(1, parts=H)
        a_neg = view(2, parts=H)
        absv = view(TOK, parts=H)
        expv = view(TOK, parts=H)
        lnv = view(TOK, parts=H)
        dtv = view(TOK, parts=H)
        dav = view(8, SEQ, parts=H)
        b_stats = view(4, 6)
        b_mv = view(4, 2)
        b_vpe = view(4)
        b_rstd = view(4)
        b_max = view(8)
        wo_f = view(2, 4 * DM)
        wo_s = halves(view(2, 2 * DM))

        b_woin = [signal(f"b_woin{n}", 16) for n in range(2)]
        b_won = signal("b_won", 1)
        b_womax = signal("b_womax", 1)
        b_woall = signal("b_woall", 1)
        b_wosc = signal("b_wosc", 4)
        b_wohi = signal("b_wohi", 1)
        b_wolo = signal("b_wolo", 1)
        b_wost = signal("b_wost", 16)
        b_w = signal("b_w", 48)
        b_a = signal("b_a", 2)
        b_stat = signal("b_stat", 9)
        b_rs = signal("b_rs", 1)
        b_xn = signal("b_xn", 4)
        b_t = signal("b_t", 4)
        b_tc = signal("b_tc", 4)
        b_hi = signal("b_hi", 4)
        b_lo = signal("b_lo", 4)
        b_st = [signal(f"b_st{n}", 16) for n in range(2)]
        b_dt = signal("b_dt", 1)
        b_sp = signal("b_sp", 4)
        b_sm = signal("b_sm", 2)
        b_z = signal("b_z", 1)
        b_da = signal("b_da", 16)
        b_tt = signal("b_tt", 1)
        b_tk = signal("b_tk", 1)

        def acc_slot(tile):
            return (tile + 1) % TILES

        def b_dve_stats(dve, u, first=False):
            slot = acc_slot(u)
            for q in range(4):
                dve.bn_stats(b_stats[:, q, :], acc[:, slot * 4 + q, :]).then_inc(b_stat.sem, 1)
            if not first:
                dve.wait_ge(b_xn.sem, b_xn.at(u - 1, 4))
            for q in range(4):
                dve.wait_ge(b_stat.sem, b_stat.at(u, q + 1))
                dve.sem_inc(stand, 1)
                dve.bn_aggr(b_mv[:, q, :], b_stats[:, q, :]).then_inc(b_stat.sem, 1)
            dve.wait_ge(b_stat.sem, b_stat.at(u, 8))
            dve.tensor_scalar(b_vpe, b_mv[:, :, 1], EPS, None, ALU.add).then_inc(b_stat.sem, 1)

        def b_dve_norm(dve, u, first=False):
            slot = acc_slot(u)
            dve.wait_ge(b_rs.sem, b_rs.at(u, 1))
            if not first:
                dve.wait_ge(b_t.sem, b_t.at(u - 1, 4))
            for q in range(4):
                dve.tensor_scalar(b_xh[:, q, :], acc[:, slot * 4 + q, :], b_mv[:, q, 0:1], b_rstd[:, q:q + 1],
                                  ALU.subtract, ALU.mult).then_inc(b_xn.sem, 1)

        def b_dve_low(dve, u, par):
            for k in range(KT):
                dve.wait_ge(b_hi.sem, b_hi.at(u, k + 1))
                dve.scalar_tensor_tensor(out=b_split[:, par, 1, k, :], in0=bank[k][:, :], scalar=X_SCALE,
                                         in1=b_split[:, par, 0, k, :], op0=ALU.mult, op1=ALU.subtract) \
                    .then_inc(b_lo.sem, 1)

        def b_dve_dt(dve, u, first=False):
            dve.wait_ge(b_sp.sem, b_sp.at(u, 1))
            if not first:
                dve.wait_ge(b_tt.sem, b_tt.at(u - 1, 1))
                dve.wait_ge(b_sp.sem, b_sp.at(u - 1, 4))
            dve.tensor_scalar(dtv, bank[4][0:H, :], dtb, 0.0, ALU.add, ALU.max).then_inc(b_sm.sem, 1)
            dve.wait_ge(b_sm.sem, b_sm.at(u, 1))
            dve.wait_ge(b_sp.sem, b_sp.at(u, 3))
            dve.tensor_tensor(dtv, dtv, lnv, ALU.add).then_inc(b_sm.sem, 1)

        def b_dve_tok(dve, u):
            dve.wait_ge(b_tt.sem, b_tt.at(u, 1))
            dve.tensor_copy(dt_tok[:, bass.ds(u * 4, 4), :], bank[5][:, 0:4 * H].rearrange("p (q h) -> p q h", h=H)) \
                .then_inc(b_tk.sem, 1)

        b_end = used[0]

        def load_wo(sp, u, par, first=False):
            if not first:
                sp.wait_ge(b_wolo.sem, b_wolo.at(u - 2, 1))
                sp.sem_inc(stand, 1)
            sp.dma_start(wo_f[:, par], w_out[u].rearrange("p t d -> p (t d)")).then_inc(b_woin[par].sem, 16)

        def store_wo(sp, u):
            sp.wait_ge(b_wolo.sem, b_wolo.at(u, 1))
            sp.sem_inc(stand, 1)
            sp.dma_start(wo_d[u], wo_s).then_inc(b_wost.sem, 16)

        def pool_wo_norm(pool, u, r, par):
            pool.wait_ge(b_woin[par].sem, b_woin[par].at(r, 16))
            pool.sem_inc(stand, 1)
            w = wo_f[:, par].rearrange("p (t d) -> p t d", t=4)
            pool.tensor_tensor(w, w, nw[:, bass.ds(u * 4, 4)].unsqueeze(2).broadcast_to([P, 4, DM]), ALU.mult) \
                .then_inc(b_won.sem, 1)

        def dve_wo_max(dve, u, par):
            dve.wait_ge(b_won.sem, b_won.at(u, 1))
            dve.sem_inc(stand, 1)
            dve.tensor_reduce(b_max[:, 0:1], wo_f[:, par], AX_X, ALU.max, apply_absolute_value=True).then_inc(b_womax.sem, 1)

        def pool_wo_max(pool, u):
            pool.wait_ge(b_womax.sem, b_womax.at(u, 1))
            pool.sem_inc(stand, 1)
            pool.partition_all_reduce(b_max[:, 1:2], b_max[:, 0:1], P, bass.bass_isa.ReduceOp.max) \
                .then_inc(b_woall.sem, 1)

        def dve_wo_scale(dve, u):
            dve.wait_ge(b_woall.sem, b_woall.at(u, 1))
            dve.sem_inc(stand, 1)
            power_of_two(dve, b_max, b_wosc, u, 0)
            dve.tensor_scalar(wo_unscale[:, bass.ds(u, 1)], b_max[:, 3:4], 1.0, None, ALU.mult).then_inc(b_wosc.sem, 1)

        def act_wo_high(act, u, par, first=False):
            act.wait_ge(b_wosc.sem, b_wosc.at(u, 4))
            if not first:
                act.wait_ge(b_wost.sem, b_wost.at(u - 1, 16))
            act.sem_inc(stand, 1)
            act.activation(wo_s[:, 0], wo_f[:, par], ACT.Copy, scale=b_max[:, 4:5]).then_inc(b_wohi.sem, 1)

        def dve_wo_low(dve, u, par):
            dve.wait_ge(b_wohi.sem, b_wohi.at(u, 1))
            dve.sem_inc(stand, 1)
            dve.scalar_tensor_tensor(out=wo_s[:, 1], in0=wo_f[:, par], scalar=b_max[:, 4:5], in1=wo_s[:, 0],
                                     op0=ALU.mult, op1=ALU.subtract).then_inc(b_wolo.sem, 1)

        def b_pool_rstd(pool, u):
            pool.wait_ge(b_stat.sem, b_stat.at(u, 9))
            pool.tensor_tensor(b_rstd, b_vpe, half_neg[:, :], ALU.pow).then_inc(b_rs.sem, 1)

        def b_pool_zero(pool, u):
            pool.wait_ge(b_sp.sem, b_sp.at(u, 4))
            pool.sem_inc(stand, 1)
            pool.memset(dav[:, :, 0:1], 0.0).then_inc(b_z.sem, 1)

        def b_pe_x(pe, u, first=False):
            pe.wait_ge(b_xn.sem, b_xn.at(u, 4))
            for k in range(KT):
                if not first:
                    pe.wait_ge(b_lo.sem, b_lo.at(u - 1, k + 1))
                for q in range(4):
                    mm = pe.transpose(bank[k][:, q * P:(q + 1) * P], b_xh[:, q, k * P:(k + 1) * P], ident[:, :])
                mm.then_inc(b_t.sem, 1)

        def b_pe_dt(pe, u, first=False):
            if first:
                pe.wait_ge(b_w.sem, 48)
            else:
                pe.wait_ge(b_sm.sem, b_sm.at(u - 1, 1))
            for k in range(KT):
                pe.wait_ge(b_tc.sem, b_tc.at(u, k + 1))
                mm = pe.matmul(bank[4][0:H, :], w_dt_sb[:, k, :], b_xT[:, k, :], start=k == 0, stop=k == KT - 1)
            mm.then_inc(b_dt.sem, 1)

        def b_pe_tok(pe, u, first=False):
            pe.wait_ge(b_sm.sem, b_sm.at(u, 2))
            if not first:
                pe.wait_ge(b_tk.sem, b_tk.at(u - 1, 1))
            pe.sem_inc(stand, 1)
            for q in range(4):
                mm = pe.transpose(bank[5][:, q * H:(q + 1) * H], dtv[:, q * P:(q + 1) * P], ident[0:H, 0:H])
            mm.then_inc(b_tt.sem, 1)

        def b_act_x(act, u, r, par, first=False):
            for k in range(KT):
                act.wait_ge(b_t.sem, b_t.at(u, k + 1))
                if k == 0 and not first:
                    act.wait_ge(b_dt.sem, b_dt.at(u - 1, 1))
                    if not (isinstance(r, int) and r == 0):
                        act.wait_ge(b_st[par].sem, b_st[par].at(r - 1, 16))
                act.activation(b_xT[:, k, :], bank[k][:, :], ACT.Copy).then_inc(b_tc.sem, 1)
                act.activation(b_split[:, par, 0, k, :], bank[k][:, :], ACT.Copy, scale=X_SCALE).then_inc(b_hi.sem, 1)

        def b_act_dt(act, u, first=False):
            act.wait_ge(b_dt.sem, b_dt.at(u, 1))
            act.activation(absv, bank[4][0:H, :], ACT.Abs, bias=dtb).then_inc(b_sp.sem, 1)
            act.wait_ge(b_sp.sem, b_sp.at(u, 1))
            act.activation(expv, absv, ACT.Exp, scale=-1.0).then_inc(b_sp.sem, 1)
            act.wait_ge(b_sp.sem, b_sp.at(u, 2))
            if not first:
                act.wait_ge(b_sm.sem, b_sm.at(u - 1, 2))
            act.activation(lnv, expv, ACT.Ln, bias=1.0).then_inc(b_sp.sem, 1)

        def b_act_da(act, u, first=False):
            act.wait_ge(b_sm.sem, b_sm.at(u, 2))
            if not first:
                act.wait_ge(b_da.sem, b_da.at(u - 1, 16))
            act.activation(dav, dtv.rearrange("p (b t) -> p b t", t=SEQ), ACT.Exp, scale=a_neg[:, 1:2]).then_inc(b_sp.sem, 1)

        def store_x(sp, u, par):
            sp.wait_ge(b_lo.sem, b_lo.at(u, 4))
            sp.sem_inc(stand, 1)
            sp.dma_start(xt_d[u], b_split[:, par]).then_inc(b_st[par].sem, 16)

        def store_da(sp, u, first=False):
            sp.wait_ge(b_z.sem, b_z.at(u, 1))
            if not first:
                sp.wait_ge(b_da.sem, b_da.at(u - 1, 16))
            sp.sem_inc(stand, 1)
            sp.dma_start(da_d[bass.ds(u * 8, 8)].rearrange("b h t -> h b t"), dav).then_inc(b_da.sem, 16)

        def b_turns(engine, turn):
            turn(0, 0, 1, first=True)
            with engine.Fori(1, TILES // 2) as r:
                turn(2 * r - 1, r, 0)
                turn(2 * r, r, 1)
            turn(TILES - 1, TILES // 2, 0, last=True)

        used[0] = 0
        cv = view(3, TOK)
        bc = view(2, TOK)
        xs = view(4, TOK)
        gs = view(4, TOK)
        yn = halves(view(2, 4, TOK // 2))
        sq = view(4, TOK)
        w_o = halves(view(2, 4, DM // 2))
        y_max = view(8)
        wo_u = view(1)
        rs = view(4)
        y = view(4, TOK)
        ms = view(4)
        rr = view(4)
        ones = view(1)
        used[0] = max(used[0], b_end)
        w_g = halves(view(CT + GATES, KT * P)).rearrange("p n (s k c) -> p n s k c", s=2, k=KT)
        xT = halves(view(2, 2, KT, TOK // 2))
        da = view(4, HG * SEQ)
        mm_sb = view(4, HG * SEQ)
        dtx = view(4, 4 * P)
        c_end = used[0]

        c_xt = [signal(f"c_xt{n}", 16) for n in range(2)]
        c_da = signal("c_da", 32)
        c_wbcx = signal("c_wbcx", 16)
        c_wgate = signal("c_wgate", 16)
        c_wo = signal("c_wo", 16)
        c_wu = signal("c_wu", 1)
        c_ymax = signal("c_ymax", 1)
        c_yall = signal("c_yall", 1)
        c_ysc = signal("c_ysc", 3)
        c_yhi = signal("c_yhi", 2)
        c_ylo = signal("c_ylo", 2)
        c_rs = signal("c_rs", 1)
        c_init = signal("c_init", 4)
        c_proj = signal("c_proj", CT + GATES)
        c_cb = signal("c_cb", 1)
        c_t = signal("c_t", 4)
        c_y = signal("c_y", 2)
        c_norm = signal("c_norm", 1)
        c_o = signal("c_o", 4)
        c_tap = signal("c_tap", CT)
        c_silu = signal("c_silu", CT)
        c_gate = signal("c_gate", GATES, GATES)
        c_sq = signal("c_sq", 1)
        c_ssum = signal("c_ssum", 2)
        c_xd = signal("c_xd", 4, 4)
        c_conv = signal("c_conv", 3 * CT)
        c_yadd = signal("c_yadd", 4)
        c_yn = signal("c_yn", 1)
        c_rms = signal("c_rms", 1)
        c_r = signal("c_r", 1)
        c_acc = signal("c_acc", 4)
        c_scan = signal("c_scan", 4)
        c_m = signal("c_m", 4, 4)
        c_dtx = signal("c_dtx", 4, 4)

        def project(pe, it, par, n):
            b = bank[n % 3]
            if n >= 3:
                m, turn = n - 3, it
            else:
                m, turn = (9, 7, 8)[n], it - 1
            if m < CT:
                pe.wait_ge(c_conv.sem, c_conv.at(turn, 3 * m + 3))
            else:
                pe.wait_ge(c_gate.sem, c_gate.at(turn, m - CT + 1))
            steps = [(w_part, x_part, k) for w_part, x_part in ((0, 0), (0, 1), (1, 0)) for k in range(KT)]
            for s, (w_part, x_part, k) in enumerate(steps):
                mm = pe.matmul(b[:, :], w_g[:, n, w_part, k, :], xT[:, par, x_part, k, :],
                               start=s == 0, stop=s == len(steps) - 1)
            mm.then_inc(c_proj.sem, 1)

        def heads_out(pe, it, half):
            pe.wait_ge(c_m.sem, c_m.at(it - 1, 2 * half + 2))
            pe.wait_ge(c_dtx.sem, c_dtx.at(it - 1, 2 * half + 2))
            if half == 1:
                pe.wait_ge(c_acc.sem, c_acc.at(it - 1, 4))
            pe.sem_inc(stand, 1)
            for q2 in range(2):
                q = 2 * half + q2
                for h in range(HG):
                    for b in range(2):
                        mm = pe.matmul(bank[4 + 2 * half + b][64 * (h % 2):64 * (h % 2) + 64,
                                                   (h // 2) * P + q2 * SEQ:(h // 2) * P + (q2 + 1) * SEQ],
                                       dtx[64 * b:64 * b + 64, q, h * HP:(h + 1) * HP],
                                       mm_sb[64 * b:64 * b + 64, q, h * SEQ:(h + 1) * SEQ], start=True, stop=True)
            mm.then_inc(c_y.sem, 1)

        def norm_sums(pe, it, last=False):
            pe.wait_ge(c_ssum.sem, c_ssum.at(it, 2))
            if not last:
                pe.wait_ge(c_dtx.sem, c_dtx.at(it, 1))
            for q in range(4):
                mm = pe.matmul(bank[4][:, q:q + 1], sq[:, 0, q * P:(q + 1) * P], ones, start=True, stop=True)
            mm.then_inc(c_norm.sem, 1)

        def out_product(pe, it, q, last=False):
            if q % 2 == 0:
                pe.wait_ge(c_ylo.sem, c_ylo.at(it, q // 2 + 1))
            if q < 2 and not last:
                pe.wait_ge(c_dtx.sem, c_dtx.at(it, 2 * q + 2))
            if q >= 2:
                pe.wait_ge(c_acc.sem, c_acc.at(it, q - 1))
            steps = [(y_part, w_part, t) for y_part, w_part in ((0, 0), (0, 1), (1, 0)) for t in range(4)]
            for s, (y_part, w_part, t) in enumerate(steps):
                mm = pe.matmul(bank[6 + q % 2][:, :], yn[:, y_part, t, q * P:(q + 1) * P], w_o[:, w_part, t, :],
                               start=s == 0, stop=s == len(steps) - 1)
            mm.then_inc(c_o.sem, 1)

        def cb_product(pe, it):
            pe.wait_ge(c_silu.sem, c_silu.at(it, 2))
            for q in range(4):
                for b in range(2):
                    at = q * P + b * SEQ
                    mm = pe.matmul(bank[3][64 * b:64 * b + 64, q * SEQ:(q + 1) * SEQ], bc[:, 0, at:at + SEQ],
                                   bc[:, 1, at:at + SEQ], start=True, stop=True)
            mm.then_inc(c_cb.sem, 1)

        def turn_x(pe, it, q):
            if q == 0:
                pe.wait_ge(c_silu.sem, c_silu.at(it, CT))
                pe.wait_ge(c_yadd.sem, c_yadd.at(it, 4))
            for t in range(4):
                mm = pe.transpose(bank[X_BANK[q]][:, t * P:(t + 1) * P], xs[:, t, q * P:(q + 1) * P], ident[:, :])
            mm.then_inc(c_t.sem, 1)

        def c_pe_turn(pe, g, j, par):
            it = g * TILES + j * 2 + par
            pe.wait_ge(c_xt[par].sem, c_xt[par].at(g * 4 + j, 16))
            pe.wait_ge(c_wbcx.sem, c_wbcx.at(g, 16))
            for n in range(3):
                project(pe, it, par, n)
            heads_out(pe, it, 0)
            project(pe, it, par, 3)
            heads_out(pe, it, 1)
            project(pe, it, par, 4)
            project(pe, it, par, 5)
            pe.wait_ge(c_wgate.sem, c_wgate.at(g, 16))
            project(pe, it, par, CT)
            project(pe, it, par, CT + 1)
            for q in range(4):
                turn_x(pe, it, q)
            project(pe, it, par, CT + 2)
            cb_product(pe, it)
            if par == 1:
                pe.wait_ge(c_wo.sem, c_wo.at(g, 16))
            out_product(pe, it, 0)
            norm_sums(pe, it)
            out_product(pe, it, 1)
            project(pe, it, par, CT + 3)
            out_product(pe, it, 2)
            out_product(pe, it, 3)

        def square(act, it):
            act.wait_ge(c_yadd.sem, c_yadd.at(it, 4))
            act.activation(sq, y, ACT.Square).then_inc(c_sq.sem, 1)

        def y_high(act, it):
            act.wait_ge(c_ysc.sem, c_ysc.at(it, 3))
            act.sem_inc(stand, 1)
            for half in range(2):
                tok = slice(half * TOK // 2, (half + 1) * TOK // 2)
                act.activation(yn[:, 0, :, tok], gs[:, :, tok], ACT.Copy, scale=y_max[:, 4:5]).then_inc(c_yhi.sem, 1)

        def c_act_turn(act, g, j, par):
            it = g * TILES + j * 2 + par

            def tap(n):
                i = g * CT + n
                act.wait_ge(c_proj.sem, c_proj.at(it, n + 1))
                if n >= 3:
                    act.wait_ge(c_silu.sem, c_silu.at(it, n - 2))
                act.sem_inc(stand, 1)
                act.activation(cv[:, n % 3, :], bank[n % 3][:, :], ACT.Identity, bias=cb[:, bass.ds(i, 1)],
                               scale=cw[:, bass.ds(i, 1), 3]).then_inc(c_tap.sem, 1)

            def silu(n):
                act.wait_ge(c_conv.sem, c_conv.at(it, 3 * n + 3))
                act.activation(bc[:, n, :] if n < 2 else xs[:, n - 2, :], cv[:, n % 3, :], ACT.Silu) \
                    .then_inc(c_silu.sem, 1)

            tap(0)
            tap(1)
            for n in range(CT - 2):
                silu(n)
                tap(n + 2)
            silu(CT - 2)
            square(act, it)
            silu(CT - 1)
            y_high(act, it)
            act.wait_ge(c_ylo.sem, c_ylo.at(it, 2))

            def gate(n):
                act.wait_ge(c_proj.sem, c_proj.at(it, CT + n + 1))
                act.sem_inc(stand, 1)
                act.activation(gs[:, n, :], bank[(CT + n) % 3][:, :], ACT.Silu,
                               scale=w_unscale[:, bass.ds(g * (CT + GATES) + CT + n, 1)]).then_inc(c_gate.sem, 1)

            for n in range(GATES - 1):
                gate(n)
            act.wait_ge(c_yn.sem, c_yn.at(it, 1))
            for t in range(4):
                act.wait_ge(c_silu.sem, c_silu.at(it, 3 + t))
                act.sem_inc(stand, 1)
                act.activation(y[:, t, :], xs[:, t, :], ACT.Copy, scale=dsk[:, bass.ds(g * 4 + t, 1)]).then_inc(c_xd.sem, 1)
            gate(GATES - 1)

        def y_add(dve, it, half):
            dve.wait_ge(c_y.sem, c_y.at(it, half + 1))
            if half == 0:
                dve.wait_ge(c_xd.sem, c_xd.at(it - 1, 4))
            for b in range(2):
                part = y.rearrange("p c (q b t) -> p c q b t", b=2, t=SEQ)[:, :, 2 * half:2 * half + 2, b, :]
                dve.tensor_tensor(part, part, bank[4 + 2 * half + b][:, :].rearrange("p (c q t) -> p c q t", q=2, t=SEQ), ALU.add) \
                    .then_inc(c_yadd.sem, 1)

        def y_gate(dve, it):
            dve.wait_ge(c_yadd.sem, c_yadd.at(it, 4))
            dve.wait_ge(c_gate.sem, c_gate.at(it - 1, GATES))
            dve.tensor_tensor(gs, y, gs, ALU.mult).then_inc(c_yn.sem, 1)

        def y_largest(dve, it):
            dve.wait_ge(c_yn.sem, c_yn.at(it, 1))
            dve.sem_inc(stand, 1)
            dve.tensor_reduce(y_max[:, 0:1], gs.rearrange("p c t -> p (c t)"), AX_X, ALU.max,
                              apply_absolute_value=True).then_inc(c_ymax.sem, 1)

        def y_scale(dve, it):
            dve.wait_ge(c_yall.sem, c_yall.at(it, 1))
            dve.sem_inc(stand, 1)
            power_of_two(dve, y_max, c_ysc, it, 0)

        def y_low(dve, it, half):
            tok = slice(half * TOK // 2, (half + 1) * TOK // 2)
            dve.wait_ge(c_yhi.sem, c_yhi.at(it, half + 1))
            dve.sem_inc(stand, 1)
            dve.scalar_tensor_tensor(out=yn[:, 1, :, tok], in0=gs[:, :, tok], scalar=y_max[:, 4:5],
                                     in1=yn[:, 0, :, tok], op0=ALU.mult, op1=ALU.subtract).then_inc(c_ylo.sem, 1)

        def mean_square(dve, it):
            dve.wait_ge(c_norm.sem, c_norm.at(it, 1))
            dve.tensor_scalar(ms, bank[4][:, 0:4], 1.0 / 512, EPS, ALU.mult, ALU.add).then_inc(c_rms.sem, 1)

        def row_scale(dve, it):
            dve.wait_ge(c_r.sem, c_r.at(it, 1))
            dve.sem_inc(stand, 1)
            dve.tensor_scalar(rs, rr, y_max[:, 3:4], wo_u, ALU.mult, ALU.mult).then_inc(c_rs.sem, 1)

        def add_out(dve, it, slot, q):
            dve.wait_ge(c_rs.sem, c_rs.at(it, 1))
            dve.wait_ge(c_o.sem, c_o.at(it, q + 1))
            a = acc[:, slot * 4 + q, :]
            dve.scalar_tensor_tensor(out=a, in0=bank[6 + q % 2][:, :], scalar=rs[:, q:q + 1], in1=a,
                                     op0=ALU.mult, op1=ALU.add).then_inc(c_acc.sem, 1)

        def c_dve_turn(dve, g, j, par):
            it = g * TILES + j * 2 + par
            u = j * 2 + par

            def conv(n):
                i = g * CT + n
                h = bank[n % 3][:, :].rearrange("p (b t) -> p b t", t=SEQ)
                o = cv[:, n % 3, :].rearrange("p (b t) -> p b t", t=SEQ)
                for tap in range(3):
                    s = 3 - tap
                    if tap == 0:
                        dve.wait_ge(c_tap.sem, c_tap.at(it, n + 1))
                    else:
                        dve.wait_ge(c_conv.sem, c_conv.at(it, 3 * n + tap))
                    dve.scalar_tensor_tensor(out=o[:, :, s:], in0=h[:, :, 0:SEQ - s], scalar=cw[:, bass.ds(i, 1), tap],
                                             in1=o[:, :, s:], op0=ALU.mult, op1=ALU.add).then_inc(c_conv.sem, 1)

            def head_values(q):
                dve.wait_ge(c_t.sem, c_t.at(it, q + 1))
                dt = dt_tok[:, u * 4 + q, bass.ds(g * HG, HG)].unsqueeze(2).broadcast_to([P, HG, HP])
                dve.tensor_tensor(dtx[:, q, :].rearrange("p (h c) -> p h c", c=HP),
                                  bank[X_BANK[q]][:, :].rearrange("p (h c) -> p h c", c=HP), dt, ALU.mult) \
                    .then_inc(c_dtx.sem, 1)

            for n in range(3):
                conv(n)
            y_add(dve, it, 0)
            conv(3)
            y_add(dve, it, 1)
            y_gate(dve, it)
            conv(4)
            conv(5)
            y_largest(dve, it)
            y_scale(dve, it)
            head_values(0)
            y_low(dve, it, 0)
            for q in range(1, 4):
                head_values(q)
            y_low(dve, it, 1)
            mean_square(dve, it)
            dve.wait_ge(c_da.sem, c_da.at(it, 32))
            for q in range(4):
                dve.tensor_tensor_scan(mm_sb[:, q, :], da[:, q, :], eye[:, :], 0.0, ALU.mult, ALU.add) \
                    .then_inc(c_scan.sem, 1)
            row_scale(dve, it)
            add_out(dve, it, u, 0)
            add_out(dve, it, u, 1)
            dve.wait_ge(c_cb.sem, c_cb.at(it, 1))
            for q in range(4):
                dve.wait_ge(c_scan.sem, c_scan.at(it, q + 1))
                m = mm_sb[:, q, :].rearrange("p (h t) -> p h t", t=SEQ)
                dve.tensor_tensor(m, m, bank[3][:, q * SEQ:(q + 1) * SEQ].unsqueeze(1).broadcast_to([P, HG, SEQ]),
                                  ALU.mult).then_inc(c_m.sem, 1)
            add_out(dve, it, u, 2)
            add_out(dve, it, u, 3)

        def c_pool_turn(pool, it):
            pool.wait_ge(c_ymax.sem, c_ymax.at(it, 1))
            pool.sem_inc(stand, 1)
            pool.partition_all_reduce(y_max[:, 1:2], y_max[:, 0:1], P, bass.bass_isa.ReduceOp.max) \
                .then_inc(c_yall.sem, 1)
            pool.wait_ge(c_sq.sem, c_sq.at(it, 1))
            pool.tensor_tensor(sq[:, 0:2, :], sq[:, 0:2, :], sq[:, 2:4, :], ALU.add).then_inc(c_ssum.sem, 1)
            pool.wait_ge(c_ssum.sem, c_ssum.at(it, 1))
            pool.tensor_tensor(sq[:, 0, :], sq[:, 0, :], sq[:, 1, :], ALU.add).then_inc(c_ssum.sem, 1)
            pool.wait_ge(c_rms.sem, c_rms.at(it, 1))
            pool.tensor_tensor(rr, ms, half_neg[:, :], ALU.pow).then_inc(c_r.sem, 1)

        def c_pool_group(pool, g):
            c_pool_turn(pool, g * TILES)
            pool.wait_ge(c_o.sem, c_o.at(g * TILES, 4))
            pool.sem_inc(stand, 1)
            pool.dma_start(w_o.rearrange("p s t d -> p s (t d)"), wo_d[g]).then_inc(c_wo.sem, 16)
            pool.wait_ge(c_rs.sem, c_rs.at(g * TILES, 1))
            pool.sem_inc(stand, 1)
            pool.tensor_copy(wo_u, wo_unscale[:, bass.ds(g, 1)]).then_inc(c_wu.sem, 1)
            pool.wait_ge(c_wu.sem, c_wu.at(g, 1))
            pool.sem_inc(stand, 1)
            with pool.Fori(1, TILES) as u:
                c_pool_turn(pool, g * TILES + u)

        def load_da(sp, tile, g):
            for b in range(2):
                src = da_d[bass.ds(tile * 8, 8)].rearrange("(q b) h t -> b q (h t)", b=2)[b][
                    :, bass.ds(g * (HG * SEQ), HG * SEQ)]
                sp.dma_start(da[64 * b:64 * b + 64], src.unsqueeze(0).broadcast_to([64, 4, HG * SEQ])) \
                    .then_inc(c_da.sem, 16)

        def load_weights(sp, g, a, b, arrived):
            sp.dma_start(w_g[:, a:b].rearrange("p n s k c -> p n (s k c)"),
                         w_d[:, bass.ds(g * (CT + GATES) + a, b - a)].rearrange("p n s c -> p n (s c)")) \
                .then_inc(arrived.sem, 16)

        def c_sp_turn(sp, g, j, par, last=False):
            it = g * TILES + j * 2 + par
            u = j * 2 + par
            final = isinstance(j, int) and u == TILES - 1
            if final and not last:
                sp.wait_ge(c_proj.sem, c_proj.at(it, CT))
                sp.sem_inc(stand, 1)
                load_weights(sp, g + 1, 0, CT, c_wbcx)
            if not (final and last):
                sp.wait_ge(c_scan.sem, c_scan.at(it, 4))
                sp.sem_inc(stand, 1)
                sp.wait_ge(c_da.sem, c_da.at(it, 32))
                sp.sem_inc(stand, 1)
                load_da(sp, 0 if final else u + 1, g + 1 if final else g)
            if not (isinstance(j, int) and j == 3 and last):
                sp.wait_ge(c_proj.sem, c_proj.at(it, CT + GATES))
                sp.sem_inc(stand, 1)
                sp.dma_start(xT[:, par], xt_d[par] if isinstance(j, int) and j == 3 else xt_d[u + 2]) \
                    .then_inc(c_xt[par].sem, 16)
            if final and not last:
                load_weights(sp, g + 1, CT, CT + GATES, c_wgate)

        def c_sp(sp):
            def group(g, last=False):
                with sp.Fori(0, 3) as j:
                    c_sp_turn(sp, g, j, 0)
                    c_sp_turn(sp, g, j, 1)
                c_sp_turn(sp, g, 3, 0, last)
                c_sp_turn(sp, g, 3, 1, last)

            with sp.Fori(0, G - 1) as g:
                group(g)
            group(G - 1, last=True)

        used[0] = c_end
        wr = view(KT, E)
        br = view(E)
        eb = view(DM, parts=E)
        used[0] = 0
        d_xh = view(2, 4, DM)
        d_xT = view(KT, TOK)
        lg = view(4, E)
        d_mx = view(4)
        top = view(4, 8)
        rest = view(4, E)
        wd = view(4, E)
        d_sum = view(4)
        d_rs = view(4)
        d_ts = view(4)
        ws = view(4)
        wT = view(TOK, parts=E)
        d_stats = view(4, 6)
        d_mv = view(4, 2)
        d_vpe = view(4)
        d_rstd = view(4)

        d_w = signal("d_w", 48)
        d_stat = signal("d_stat", 9)
        d_rp = signal("d_rp", 1)
        d_xn = signal("d_xn", 4)
        d_t = signal("d_t", 4)
        d_tc = signal("d_tc", 4)
        d_lg = signal("d_lg", 1)
        d_l = signal("d_l", 3)
        d_e = signal("d_e", 1)
        d_k = signal("d_k", 14)
        d_wt = signal("d_wt", 1)
        d_wc = signal("d_wc", 1)
        d_mix = signal("d_mix", 4)
        d_o = signal("d_o", 8)
        d_st = signal("d_st", 16)

        def d_dve_stats(dve, n, first=False):
            for q in range(4):
                dve.bn_stats(d_stats[:, q, :], acc[:, n * 4 + q, :]).then_inc(d_stat.sem, 1)
            if not first:
                dve.wait_ge(d_xn.sem, d_xn.at(n - 1, 4))
            for q in range(4):
                dve.wait_ge(d_stat.sem, d_stat.at(n, q + 1))
                dve.sem_inc(stand, 1)
                dve.bn_aggr(d_mv[:, q, :], d_stats[:, q, :]).then_inc(d_stat.sem, 1)
            dve.wait_ge(d_stat.sem, d_stat.at(n, 8))
            dve.tensor_scalar(d_vpe, d_mv[:, :, 1], EPS, None, ALU.add).then_inc(d_stat.sem, 1)

        def d_dve_norm(dve, n, par):
            dve.wait_ge(d_rp.sem, d_rp.at(n, 1))
            for q in range(4):
                dve.tensor_scalar(d_xh[:, par, q, :], acc[:, n * 4 + q, :], d_mv[:, q, 0:1], d_rstd[:, q:q + 1],
                                  ALU.subtract, ALU.mult).then_inc(d_xn.sem, 1)

        def d_dve_logits(dve, n):
            dve.wait_ge(d_lg.sem, d_lg.at(n, 1))
            dve.tensor_tensor(lg, bank[4][:, 0:4 * E].rearrange("p (q e) -> p q e", e=E),
                              br.unsqueeze(1).broadcast_to([P, 4, E]), ALU.add).then_inc(d_l.sem, 1)
            dve.wait_ge(d_l.sem, d_l.at(n, 1))
            dve.tensor_reduce(d_mx, lg, AX_X, ALU.max).then_inc(d_l.sem, 1)
            dve.wait_ge(d_l.sem, d_l.at(n, 2))
            dve.tensor_tensor(lg, lg, d_mx.unsqueeze(2).broadcast_to([P, 4, E]), ALU.subtract).then_inc(d_l.sem, 1)

        def d_dve_choose(dve, n):
            dve.wait_ge(d_e.sem, d_e.at(n, 1))
            dve.tensor_reduce(d_sum, lg, AX_X, ALU.add).then_inc(d_k.sem, 1)
            for q in range(4):
                dve.max(top[:, q, :], lg[:, q, :]).then_inc(d_k.sem, 1)
            dve.wait_ge(d_k.sem, d_k.at(n, 1))
            dve.reciprocal(d_rs, d_sum).then_inc(d_k.sem, 1)
            dve.wait_ge(d_k.sem, d_k.at(n, 5))
            dve.tensor_reduce(d_ts, top, AX_X, ALU.add).then_inc(d_k.sem, 1)
            for q in range(4):
                dve.sem_inc(stand, 1)
                dve.match_replace(rest[:, q, :], top[:, q, :], lg[:, q, :], 0.0).then_inc(d_k.sem, 1)
            dve.wait_ge(d_k.sem, d_k.at(n, 11))
            dve.tensor_tensor(wd, lg, rest, ALU.subtract).then_inc(d_k.sem, 1)
            dve.wait_ge(d_k.sem, d_k.at(n, 12))
            dve.tensor_tensor(wd, wd, d_rs.unsqueeze(2).broadcast_to([P, 4, E]), ALU.mult).then_inc(d_k.sem, 1)
            dve.tensor_tensor(ws, d_ts, d_rs, ALU.mult).then_inc(d_k.sem, 1)

        def d_dve_scaled(dve, n, par):
            dve.wait_ge(d_k.sem, d_k.at(n, 14))
            for q in range(4):
                a = acc[:, n * 4 + q, :]
                dve.scalar_tensor_tensor(out=a, in0=d_xh[:, par, q, :], scalar=ws[:, q:q + 1], in1=a,
                                         op0=ALU.mult, op1=ALU.add).then_inc(d_o.sem, 1)

        def d_dve_mixed(dve, n):
            for q in range(4):
                a = acc[:, n * 4 + q, :]
                dve.wait_ge(d_o.sem, d_o.at(n, q + 1))
                dve.wait_ge(d_mix.sem, d_mix.at(n, q + 1))
                dve.tensor_tensor(a, a, bank[6 + q % 2][:, :], ALU.add).then_inc(d_o.sem, 1)

        def d_pe_x(pe, n, par, first=False):
            pe.wait_ge(d_xn.sem, d_xn.at(n, 4))
            for k in range(KT):
                if not first:
                    pe.wait_ge(d_tc.sem, d_tc.at(n - 1, k + 1))
                for q in range(4):
                    mm = pe.transpose(bank[k][:, q * P:(q + 1) * P], d_xh[:, par, q, k * P:(k + 1) * P], ident[:, :])
                mm.then_inc(d_t.sem, 1)

        def d_pe_logits(pe, n, first=False):
            pe.wait_ge(d_tc.sem, d_tc.at(n, 4))
            if not first:
                pe.wait_ge(d_l.sem, d_l.at(n - 1, 1))
            for q in range(4):
                for k in range(KT):
                    mm = pe.matmul(bank[4][:, q * E:(q + 1) * E], d_xT[:, k, q * P:(q + 1) * P], wr[:, k, :],
                                   start=k == 0, stop=k == KT - 1)
            mm.then_inc(d_lg.sem, 1)

        def d_pe_turn_w(pe, n, first=False):
            pe.wait_ge(d_k.sem, d_k.at(n, 13))
            if not first:
                pe.wait_ge(d_wc.sem, d_wc.at(n - 1, 1))
            pe.sem_inc(stand, 1)
            for q in range(4):
                mm = pe.transpose(bank[5][0:E, q * P:(q + 1) * P], wd[:, q, :], ident[:, :])
            mm.then_inc(d_wt.sem, 1)

        def d_pe_mix(pe, n, first=False):
            pe.wait_ge(d_wc.sem, d_wc.at(n, 1))
            for q in range(4):
                if q >= 2:
                    pe.wait_ge(d_o.sem, d_o.at(n, q + 3))
                elif not first:
                    pe.wait_ge(d_o.sem, d_o.at(n - 1, q + 7))
                pe.sem_inc(stand, 1)
                pe.matmul(bank[6 + q % 2][:, :], wT[:, q * P:(q + 1) * P], eb, start=True, stop=True) \
                    .then_inc(d_mix.sem, 1)

        def d_act_x(act, n, first=False):
            for k in range(KT):
                act.wait_ge(d_t.sem, d_t.at(n, k + 1))
                if k == 0 and not first:
                    act.wait_ge(d_lg.sem, d_lg.at(n - 1, 1))
                act.activation(d_xT[:, k, :], bank[k][:, :], ACT.Copy).then_inc(d_tc.sem, 1)

        def d_act_exp(act, n):
            act.wait_ge(d_l.sem, d_l.at(n, 3))
            act.activation(lg, lg, ACT.Exp).then_inc(d_e.sem, 1)

        def d_act_w(act, n):
            act.wait_ge(d_wt.sem, d_wt.at(n, 1))
            act.activation(wT, bank[5][0:E, :], ACT.Copy).then_inc(d_wc.sem, 1)

        def d_pool(pool, n):
            pool.wait_ge(d_stat.sem, d_stat.at(n, 9))
            pool.tensor_tensor(d_rstd, d_vpe, half_neg[:, :], ALU.pow).then_inc(d_rp.sem, 1)

        def d_turns(engine, turn):
            turn(0, 0, first=True)
            with engine.Fori(1, TILES // 2 - 1) as r:
                turn(2 * r - 1, 1)
                turn(2 * r, 0)
            turn(TILES - 3, 1)
            turn(TILES - 2, 0, late=True)
            turn(TILES - 1, 1, late=True, last=True)

        def d_sp(sp):
            for n in range(TILES):
                t = (n + 7) % TILES
                sp.wait_ge(d_o.sem, d_o.at(n, 8))
                sp.dma_start(out_v[:, 4 * t:4 * t + 4, :], acc[:, 4 * n:4 * n + 4, :]).then_inc(d_st.sem, 16)
            sp.wait_ge(d_st.sem, d_st.at(TILES - 1, 16))

        block = ctx.enter_context(nc.Block())

        @block.sync
        def _(sp):
            for dst, src in ((ident[:, :], ident_in), (parity[:, :], parity_in), (eye[:, :], eye_in),
                             (cw[:, :, :], conv_w), (cb[:, :], conv_b), (dsk[:, :], d_skip), (nw[:, :], norm_w),
                             (maskb[0:SEQ, :], mask), (maskb[SEQ:P, :], mask)):
                sp.dma_start(dst, src).then_inc(consts_in, 16)
            load_pair(sp, 0, 0, first=True)
            load_pair(sp, 1, 1, second=True)
            load_w(sp, 0, 0, first=True)
            load_w(sp, 0, 1, first=True)
            load_pair(sp, 2, 0)
            load_pair(sp, 3, 1)
            with sp.Fori(2, PAIRS // 2) as r:
                for par in range(2):
                    load_pair(sp, 2 * r + par, par)
                    store_w(sp, r - 2, par)
                    load_w(sp, r - 1, par)
            for par in range(2):
                store_w(sp, PAIRS // 2 - 2, par)
                load_w(sp, PAIRS // 2 - 1, par)
            for par in range(2):
                store_w(sp, PAIRS // 2 - 1, par)
            for par in range(2):
                sp.wait_ge(a_wst[par].sem, a_wst[par].at(PAIRS // 2 - 1, 16))
            sp.wait_ge(a_out.sem, a_out.at(PAIRS - 1, 6))
            sp.wait_ge(b_go, 1)
            for dst, src in ((w_dt_sb, w_dt), (dtb, dt_bias), (alog, a_log)):
                sp.dma_start(dst, src).then_inc(b_w.sem, 16)
            for dst, src in ((wr, w_router), (br, b_router.broadcast_to([P, E])), (eb, e_bias)):
                sp.dma_start(dst, src).then_inc(d_w.sem, 16)
            load_weights(sp, 0, 0, CT, c_wbcx)
            load_weights(sp, 0, CT, CT + GATES, c_wgate)
            load_wo(sp, 0, 0, first=True)
            store_x(sp, 0, 0)

            def b_turn(u, r, par, first=False, last=False):
                if not last:
                    load_wo(sp, u + 1, par, first)
                    store_x(sp, u + 1, par)
                store_da(sp, u, first)
                store_wo(sp, u)

            b_turns(sp, b_turn)
            for par in range(2):
                sp.wait_ge(b_st[par].sem, b_st[par].at(TILES // 2 - 1, 16))
            sp.wait_ge(b_da.sem, b_da.at(TILES - 1, 16))
            for par in range(2):
                sp.dma_start(xT[:, par], xt_d[par]).then_inc(c_xt[par].sem, 16)
            load_da(sp, 0, 0)
            c_sp(sp)
            d_sp(sp)

        @block.gpsimd
        def _(pool):
            pool.memset(half_neg[:, :], -0.5).then_inc(half_set, 1)
            pool.memset(v32, 0.0).then_inc(v_zero, 1)
            pool.wait_ge(v_zero, 1)
            pool.memset(v32[:, :, :, :, HD:HD + 1].rearrange("p a b g o -> p (a b g) o"), 1.0).then_inc(a_v.sem, 1)
            pool.wait_ge(half_set, 1)
            pool_front(pool, 0, 0, 0, first=True)
            pool_values(pool, 0, 0, first=True)
            pool_front(pool, 1, 1, 0)
            pool_values(pool, 1, 1, first=True)
            for par in range(2):
                pool_front(pool, 2 + par, par, 1)
                pool_w_max(pool, par, first=par == 0)
                pool_values(pool, 2 + par, par)
            with pool.Fori(1, PAIRS // 2 - 1) as r:
                for par in range(2):
                    pool_front(pool, 2 * r + 2 + par, par, r + 1)
                    pool_w_max(pool, 2 * r + par)
                    pool_values(pool, 2 * r + 2 + par, par)
            pool_w_max(pool, PAIRS - 2)
            pool_w_max(pool, PAIRS - 1)
            pool.wait_ge(b_go, 1)
            b_pool_rstd(pool, 0)
            pool_wo_norm(pool, 0, 0, 0)
            pool.memset(mm_sb, 0.0).then_inc(c_m.sem, 4)
            pool.memset(dtx, 0.0).then_inc(c_dtx.sem, 4)

            def b_turn(u, r, par, first=False, last=False):
                if not last:
                    b_pool_rstd(pool, u + 1)
                pool_wo_max(pool, u)
                b_pool_zero(pool, u)
                if not last:
                    pool_wo_norm(pool, u + 1, r, par)

            b_turns(pool, b_turn)
            pool.wait_ge(b_tk.sem, b_tk.at(TILES - 1, 1))
            pool.wait_ge(b_sp.sem, b_sp.at(TILES - 1, 4))
            pool.wait_ge(b_da.sem, b_da.at(TILES - 1, 16))
            for par in range(2):
                pool.wait_ge(b_st[par].sem, b_st[par].at(TILES // 2 - 1, 16))
            pool.wait_ge(b_wost.sem, b_wost.at(TILES - 1, 16))
            pool.memset(gs, 0.0).then_inc(c_gate.sem, 4)
            pool.memset(y, 0.0).then_inc(c_xd.sem, 4)
            pool.memset(w_o.bitcast(F32), 0.0).then_inc(c_init.sem, 1)
            pool.memset(wo_u, 1.0).then_inc(c_init.sem, 1)
            pool.memset(ones, 1.0).then_inc(c_init.sem, 1)
            pool.wait_ge(a_wsc.sem, a_wsc.at(PAIRS - 1, 4))
            taps = cw[:, :, :].rearrange("p (g n) t -> p g n t", n=CT)
            pool.tensor_tensor(taps, taps, w_unscale[:, :].rearrange("p (g n) -> p g n", n=CT + GATES)
                               [:, :, 0:CT].unsqueeze(3).broadcast_to([P, G, CT, 4]), ALU.mult).then_inc(c_init.sem, 1)
            pool.wait_ge(c_init.sem, 4)
            pool.sem_inc(c_go, 5)
            with pool.Fori(0, G) as g:
                c_pool_group(pool, g)
            c_pool_turn(pool, G * TILES)
            pool.wait_ge(d_w.sem, 48)
            d_pool(pool, 0)
            with pool.Fori(1, TILES) as n:
                d_pool(pool, n)

        @block.scalar
        def _(act):
            act.wait_ge(consts_in, N_CONSTS)
            act_front_x(act, 0, first=True)
            act_front_k(act, 0)
            act_exp(act, 0, 0)

            def turn(i, r, par, first=False, late=False, last=False):
                if not last:
                    act_front_x(act, i + 1)
                act_copy_probs(act, i, 0, first)
                act_outT(act, i, 0)
                if not last:
                    act_front_k(act, i + 1)
                act_exp(act, i, 1)
                act_copy_probs(act, i, 1)
                act_outT(act, i, 1)
                act_w_high(act, i, r, par, first=isinstance(r, int) and r == 0)
                if not last:
                    act_exp(act, i + 1, 0)

            a_turns(act, turn)
            act.wait_ge(b_w.sem, 48)
            act.activation(a_neg[:, 0:1], alog, ACT.Exp).then_inc(b_a.sem, 1)
            act.wait_ge(b_a.sem, 1)
            act.activation(a_neg[:, 1:2], a_neg[:, 0:1], ACT.Copy, scale=-1.0).then_inc(b_a.sem, 1)
            act.wait_ge(b_a.sem, 2)
            b_act_x(act, 0, 0, 0, first=True)

            def b_turn(u, r, par, first=False, last=False):
                b_act_dt(act, u, first)
                if not last:
                    b_act_x(act, u + 1, r, par)
                act_wo_high(act, u, 1 - par, first)
                b_act_da(act, u, first)

            b_turns(act, b_turn)
            act.wait_ge(c_go, 5)
            with act.Fori(0, G) as g:
                with act.Fori(0, 4) as j:
                    c_act_turn(act, g, j, 0)
                    c_act_turn(act, g, j, 1)
            square(act, G * TILES)
            y_high(act, G * TILES)
            act.wait_ge(d_w.sem, 48)
            d_act_x(act, 0, first=True)

            def d_turn(n, par, first=False, late=False, last=False):
                d_act_exp(act, n)
                if not last:
                    d_act_x(act, n + 1)
                d_act_w(act, n)

            d_turns(act, d_turn)

        @block.vector
        def _(dve):
            norm_pair(dve, 0, first=True)
            apply_norm(dve, 0, first=True)
            dve.wait_ge(consts_in, N_CONSTS)
            norm_pair(dve, 1)
            dve_mask(dve, 0, 0, first=True)
            dve_softmax(dve, 0, 0)
            apply_norm(dve, 1)

            def turn(i, r, par, first=False, late=False, last=False):
                dve_mask(dve, i, 1, first)
                if not first:
                    dve_out(dve, i - 1, 1)
                if not late:
                    norm_pair(dve, i + 2)
                dve_softmax(dve, i, 1)
                if not late:
                    apply_norm(dve, i + 2)
                dve_w_max(dve, i, r, par, first)
                dve_w_scale(dve, i, r, par, first)
                if not last:
                    dve_mask(dve, i + 1, 0)
                dve_out(dve, i, 0, first)
                if not last:
                    dve_softmax(dve, i + 1, 0)
                dve_w_low(dve, i, par)

            a_turns(dve, turn)
            dve_out(dve, PAIRS - 1, 1)
            dve.wait_ge(a_out.sem, a_out.at(PAIRS - 1, 6))
            dve.sem_inc(b_go, 1)
            dve.wait_ge(b_w.sem, 48)
            b_dve_stats(dve, 0, first=True)
            b_dve_norm(dve, 0, first=True)
            b_dve_low(dve, 0, 0)

            def b_turn(u, r, par, first=False, last=False):
                if not last:
                    b_dve_stats(dve, u + 1)
                dve_wo_max(dve, u, 1 - par)
                if not last:
                    b_dve_norm(dve, u + 1)
                b_dve_dt(dve, u, first)
                dve_wo_scale(dve, u)
                if not last:
                    b_dve_low(dve, u + 1, par)
                b_dve_tok(dve, u)
                dve_wo_low(dve, u, 1 - par)

            b_turns(dve, b_turn)
            dve.wait_ge(c_go, 5)
            with dve.Fori(0, G) as g:
                with dve.Fori(0, 4) as j:
                    c_dve_turn(dve, g, j, 0)
                    c_dve_turn(dve, g, j, 1)
            y_add(dve, G * TILES, 0)
            y_add(dve, G * TILES, 1)
            y_gate(dve, G * TILES)
            y_largest(dve, G * TILES)
            y_scale(dve, G * TILES)
            y_low(dve, G * TILES, 0)
            y_low(dve, G * TILES, 1)
            mean_square(dve, G * TILES)
            row_scale(dve, G * TILES)
            for q in range(4):
                add_out(dve, G * TILES, 0, q)
            dve.wait_ge(d_w.sem, 48)
            dve.wait_ge(c_acc.sem, c_acc.at(G * TILES, 4))
            d_dve_stats(dve, 0, first=True)
            d_dve_norm(dve, 0, 0)
            d_dve_stats(dve, 1)

            def d_turn(n, par, first=False, late=False, last=False):
                if not last:
                    d_dve_norm(dve, n + 1, 1 - par)
                d_dve_logits(dve, n)
                d_dve_choose(dve, n)
                d_dve_scaled(dve, n, par)
                if not late:
                    d_dve_stats(dve, n + 2)
                d_dve_mixed(dve, n)

            d_turns(dve, d_turn)

        @block.tensor
        def _(pe):
            pe.wait_ge(consts_in, N_CONSTS)
            pe_front_x(pe, 0, first=True)
            pe_front_k(pe, 0, first=True)
            pe_scores(pe, 0, 0, first=True)

            def turn(i, r, par, first=False, late=False, last=False):
                pe_scores(pe, i, 1)
                if not first:
                    pe_back(pe, i - 1, 1)
                if not last:
                    pe_front_x(pe, i + 1)
                pe_values(pe, i, 0, par, first)
                if not last:
                    pe_front_k(pe, i + 1)
                    pe_scores(pe, i + 1, 0)
                pe_back(pe, i, 0)
                pe_values(pe, i, 1, par, last=last)

            a_turns(pe, turn)
            pe_back(pe, PAIRS - 1, 1)
            b_pe_x(pe, 0, first=True)
            b_pe_dt(pe, 0, first=True)

            def b_turn(u, r, par, first=False, last=False):
                if not last:
                    b_pe_x(pe, u + 1)
                b_pe_tok(pe, u, first)
                if not last:
                    b_pe_dt(pe, u + 1)

            b_turns(pe, b_turn)
            pe.wait_ge(c_go, 5)
            with pe.Fori(0, G) as g:
                with pe.Fori(0, 4) as j:
                    c_pe_turn(pe, g, j, 0)
                    c_pe_turn(pe, g, j, 1)
            heads_out(pe, G * TILES, 0)
            heads_out(pe, G * TILES, 1)
            out_product(pe, G * TILES, 0, last=True)
            out_product(pe, G * TILES, 1, last=True)
            norm_sums(pe, G * TILES, last=True)
            out_product(pe, G * TILES, 2, last=True)
            out_product(pe, G * TILES, 3, last=True)
            pe.wait_ge(d_w.sem, 48)
            d_pe_x(pe, 0, 0, first=True)
            d_pe_logits(pe, 0, first=True)

            def d_turn(n, par, first=False, late=False, last=False):
                if not last:
                    d_pe_x(pe, n + 1, 1 - par)
                    d_pe_logits(pe, n + 1)
                d_pe_turn_w(pe, n, first)
                d_pe_mix(pe, n, first)

            d_turns(pe, d_turn)


def kernel(**inputs):
    import numpy as np
    import concourse.bacc as bacc
    from concourse.bass_utils import run_bass_kernel_spmd

    a = {k: np.asarray(v) for k, v in inputs.items()}
    w = a["L0_attn_in_proj_w"]
    inner, gn = H * HP, G * N_ST
    gate_r = w[:inner].reshape(G, 512, DM)
    x_r = w[inner:2 * inner].reshape(G, 512, DM)
    b_r = w[2 * inner:2 * inner + gn].reshape(G, P, DM)
    c_r = w[2 * inner + gn:2 * inner + 2 * gn].reshape(G, P, DM)

    def k_major(rows):
        g, n, _ = rows.shape
        return rows.transpose(0, 2, 1).reshape(g, KT, P, n).transpose(0, 2, 1, 3)

    def channel_slices(rows):
        return rows.reshape(W_TILES, P, KT, P).transpose(3, 0, 2, 1).reshape(P, W_TILES, KT * P)

    def channel_tiles(rows):
        xs = rows[:inner].reshape(G, 4, P, -1)
        bs = rows[inner:inner + gn].reshape(G, 1, P, -1)
        cs = rows[inner + gn:].reshape(G, 1, P, -1)
        return np.concatenate([bs, cs, xs], 1).transpose(2, 0, 1, 3).reshape(P, G * CT, -1)

    arrays = {
        "x": a["x"], "ctx": a["ctx_1024"], "mask": a["mask_SxS2_ff0"],
        "w_in": channel_slices(np.concatenate([b_r, c_r, x_r, gate_r], 1)),
        "w_dt": k_major(w[-H:][None])[0],
        "w_out": a["L0_attn_out_proj_w"].T.reshape(G, 4, P, DM).transpose(0, 2, 1, 3),
        "conv_w": channel_tiles(a["L0_attn_conv_weight"]),
        "conv_b": channel_tiles(a["L0_attn_conv_bias"][:, None])[:, :, 0],
        "dt_bias": a["L0_attn_dt_bias"][:, None], "a_log": a["L0_attn_A_log"][:, None],
        "d_skip": np.repeat(a["L0_attn_D"], HP).reshape(G * 4, P).T,
        "norm_w": a["L0_attn_norm_weight"].reshape(G * 4, P).T,
        "w_router": a["L0_ffn_router_weight"].T.reshape(KT, P, E).transpose(1, 0, 2),
        "b_router": a["L0_ffn_router_bias"][None],
        "e_bias": a["L0_ffn_expert_bias"],
        "ident": np.eye(P, dtype=np.float32),
        "parity": np.stack([1 - np.arange(P) // HD % 2, np.arange(P) // HD % 2], 1).astype(np.float32),
        "eye": np.tile(np.eye(SEQ, dtype=np.float32), (2, HG)),
    }
    arrays = {f"in_{k}": np.ascontiguousarray(v) for k, v in arrays.items()}
    nc = bacc.Bacc("TRN2", target_bir_lowering=False, num_devices=1)
    args = [nc.dram_tensor(k, v.shape, F32, kind="ExternalInput").ap() for k, v in arrays.items()]
    out = nc.dram_tensor("out", [BATCH, SEQ, DM], F32, kind="ExternalOutput").ap()
    xt_d = nc.dram_tensor("xt", [TILES, P, 2, KT, TOK], F16).ap()
    wo_d = nc.dram_tensor("wo_split", [G, P, 2, 4 * DM], F16).ap()
    w_d = nc.dram_tensor("w_split", [P, W_TILES, 2, KT * P], F16).ap()
    da_d = nc.dram_tensor("da", [BATCH, H, SEQ], F32).ap()
    build(nc, *args, out, xt_d, da_d, w_d, wo_d)
    r = run_bass_kernel_spmd(nc, [arrays], core_ids=[0])
    return r.results[0]["out"]
```
